# Optimizing a Trainium2 kernel written in Bass

```python
import numpy as np
import jax
import jax.numpy as jnp

def _softmax(x, axis=-1):
    return jax.nn.softmax(x, axis=axis)

def _gelu(x):
    return jax.nn.gelu(x, approximate=True)

def _silu(x):
    return jax.nn.silu(x)

def _sigmoid(x):
    return jax.nn.sigmoid(x)

def _layernorm(x, axis=-1, eps=1e-05):
    m = jnp.mean(x, axis=axis, keepdims=True)
    v = jnp.var(x, axis=axis, keepdims=True)
    return (x - m) / jnp.sqrt(v + eps)

def _scatter_add(tgt, idx, src, axis=0):
    return tgt.at[idx].add(src)

def _segment_sum(src, seg, n):
    return jax.ops.segment_sum(src, seg, n)
kernel_name = 'mk_hybrid_d1_jaxref_r8_fb163c'

def setup_inputs(seed: int=0):
    np.random.seed(seed)
    _w = jnp.asarray

    def _L0_attn_a_setup():
        import math
        import jax, jax.numpy as jnp
        import numpy as np
        B, S, D, H = (2, 256, 128, 16)
        HD = D // H
        key = jax.random.key(seed)
        k1, k2, k3 = jax.random.split(key, 3)
        h = jax.random.normal(k1, (B, S, D), dtype=jnp.float32)
        Wqvk = jax.random.normal(k2, (D, 3 * D), dtype=jnp.float32) * (1.0 / math.sqrt(D))
        Wo = jax.random.normal(k3, (D, D), dtype=jnp.float32) * (1.0 / math.sqrt(D))
        return {'h': h, 'Wqvk': Wqvk, 'Wo': Wo}
    _L0_attn_a_in = _L0_attn_a_setup()

    def _L0_attn_b_setup():
        import jax, jax.numpy as jnp
        import numpy as np
        D_MODEL = 128
        N_HEADS = 16
        D_LATENT = 32
        HEAD_DIM = D_MODEL // N_HEADS

        def apply_rope(x):
            B, T, H, D = x.shape
            inv_freq = 1.0 / 10000.0 ** (jnp.arange(0, D, 2, dtype=jnp.float32) / D)
            t = jnp.arange(T, dtype=jnp.float32)
            freqs = t[:, None] * inv_freq[None, :]
            sin_f = jnp.sin(freqs)[None, :, None, :]
            cos_f = jnp.cos(freqs)[None, :, None, :]
            x1, x2 = jnp.split(x, 2, axis=-1)
            return jnp.concatenate([x1 * cos_f - x2 * sin_f, x1 * sin_f + x2 * cos_f], axis=-1)
        key = jax.random.key(seed)
        ks = jax.random.split(key, 10)
        B, T = (4, 512)
        s = lambda fan_in: 1.0 / np.sqrt(fan_in)
        return {'x': jax.random.normal(ks[0], (B, T, D_MODEL), dtype=jnp.float32), 'Wq': jax.random.normal(ks[1], (D_MODEL, D_MODEL), dtype=jnp.float32) * s(D_MODEL), 'bq': jnp.zeros((D_MODEL,), jnp.float32), 'Wdown': jax.random.normal(ks[2], (D_MODEL, D_LATENT), dtype=jnp.float32) * s(D_MODEL), 'bdown': jnp.zeros((D_LATENT,), jnp.float32), 'Wup': jax.random.normal(ks[3], (D_LATENT, 2 * D_MODEL), dtype=jnp.float32) * s(D_LATENT), 'bup': jnp.zeros((2 * D_MODEL,), jnp.float32), 'Wout': jax.random.normal(ks[4], (D_MODEL, D_MODEL), dtype=jnp.float32) * s(D_MODEL), 'bout': jnp.zeros((D_MODEL,), jnp.float32)}
    _L0_attn_b_in = _L0_attn_b_setup()

    def _L0_ffn_setup():
        import jax, jax.numpy as jnp
        import numpy as np
        from jax import lax
        D_MODEL = 128
        D_FF = 512
        NUM_EXPERTS = 24
        TOP_K = 2
        key = jax.random.key(seed)
        ks = jax.random.split(key, 7)
        s1 = 1.0 / np.sqrt(D_MODEL)
        s2 = 1.0 / np.sqrt(D_FF)
        x = jax.random.normal(ks[0], (2, 128, D_MODEL), dtype=jnp.float32)
        gate_w = jax.random.uniform(ks[1], (D_MODEL, NUM_EXPERTS), jnp.float32, -s1, s1)
        gate_b = jax.random.uniform(ks[2], (NUM_EXPERTS,), jnp.float32, -s1, s1)
        w1 = jax.random.uniform(ks[3], (NUM_EXPERTS, D_MODEL, D_FF), jnp.float32, -s1, s1)
        b1 = jax.random.uniform(ks[4], (NUM_EXPERTS, D_FF), jnp.float32, -s1, s1)
        w2 = jax.random.uniform(ks[5], (NUM_EXPERTS, D_FF, D_MODEL), jnp.float32, -s2, s2)
        b2 = jax.random.uniform(ks[6], (NUM_EXPERTS, D_MODEL), jnp.float32, -s2, s2)
        return {'x': x, 'gate_w': gate_w, 'gate_b': gate_b, 'w1': w1, 'b1': b1, 'w2': w2, 'b2': b2}
    _L0_ffn_in = _L0_ffn_setup()
    _d = {'L0_attn_a_h': _L0_attn_a_in['h'], 'L0_attn_a_Wqvk': _L0_attn_a_in['Wqvk'], 'L0_attn_a_Wo': _L0_attn_a_in['Wo'], 'L0_attn_b_Wq': _L0_attn_b_in['Wq'], 'L0_attn_b_bq': _L0_attn_b_in['bq'], 'L0_attn_b_Wdown': _L0_attn_b_in['Wdown'], 'L0_attn_b_bdown': _L0_attn_b_in['bdown'], 'L0_attn_b_Wup': _L0_attn_b_in['Wup'], 'L0_attn_b_bup': _L0_attn_b_in['bup'], 'L0_attn_b_Wout': _L0_attn_b_in['Wout'], 'L0_attn_b_bout': _L0_attn_b_in['bout'], 'L0_ffn_gate_w': _L0_ffn_in['gate_w'], 'L0_ffn_gate_b': _L0_ffn_in['gate_b'], 'L0_ffn_w1': _L0_ffn_in['w1'], 'L0_ffn_b1': _L0_ffn_in['b1'], 'L0_ffn_w2': _L0_ffn_in['w2'], 'L0_ffn_b2': _L0_ffn_in['b2']}
    _x0 = _d['L0_attn_a_h']
    _d['L0_attn_a_h'] = jax.random.normal(jax.random.fold_in(jax.random.key(seed), 1), (8, 512, 128), dtype=_x0.dtype)
    del _x0
    return _d

def reference(L0_attn_a_h, L0_attn_a_Wqvk, L0_attn_a_Wo, L0_attn_b_Wq, L0_attn_b_bq, L0_attn_b_Wdown, L0_attn_b_bdown, L0_attn_b_Wup, L0_attn_b_bup, L0_attn_b_Wout, L0_attn_b_bout, L0_ffn_gate_w, L0_ffn_gate_b, L0_ffn_w1, L0_ffn_b1, L0_ffn_w2, L0_ffn_b2):

    def _L0_attn_a_ref(h, Wqvk, Wo):
        import math
        import jax, jax.numpy as jnp
        import numpy as np
        B, S, D, H = (2, 256, 128, 16)
        HD = D // H
        b, s, d = h.shape
        qvk = (h @ Wqvk).reshape(b, s, 3, H, HD)
        q, v, k = (qvk[:, :, 0], qvk[:, :, 1], qvk[:, :, 2])
        scores = jnp.einsum('bshi,bthi->bsth', q, k)
        mask = jnp.where(jnp.arange(s)[None, :] > jnp.arange(s)[:, None], jnp.float32(-jnp.inf), jnp.float32(0.0))
        scores = scores + mask[None, :, :, None]
        scores = scores / math.sqrt(d)
        weights = jax.nn.softmax(scores, axis=2)
        wv = jnp.einsum('bsth,bthi->bshi', weights, v).reshape(b, s, d)
        return wv @ Wo

    def _L0_attn_b_ref(x, Wq, bq, Wdown, bdown, Wup, bup, Wout, bout):
        import jax, jax.numpy as jnp
        import numpy as np
        D_MODEL = 128
        N_HEADS = 16
        D_LATENT = 32
        HEAD_DIM = D_MODEL // N_HEADS

        def apply_rope(x):
            B, T, H, D = x.shape
            inv_freq = 1.0 / 10000.0 ** (jnp.arange(0, D, 2, dtype=jnp.float32) / D)
            t = jnp.arange(T, dtype=jnp.float32)
            freqs = t[:, None] * inv_freq[None, :]
            sin_f = jnp.sin(freqs)[None, :, None, :]
            cos_f = jnp.cos(freqs)[None, :, None, :]
            x1, x2 = jnp.split(x, 2, axis=-1)
            return jnp.concatenate([x1 * cos_f - x2 * sin_f, x1 * sin_f + x2 * cos_f], axis=-1)
        B, T, D = x.shape
        H, Dh = (N_HEADS, HEAD_DIM)
        q = x @ Wq + bq
        kv_latent = x @ Wdown + bdown
        kv = kv_latent @ Wup + bup
        q = q.reshape(B, T, H, Dh)
        kv = kv.reshape(B, T, H, 2 * Dh)
        k, v = jnp.split(kv, 2, axis=-1)
        q = apply_rope(q)
        k = apply_rope(k)
        att = jnp.einsum('bthd,btgd->bthg', q, k) / jnp.sqrt(jnp.float32(Dh))
        att = jax.nn.softmax(att, axis=-1)
        out = jnp.einsum('bthg,btgd->bthd', att, v)
        out = out.reshape(B, T, D)
        return out @ Wout + bout

    def _L0_ffn_ref(x, gate_w, gate_b, w1, b1, w2, b2):
        import jax, jax.numpy as jnp
        import numpy as np
        from jax import lax
        D_MODEL = 128
        D_FF = 512
        NUM_EXPERTS = 24
        TOP_K = 2
        gate_scores = jnp.einsum('bsd,de->bse', x, gate_w) + gate_b
        topk_val, topk_idx = lax.top_k(gate_scores, TOP_K)
        sparse_gates = jax.nn.softmax(topk_val, axis=-1)
        combine = jnp.sum(jax.nn.one_hot(topk_idx, NUM_EXPERTS, dtype=x.dtype) * sparse_gates[..., None], axis=-2)
        h = jax.nn.gelu(jnp.einsum('bsd,edf->besf', x, w1) + b1[None, :, None, :], approximate=False)
        y = jnp.einsum('besf,efd->besd', h, w2) + b2[None, :, None, :]
        out = jnp.einsum('bse,besd->bsd', combine, y)
        return out + x
    x = L0_attn_a_h
    x = x + _L0_attn_a_ref(_layernorm(x, axis=-1), L0_attn_a_Wqvk, L0_attn_a_Wo)
    x = x + _L0_ffn_ref(_layernorm(x, axis=-1), L0_ffn_gate_w, L0_ffn_gate_b, L0_ffn_w1, L0_ffn_b1, L0_ffn_w2, L0_ffn_b2)
    x = x + _L0_attn_b_ref(_layernorm(x, axis=-1), L0_attn_b_Wq, L0_attn_b_bq, L0_attn_b_Wdown, L0_attn_b_bdown, L0_attn_b_Wup, L0_attn_b_bup, L0_attn_b_Wout, L0_attn_b_bout)
    x = x + _L0_ffn_ref(_layernorm(x, axis=-1), L0_ffn_gate_w, L0_ffn_gate_b, L0_ffn_w1, L0_ffn_b1, L0_ffn_w2, L0_ffn_b2)
    return x

_drawn_inputs = setup_inputs


def setup_inputs(seed=0):
    import zlib

    import numpy as np

    out = dict(_drawn_inputs(seed))
    spreads = {'L0_attn_b_bq': (0.0, 0.47),
     'L0_attn_b_bdown': (0.0, 0.423),
     'L0_attn_b_bup': (0.0, 0.306),
     'L0_attn_b_bout': (0.0, 0.1)}
    factors = {'L0_ffn_b1': 5.13, 'L0_ffn_b2': 3.699}
    for name, (base, spread) in spreads.items():
        noise = np.random.default_rng([zlib.crc32(name.encode()), seed]).standard_normal(out[name].shape)
        drawn = base * np.exp(spread * noise) if base else spread * noise
        out[name] = jnp.asarray(drawn.astype(out[name].dtype))
    for name, factor in factors.items():
        out[name] = (out[name] * factor).astype(out[name].dtype)
    return out
```

```python
from contextlib import ExitStack

import concourse.bass as bass
from concourse import mybir

F32 = mybir.dt.float32
BF16 = mybir.dt.bfloat16
I32 = mybir.dt.int32
U32 = mybir.dt.uint32
ALU = mybir.AluOpType
ACT = mybir.ActivationFunctionType
AX = mybir.AxisListType

P = 128
D = 128
BATCH, SEQ = 8, 512
TILES = BATCH * SEQ // P
TPB = SEQ // P
H, HD = 16, 8
PAIRS = H // 2
G4 = H // 4
LAG = 3
RING = 2 * TPB
EPS = 1e-5
NEG = -1e30
SLOTS = 6
HEADW = 64
K48 = SLOTS * HD


LATENT = 32
NE, FF = 24, 512
FC = FF // P
ROW_TILES = 4 * -(-((2 * TILES * P - NE) // P + NE) // 4)
W_COLS = FF + FC * D + FC
WBUFS = 4
YBUFS = 4


def hybrid_layer(nc, h, Wqvk, Wo, gate_w, gate_b, wpack, b2, Wq, bq, Wdown, bdown, Wup, bup, Wout, bout, rope, out):
    ctx = ExitStack()
    with ctx:
        def sb(name, shape, dt=F32):
            return ctx.enter_context(nc.sbuf_tensor(name, shape, dt))

        def ps(name, shape, dt=F32):
            return ctx.enter_context(nc.psum_tensor(name, shape, dt))

        def sem(name):
            return ctx.enter_context(nc.semaphore(name))

        X = sb("X", [P, TILES, D])
        NHALF = sb("NHALF", [P, TILES])
        ZERO = sb("ZERO", [P, 2 * H])
        ONE = sb("ONE", [P, 1])
        IDF = sb("IDF", [P, P])
        IDB = sb("IDB", [P, P], BF16)
        MASK = sb("MASK", [P, P], BF16)
        MASKT = sb("MASKT", [P, P], BF16)
        WQ = sb("WQ", [D, 3 * D])
        WO = sb("WO", [D, D])
        XN = sb("XN", [P, D])
        XT = sb("XT", [D, P])
        QK = sb("QK", [P, 2, D])
        R1 = sb("R1", [P, 2, D])
        QS = sb("QS", [P, 2, H, HEADW], BF16)
        KS = sb("KS", [P, H, HEADW], BF16)
        QT = sb("QT", [P, 2, PAIRS, P], BF16)
        QT2 = sb("QT2", [P, 2, PAIRS, P], BF16)
        KT = sb("KT", [P, RING, PAIRS, P], BF16)
        V32 = sb("V32", [P, RING, H, 32])
        NM = sb("NM", [P, 2, H])
        PT = sb("PT", [P, 2, 4, SEQ])
        OS = sb("OS", [P, G4, P])
        RS = sb("RS", [P, H])
        WV = sb("WV", [P, D])
        WVT = sb("WVT", [D, P])


        XN_ALL = sb("XN_ALL", [P, TILES, D])
        XS = sb("XS", [P, 2, D])
        XST = sb("XST", [D, 2, P])
        GW = sb("GW", [D, NE])
        GB = sb("GB", [1, NE])
        ONER = sb("ONER", [1, P])
        UT = sb("UT", [P, P], BF16)
        ONESB = sb("ONESB", [P, P], BF16)
        STAT = sb("STAT", [P, TILES, 6])
        MEAN = sb("MEAN", [P, TILES])
        VAR = sb("VAR", [P, TILES])
        DIFF = sb("DIFF", [P, TILES])
        RSD = sb("RSD", [P, TILES])
        LG = sb("LG", [P, TILES, NE])
        IOTA_E = sb("IOTA_E", [P, NE])
        IOTA_J = sb("IOTA_J", [1, ROW_TILES])
        O1H = [sb(f"O1H{k}", [P, TILES, NE]) for k in range(2)]
        CAND = sb("CAND", [P, TILES, NE])
        MSK = sb("MSK", [P, TILES, NE], BF16)
        TOP = sb("TOP", [P, 2, TILES])
        IDX = sb("IDX", [P, TILES])
        GATE = sb("GATE", [P, TILES, 2])
        EXPD = sb("EXPD", [P, TILES])
        KEEP = sb("KEEP", [P, NE, TILES])
        CNT = sb("CNT", [P, NE, TILES])
        INC = sb("INC", [P, NE, TILES])
        TI = sb("TI", [P, NE], I32)
        TF = sb("TF", [P, NE])
        TEND = sb("TEND", [P, NE])
        ONES_E = sb("ONES_E", [P, NE])
        CMP = sb("CMP", [1, ROW_TILES, NE])
        EJF = sb("EJF", [1, ROW_TILES])
        EJ = sb("EJ", [1, ROW_TILES], I32)
        POSF = sb("POSF", [P, TILES, 2])
        POS = sb("POS", [P, TILES, 2], I32)
        W = sb("W", [P, WBUFS, W_COLS])
        B2 = sb("B2", [1, WBUFS, D])
        XI = sb("XI", [P, WBUFS, D])
        XIT = sb("XIT", [D, 2, P])
        HT = sb("HT", [P, 2, FC, P])
        Y = sb("Y", [P, 2, D])
        YG = sb("YG", [P, YBUFS, 2, D])
        ACC = sb("ACC", [P, 2, D])

        f_w_in = sem("f_w_in")
        f_const = sem("f_const")
        f_zeroed = sem("f_zeroed")
        f_stat = sem("f_stat")
        f_link = sem("f_link")
        f_stat1 = sem("f_stat1")
        f_stat2 = sem("f_stat2")
        f_var = sem("f_var")
        f_eps = sem("f_eps")
        f_rstd = sem("f_rstd")
        f_xs = sem("f_xs")
        f_xn = sem("f_xn")
        f_xsT = sem("f_xsT")
        f_xst = sem("f_xst")
        f_lg = sem("f_lg")
        f_lgc = sem("f_lgc")
        f_top = sem("f_top")
        f_exp = sem("f_exp")
        f_mask = sem("f_mask")
        f_rank = sem("f_rank")
        f_ej = sem("f_ej")
        f_pos = sem("f_pos")
        f_scat = sem("f_scat")
        f_wl = [sem(f"f_wl{i}") for i in range(WBUFS)]
        f_bl = [sem(f"f_bl{i}") for i in range(WBUFS)]
        f_xl = [sem(f"f_xl{i}") for i in range(WBUFS)]
        f_xiT = sem("f_xiT")
        f_xit = sem("f_xit")
        f_up = sem("f_up")
        f_gelu = sem("f_gelu")
        f_down = sem("f_down")
        f_y = sem("f_y")
        f_ys = [sem(f"f_ys{i}") for i in range(2)]
        f_yg = [sem(f"f_yg{i}") for i in range(YBUFS)]
        f_acc = sem("f_acc")
        f_acc0 = sem("f_acc0")
        f_done = sem("f_done")

        rows_in = nc.dram_tensor("rows_in", [ROW_TILES * P, D], F32, kind="Internal").ap()
        rows_out = nc.dram_tensor("rows_out", [ROW_TILES * P, D], F32, kind="Internal").ap()
        rows_out_v = rows_out.rearrange("(j p) d -> p j d", p=P)
        rows_in_v = rows_in.rearrange("(j p) d -> p j d", p=P)
        LINKS = 26

        BQ_W = sb("BQ_W", [D, D])
        BQ_B = sb("BQ_B", [1, D])
        BD_W = sb("BD_W", [D, LATENT])
        BD_B = sb("BD_B", [LATENT, 1])
        BU_W = sb("BU_W", [LATENT + 1, 2 * D])
        BO_W = sb("BO_W", [D, D])
        BO_B = sb("BO_B", [1, D])
        ROPE = sb("ROPE", [P, TPB, 2, HD])
        LT = sb("LT", [LATENT + 1, 2, P])
        QKR = sb("QKR", [P, 2, 2, H, HD])
        VB = sb("VB", [P, 4, H, HD])
        T1 = sb("T1", [P, 2, H, HD])
        T2 = sb("T2", [P, 2, H, HD])
        ROT = sb("ROT", [P, 2, 2, H, HD])
        PROD = PT[:, :, :, :].rearrange("p a j (h g d) -> p a (j h) g d", g=H, d=HD)
        ATT = sb("ATT", [P, H, H])
        AMX = sb("AMX", [P, H])
        SH = sb("SH", [P, 2, H, H])
        EX = sb("EX", [P, 2, H, H])
        PROD2 = V32[:, 0:TPB, :, :].rearrange("p t h (a b) -> p (t h a b)", b=H).rearrange("p (h d g) -> p h d g", d=HD, g=H)
        ASUM = sb("ASUM", [P, H])
        ARS = sb("ARS", [P, H])
        AO = sb("AO", [P, H, HD])
        BWV = sb("BWV", [P, 2, D])
        BWVT = sb("BWVT", [D, 2, P])

        b_w_in = sem("b_w_in")
        b_const = sem("b_const")
        b_xs = sem("b_xs")
        b_xsT = sem("b_xsT")
        b_xst = sem("b_xst")
        b_ql = sem("b_ql")
        b_lat = sem("b_lat")
        b_kv = sem("b_kv")
        b_qk = sem("b_qk")
        b_v = sem("b_v")
        b_rope1 = sem("b_rope1")
        b_rot = sem("b_rot")
        b_prod = sem("b_prod")
        b_att = sem("b_att")
        b_max = sem("b_max")
        b_sh = sem("b_sh")
        b_ex = sem("b_ex")
        b_p2 = sem("b_p2")
        b_red2 = sem("b_red2")
        b_red2b = sem("b_red2b")
        b_rs = sem("b_rs")
        b_wv = sem("b_wv")
        b_wvT = sem("b_wvT")
        b_wvt = sem("b_wvt")
        b_o = sem("b_o")
        b_x = sem("b_x")
        banks = [ps(f"bank{i}", [P, SEQ]) for i in range(8)]
        psA, psB = banks[0:2], banks[2:4]
        psO = banks[4][:, :].rearrange("p (q t) -> p q t", q=G4)
        psM = banks[5]
        psT = banks[6][:, :].bitcast(BF16).rearrange("p (g t) -> p g t", g=PAIRS)
        psXS, psR, psC = banks[0:2], banks[2:4], banks[4:6]
        psXI, psH, psY = banks[0:2], banks[2:4], banks[4:6]
        psP, psF = banks[0:2], banks[2:4]

        x_in = [sem(f"x_in{b}") for b in range(BATCH)]
        w_in = sem("w_in")
        const_a = sem("const_a")
        const_ready = sem("const_ready")
        stats_done = sem("stats_done")
        mv_done = sem("mv_done")
        rstd_step = sem("rstd_step")
        rstd_done = sem("rstd_done")
        xn_done = sem("xn_done")
        xT_done = sem("xT_done")
        xT_copied = sem("xT_copied")
        qkv_done = sem("qkv_done")
        qk_copied = sem("qk_copied")
        v_copied = sem("v_copied")
        hi_done = sem("hi_done")
        mid_done = sem("mid_done")
        r1_done = sem("r1_done")
        parts_done = sem("parts_done")
        qT_done = sem("qT_done")
        kT_done = sem("kT_done")
        q2T_done = sem("q2T_done")
        qT_copied = sem("qT_copied")
        kT_copied = sem("kT_copied")
        q2T_copied = sem("q2T_copied")
        scoresA_done = sem("scoresA_done")
        max_done = sem("max_done")
        m_hi_done = sem("m_hi_done")
        m_done = sem("m_done")
        scoresB_done = sem("scoresB_done")
        exp_done = sem("exp_done")
        pv_done = sem("pv_done")
        o_copied = sem("o_copied")
        oT_done = sem("oT_done")
        rs_done = sem("rs_done")
        wv_done = sem("wv_done")
        wvT_done = sem("wvT_done")
        wvT_copied = sem("wvT_copied")
        wo_done = sem("wo_done")
        x1_done = sem("x1_done")
        out_sent = sem("out_sent")
        const_v = sem("const_v")

        h_v = h.rearrange("b (t p) d -> p (b t) d", p=P)
        out_v = out.rearrange("b (t p) d -> p (b t) d", p=P)

        block = ctx.enter_context(nc.Block())

        def wait(eng, semaphore, n):
            if not isinstance(n, int) or n > 0:
                eng.wait_ge(semaphore, n)

        def exists(T):
            return not isinstance(T, int) or 0 <= T < TILES

        def over_tiles(eng, slot):
            for T in range(-2, RING):
                slot(T, T % RING)
            with eng.Fori(1, TILES // RING - 1) as i:
                for r in range(RING):
                    slot(RING * i + r, r)
            for T in range(TILES - RING, TILES + 1):
                slot(T, T % RING)


        def statistics(dve, n):
            with dve.Fori(0, TILES) as T:
                dve.bn_stats(STAT[:, bass.ds(T, 1), :].rearrange("p a d -> p (a d)"),
                             X[:, bass.ds(T, 1), :].rearrange("p a d -> p (a d)")).then_inc(f_stat, 1)
            dve.wait_ge(f_stat, TILES * (n + 1))
            dve.tensor_tensor(MEAN[:, :], STAT[:, :, 1], STAT[:, :, 4], ALU.add).then_inc(f_stat1, 1)
            dve.tensor_tensor(DIFF[:, :], STAT[:, :, 1], STAT[:, :, 4], ALU.subtract).then_inc(f_stat1, 1)
            dve.wait_ge(f_stat1, 4 * n + 2)
            dve.tensor_scalar(MEAN[:, :], MEAN[:, :], 0.5, None, ALU.mult).then_inc(f_stat2, 1)
            dve.tensor_tensor(VAR[:, :], STAT[:, :, 2], STAT[:, :, 5], ALU.add).then_inc(f_stat1, 1)
            dve.tensor_tensor(DIFF[:, :], DIFF[:, :], DIFF[:, :], ALU.mult).then_inc(f_stat1, 1)
            dve.wait_ge(f_stat1, 4 * n + 4)
            dve.scalar_tensor_tensor(VAR[:, :], DIFF[:, :], D / 4.0, VAR[:, :], ALU.mult, ALU.add).then_inc(f_var, 1)
            dve.wait_ge(f_stat2, n + 1)
            dve.wait_ge(f_rstd, n + 1)

        def deviations(pool, n):
            pool.wait_ge(f_var, n + 1)
            pool.tensor_scalar(RSD[:, :], VAR[:, :], 1.0 / D, EPS, ALU.mult, ALU.add).then_inc(f_eps, 1)
            pool.wait_ge(f_eps, n + 1)
            pool.tensor_tensor(RSD[:, :], RSD[:, :], NHALF[:, :], ALU.pow).then_inc(f_rstd, 1)

        def ffn_consts_pool(pool):
            pool.memset(UT[:, :], 1.0).then_inc(f_const, 1)
            pool.memset(ONESB[:, :], 1.0).then_inc(f_const, 1)
            pool.memset(ONES_E[:, :], 1.0).then_inc(f_const, 1)
            pool.memset(ONER[:, :], 1.0).then_inc(f_const, 1)
            pool.memset(KEEP[:, :, :], 1.0).then_inc(f_const, 1)
            pool.memset(XN_ALL[:, :, :], 0.0).then_inc(f_const, 1)
            pool.wait_ge(f_const, 6)
            pool.affine_select(out=UT[:, :], in_=UT[:, :], compare_op=ALU.is_gt, fill=0.0, base=0,
                               pattern=[[1, P]], channel_multiplier=-1).then_inc(f_const, 1)
            pool.memset(KEEP[:, :, 0], 0.0).then_inc(f_const, 1)
            pool.iota(IOTA_E[:, :], pattern=[[1, NE]], base=0, channel_multiplier=0,
                      allow_small_or_imprecise_dtypes=True).then_inc(f_const, 1)
            pool.iota(IOTA_J[:, :], pattern=[[1, ROW_TILES]], base=0, channel_multiplier=0,
                      allow_small_or_imprecise_dtypes=True).then_inc(f_const, 1)

        def ffn_consts_sp(sp):
            sp.dma_start(GW[:, :], gate_w).then_inc(f_w_in, 16)
            sp.dma_start(GB[:, :], gate_b).then_inc(f_w_in, 16)
            sp.wait_ge(f_const, 6)
            for a in range(0, ROW_TILES, TILES):
                n = min(TILES, ROW_TILES - a)
                sp.dma_start(rows_in_v[:, a:a + n, :], XN_ALL[:, 0:n, :]).then_inc(f_zeroed, 16)

        ZEROED = 16 * -(-ROW_TILES // TILES)

        def ffn_pool(pool, ph):
            deviations(pool, 2 * ph + 1)
            pool.wait_ge(f_zeroed, ZEROED)

            def keep(T, par):
                pool.wait_ge(f_xs, ph * TILES + T + 1)
                pool.tensor_tensor(XN_ALL[:, bass.ds(T, 1), :].rearrange("p a d -> p (a d)"), XS[:, par, :],
                                   ONE[:, :].broadcast_to([P, D]), ALU.mult).then_inc(f_xn, 1)

            with pool.Fori(0, TILES // 2) as i:
                keep(2 * i, 0)
                keep(2 * i + 1, 1)
            pool.wait_ge(f_pos, ph + 1)
            pool.wait_ge(f_xn, TILES * (ph + 1))
            for T in range(TILES):
                for k in range(2):
                    pool.indirect_dma_start(out=rows_in, out_offset=bass.IndirectOffsetOnAxis(ap=POS[:, T, k:k + 1], axis=0),
                                            in_=XN_ALL[:, T, :], in_offset=None).then_inc(f_scat, 16)
            for i in range(2):
                pool.wait_ge(f_ys[i], 16 * (ROW_TILES // 2) * (ph + 1))
            for T in range(TILES):
                n = ph * TILES + T
                if n >= YBUFS:
                    pool.wait_ge(f_acc, n - YBUFS + 1)
                for k in range(2):
                    pool.indirect_dma_start(out=YG[:, T % YBUFS, k, :], out_offset=None, in_=rows_out,
                                            in_offset=bass.IndirectOffsetOnAxis(ap=POS[:, T, k:k + 1], axis=0)
                                            ).then_inc(f_yg[T % YBUFS], 16)

        def ffn_sp(sp, ph):
            base = ph * ROW_TILES
            sp.wait_ge(f_ej, ph + 1)
            sp.wait_ge(f_scat, 16 * 2 * TILES * (ph + 1))

            def load(j, u, first):
                b = u % WBUFS
                if not first:
                    sp.wait_ge(f_down, base + j - WBUFS + 1)
                e = sp.value_load(EJ[0:1, bass.ds(j, 1)], min_val=0, max_val=NE - 1)
                sp.dma_start(XI[:, b, :], rows_in_v[:, bass.ds(j, 1), :].rearrange("p a d -> p (a d)")).then_inc(f_xl[b], 16)
                sp.dma_start(W[:, b, :], wpack[bass.ds(e, 1), :, :].rearrange("a p n -> (a p) n")).then_inc(f_wl[b], 16)
                sp.dma_start(B2[:, b, :], b2[bass.ds(e, 1), :]).then_inc(f_bl[b], 16)

            def store(j, u):
                sp.wait_ge(f_y, base + j + 1)
                sp.dma_start(rows_out_v[:, bass.ds(j, 1), :].rearrange("p a d -> p (a d)"), Y[:, u % 2, :]).then_inc(f_ys[u % 2], 16)

            def both(j, u, first):
                load(j, u, first and ph == 0 and u < WBUFS)
                if not (first and u < WBUFS):
                    store(j - WBUFS, (u - WBUFS) % 12)

            over_rows(sp, both)
            for j in range(ROW_TILES - WBUFS, ROW_TILES):
                store(j, j % 12)

        def over_rows(eng, body):
            step = 12
            for j in range(step):
                body(j, j, True)
            rounds = ROW_TILES // step
            with eng.Fori(1, rounds) as i:
                for u in range(step):
                    body(step * i + u, u, False)
            for j in range(rounds * step, ROW_TILES):
                body(j, j % step, False)

        def ffn_act(act, ph):
            base = ph * ROW_TILES

            def xst(T, par):
                act.wait_ge(f_xsT, ph * TILES + T + 1)
                act.activation(XST[:, par, :], psXS[par][:, 0:P], ACT.Copy).then_inc(f_xst, 1)

            with act.Fori(0, TILES // 2) as i:
                xst(2 * i, 0)
                xst(2 * i + 1, 1)
            act.wait_ge(f_top, ph + 1)
            act.activation(EXPD[:, :], DIFF[:, :], ACT.Exp).then_inc(f_exp, 1)

            def gelu(j, u, first):
                act.wait_ge(f_up, base + j + 1)
                act.wait_ge(f_wl[u % WBUFS], w_count(ph, j, u))
                if not (first and ph == 0 and u < 2):
                    act.wait_ge(f_down, base + j - 1)
                for c in range(FC):
                    a = act.activation(HT[:, u % 2, c, :], psH[u % 2][:, c * P:(c + 1) * P], ACT.Gelu,
                                       bias=W[:, u % WBUFS, FF + FC * D + c:FF + FC * D + c + 1])
                a.then_inc(f_gelu, 1)

            over_rows(act, gelu)

        def w_count(ph, j, u):
            b = u % WBUFS
            before = len(range(b, ROW_TILES, WBUFS)) * ph
            if isinstance(j, int):
                return 16 * (before + j // WBUFS + 1)
            return (j - b) * 16 // WBUFS + 16 * (before + 1)

        def ffn_pe(pe, ph):
            base = ph * ROW_TILES

            def logits(T, par, first):
                n = ph * TILES + T
                pe.wait_ge(f_xs, n + 1)
                if not first:
                    pe.wait_ge(f_lgc, n - 1)
                pe.transpose(psXS[par][:, 0:P], XS[:, par, :], IDF[:, :]).then_inc(f_xsT, 1)
                pe.wait_ge(f_xst, n + 1)
                pe.matmul(psXS[par][:, P:P + NE], XST[:, par, :], GW[:, :], start=True, stop=False)
                pe.matmul(psXS[par][:, P:P + NE], ONER[:, :], GB[:, :], start=False, stop=True).then_inc(f_lg, 1)

            logits(0, 0, ph == 0)
            logits(1, 1, ph == 0)
            with pe.Fori(1, TILES // 2) as i:
                logits(2 * i, 0, False)
                logits(2 * i + 1, 1, False)
            pe.wait_ge(f_mask, ph + 1)
            m = MSK[:, :, :].rearrange("p t e -> p (t e)")
            half = TILES * NE // 2
            for a in range(2):
                pe.matmul(psR[a][:, 0:half], UT[:, :], m[:, a * half:(a + 1) * half], start=True, stop=True)
                mm = pe.matmul(psC[a][:, 0:half], ONESB[:, :], m[:, a * half:(a + 1) * half], start=True, stop=True)
            mm.then_inc(f_rank, 1)

            def turn(j, u, first):
                b = u % WBUFS
                pe.wait_ge(f_xl[b], w_count(ph, j, u))
                if not (first and ph == 0 and u < 2):
                    pe.wait_ge(f_xit, base + j - 1)
                pe.transpose(psXI[u % 2][:, 0:P], XI[:, b, :], IDF[:, :]).then_inc(f_xiT, 1)

            def up(j, u, first):
                b = u % WBUFS
                pe.wait_ge(f_wl[b], w_count(ph, j, u))
                pe.wait_ge(f_xit, base + j + 1)
                if not (first and ph == 0 and u < 2):
                    pe.wait_ge(f_gelu, base + j - 1)
                for c in range(FC):
                    mm = pe.matmul(psH[u % 2][:, c * P:(c + 1) * P], W[:, b, c * P:(c + 1) * P], XIT[:, u % 2, :],
                                   start=True, stop=True)
                mm.then_inc(f_up, 1)

            def down(j, u, first):
                b = u % WBUFS
                pe.wait_ge(f_gelu, base + j + 1)
                pe.wait_ge(f_bl[b], w_count(ph, j, u))
                if not (first and ph == 0 and u < 2):
                    pe.wait_ge(f_y, base + j - 1)
                for c in range(FC):
                    pe.matmul(psY[u % 2][:, 0:D], HT[:, u % 2, c, :], W[:, b, FF + c * D:FF + (c + 1) * D],
                              start=(c == 0), stop=False)
                pe.matmul(psY[u % 2][:, 0:D], ONER[:, :], B2[:, b, :], start=False, stop=True).then_inc(f_down, 1)

            def step(j, u, first, last=False):
                if not last:
                    turn(j + 1, (u + 1) % 12, first and u < 11)
                    up(j + 1, (u + 1) % 12, first and u < 11)
                down(j, u, first)

            pe.wait_ge(f_ej, ph + 1)
            pe.wait_ge(f_pos, ph + 1)
            turn(0, 0, True)
            up(0, 0, True)
            over_rows(pe, lambda j, u, first: step(j, u, first, isinstance(j, int) and j == ROW_TILES - 1))

        def ffn_dve(dve, ph):
            links = [LINKS * ph]
            done = f_link

            def link(ins):
                links[0] += 1
                ins.then_inc(done, 1)
                dve.wait_ge(done, links[0])

            def tile_at(x, T):
                return x[:, bass.ds(T, 1), :].rearrange("p a d -> p (a d)")

            def by_e(x):
                return x.rearrange("p t e -> p e t")

            def over_e(x):
                return x.unsqueeze(2).broadcast_to([P, TILES, NE])

            statistics(dve, 2 * ph + 1)

            def normalize(T, par, first):
                n = ph * TILES + T
                if not first:
                    dve.wait_ge(f_xsT, n - 1)
                    dve.wait_ge(f_xn, n - 1)
                dve.tensor_scalar(XS[:, par, :], tile_at(X, T), MEAN[:, bass.ds(T, 1)], RSD[:, bass.ds(T, 1)],
                                  ALU.subtract, ALU.mult).then_inc(f_xs, 1)

            def logits_copy(T, par):
                dve.wait_ge(f_lg, ph * TILES + T + 1)
                dve.tensor_copy(tile_at(LG, T), psXS[par][:, P:P + NE]).then_inc(f_lgc, 1)

            normalize(0, 0, ph == 0)
            normalize(1, 1, ph == 0)
            logits_copy(0, 0)
            with dve.Fori(1, TILES // 2) as i:
                normalize(2 * i, 0, False)
                logits_copy(2 * i - 1, 1)
                normalize(2 * i + 1, 1, False)
                logits_copy(2 * i, 0)
            logits_copy(TILES - 1, 1)
            dve.wait_ge(f_lgc, TILES * (ph + 1))
            for k in range(2):
                link(dve.tensor_reduce(TOP[:, k, :], LG[:, :, :], AX.X, ALU.max))
                link(dve.tensor_tensor(CAND[:, :, :], LG[:, :, :], over_e(TOP[:, k, :]), ALU.is_lt))
                link(dve.scalar_tensor_tensor(CAND[:, :, :], CAND[:, :, :], float(NE), 
                                              IOTA_E[:, :].unsqueeze(1).broadcast_to([P, TILES, NE]), ALU.mult, ALU.add))
                link(dve.tensor_reduce(IDX[:, :], CAND[:, :, :], AX.X, ALU.min))
                link(dve.tensor_tensor(O1H[k][:, :, :], IOTA_E[:, :].unsqueeze(1).broadcast_to([P, TILES, NE]),
                                       over_e(IDX[:, :]), ALU.is_equal))
                if k == 0:
                    link(dve.scalar_tensor_tensor(LG[:, :, :], O1H[0][:, :, :], NEG, LG[:, :, :], ALU.mult, ALU.add))
            dve.tensor_tensor(MSK[:, :, :], O1H[0][:, :, :], O1H[1][:, :, :], ALU.add).then_inc(f_mask, 1)
            dve.tensor_tensor(DIFF[:, :], TOP[:, 1, :], TOP[:, 0, :], ALU.subtract).then_inc(f_top, 1)
            dve.wait_ge(f_rank, ph + 1)
            half = TILES // 2
            for a in range(2):
                c = dve.tensor_copy(CNT[:, :, a * half:(a + 1) * half],
                                    by_e(psC[a][:, 0:half * NE].rearrange("p (t e) -> p t e", e=NE)))
            link(c)
            flat = "p e t -> p (e t)"
            link(dve.tensor_tensor_scan(INC[:, :, :].rearrange(flat), KEEP[:, :, :].rearrange(flat),
                                        CNT[:, :, :].rearrange(flat), 0.0, ALU.mult, ALU.add))
            link(dve.tensor_scalar(TI[:, :], INC[:, :, TILES - 1], float(P - 1), None, ALU.add))
            link(dve.tensor_scalar(TI[:, :], TI[:, :], 7, None, ALU.arith_shift_right))
            link(dve.tensor_copy(TF[:, :], TI[:, :]))
            link(dve.tensor_tensor_scan(TEND[:, :], ONES_E[:, :], TF[:, :], 0.0, ALU.mult, ALU.add))
            dve.tensor_tensor(TF[:, :], TEND[:, :], TF[:, :], ALU.subtract)
            link(dve.tensor_tensor(CMP[:, :, :], IOTA_J[:, :].unsqueeze(2).broadcast_to([1, ROW_TILES, NE]),
                                   TEND[0:1, :].unsqueeze(1).broadcast_to([1, ROW_TILES, NE]), ALU.is_ge))
            link(dve.tensor_reduce(EJF[:, :], CMP[:, :, :], AX.X, ALU.add))
            dve.tensor_scalar(EJ[:, :], EJF[:, :], float(NE - 1), None, ALU.min).then_inc(f_ej, 1)
            link(dve.tensor_tensor(INC[:, :, :], INC[:, :, :], CNT[:, :, :], ALU.subtract))
            link(dve.scalar_tensor_tensor(INC[:, :, :], TF[:, :].unsqueeze(2).broadcast_to([P, NE, TILES]), float(P),
                                          INC[:, :, :], ALU.mult, ALU.add))
            for a in range(2):
                t = slice(a * half, (a + 1) * half)
                c = dve.tensor_tensor(CAND[:, t, :], psR[a][:, 0:half * NE].rearrange("p (t e) -> p t e", e=NE),
                                      INC[:, :, t].rearrange("p e t -> p t e"), ALU.add)
            link(c)
            for k in range(2):
                c = dve.tensor_tensor(O1H[k][:, :, :], O1H[k][:, :, :], CAND[:, :, :], ALU.mult)
            link(c)
            for k in range(2):
                c = dve.tensor_reduce(POSF[:, :, k], O1H[k][:, :, :], AX.X, ALU.add)
            link(c)
            dve.tensor_copy(POS[:, :, :], POSF[:, :, :]).then_inc(f_pos, 1)
            dve.wait_ge(f_exp, ph + 1)
            link(dve.tensor_scalar(TOP[:, 0, :], EXPD[:, :], 1.0, None, ALU.add))
            link(dve.reciprocal(GATE[:, :, 0], TOP[:, 0, :]))
            dve.tensor_tensor(GATE[:, :, 1], EXPD[:, :], GATE[:, :, 0], ALU.mult)
            base = ph * ROW_TILES

            def xit(j, u, first):
                dve.wait_ge(f_xiT, base + j + 1)
                if not (first and ph == 0 and u < 2):
                    dve.wait_ge(f_up, base + j - 1)
                dve.tensor_copy(XIT[:, u % 2, :], psXI[u % 2][:, 0:P]).then_inc(f_xit, 1)

            def y_copy(j, u, first):
                dve.wait_ge(f_down, base + j + 1)
                if not (first and ph == 0 and u < 2):
                    dve.wait_ge(f_ys[u % 2], y_count(ph, j, u))
                dve.tensor_copy(Y[:, u % 2, :], psY[u % 2][:, 0:D]).then_inc(f_y, 1)

            def step(j, u, first, last=False):
                if not last:
                    xit(j + 1, (u + 1) % 12, first and u < 11)
                y_copy(j, u, first)

            xit(0, 0, True)
            over_rows(dve, lambda j, u, first: step(j, u, first, isinstance(j, int) and j == ROW_TILES - 1))
            per = TILES // YBUFS

            def combine(i, T, u):
                n = ph * TILES + T
                a = ACC[:, u % 2, :]
                dve.wait_ge(f_yg[u], (ph * per + i + 1) * 32)
                dve.scalar_tensor_tensor(a, YG[:, u, 0, :], GATE[:, bass.ds(T, 1), 0], tile_at(XN_ALL, T),
                                         ALU.mult, ALU.add).then_inc(f_acc0, 1)
                dve.wait_ge(f_acc0, n + 1)
                dve.scalar_tensor_tensor(a, YG[:, u, 1, :], GATE[:, bass.ds(T, 1), 1], a,
                                         ALU.mult, ALU.add).then_inc(f_acc, 1)
                dve.wait_ge(f_acc, n + 1)
                dve.tensor_tensor(tile_at(X, T), tile_at(X, T), a, ALU.add).then_inc(f_done, 1)

            with dve.Fori(0, per) as i:
                for u in range(YBUFS):
                    combine(i, YBUFS * i + u, u)
            dve.wait_ge(f_done, TILES * (ph + 1))

        def y_count(ph, j, u):
            before = (ROW_TILES // 2) * ph
            if isinstance(j, int):
                return 16 * (before + j // 2)
            return (j - u % 2) * 8 + 16 * before

        def over_fours(eng, slot):
            for T in range(-2, TPB):
                slot(T, T % TPB)
            with eng.Fori(1, TILES // TPB - 1) as i:
                for s in range(TPB):
                    slot(TPB * i + s, s)
            for T in range(TILES - TPB, TILES + 2):
                slot(T, T % TPB)

        def attb_load(sp):
            for dst, src in ((BQ_W[:, :], Wq), (BQ_B[:, :], bq), (BD_W[:, :], Wdown), (BD_B[:, :], bdown),
                             (BU_W[0:LATENT, :], Wup), (BU_W[LATENT:LATENT + 1, :], bup), (BO_W[:, :], Wout),
                             (BO_B[:, :], bout), (ROPE[:, :, :, :], rope)):
                sp.dma_start(dst, src).then_inc(b_w_in, 16)

        def attb_pool(pool):
            def rotate(T, s):
                par = s % 2
                x, r = QKR[:, par], ROT[:, par]
                half = HD // 2

                def table(i, a, b):
                    return ROPE[:, s, i, a:b].unsqueeze(1).unsqueeze(1).broadcast_to([P, 2, H, b - a])

                pool.wait_ge(b_qk, 2 * (T + 1))
                wait(pool, b_rot, T)
                wait(pool, b_prod, T - 1)
                pool.tensor_tensor(T1[:, :, :, :], x, table(0, 0, HD), ALU.mult).then_inc(b_rope1, 1)
                pool.tensor_tensor(T2[:, :, :, 0:half], x[:, :, :, half:HD], table(1, 0, half), ALU.mult).then_inc(b_rope1, 1)
                pool.tensor_tensor(T2[:, :, :, half:HD], x[:, :, :, 0:half], table(1, half, HD), ALU.mult).then_inc(b_rope1, 1)
                pool.wait_ge(b_rope1, 3 * (T + 1))
                pool.tensor_tensor(r, T1[:, :, :, :], T2[:, :, :, :], ALU.add).then_inc(b_rot, 1)

            def products(T, s):
                par = s % 2
                pool.wait_ge(b_rot, T + 1)
                wait(pool, b_att, T - 1)
                pool.tensor_tensor(PROD[:, par], ROT[:, par, 0].unsqueeze(2).broadcast_to([P, H, H, HD]),
                                   ROT[:, par, 1].unsqueeze(1).broadcast_to([P, H, H, HD]), ALU.mult).then_inc(b_prod, 1)

            def slot(T, s):
                if exists(T + 1):
                    rotate(T + 1, (s + 1) % TPB)
                    products(T + 1, (s + 1) % TPB)

            over_fours(pool, slot)

        def attb_pe(pe):
            def project(T, s):
                par = s % 2
                ps_ = psP[par]
                pe.wait_ge(b_xs, T + 1)
                wait(pe, b_v, T - 1)
                pe.transpose(ps_[:, 0:P], XS[:, par, :], IDF[:, :]).then_inc(b_xsT, 1)
                pe.wait_ge(b_xst, T + 1)
                pe.matmul(ps_[:, 0:D], XST[:, par, :], BQ_W[:, :], start=True, stop=False)
                pe.matmul(ps_[:, 0:D], ONER[:, :], BQ_B[:, :], start=False, stop=True)
                pe.matmul(ps_[0:LATENT, D:D + P], BD_W[:, :], XST[:, par, :], start=True, stop=True).then_inc(b_ql, 1)
                pe.wait_ge(b_lat, T + 1)
                pe.matmul(ps_[:, 2 * D:4 * D], LT[:, par, :], BU_W[:, :], start=True, stop=True).then_inc(b_kv, 1)

            def finish(T, s):
                par = s % 2
                pe.wait_ge(b_wv, T + 1)
                wait(pe, b_x, T - 1)
                pe.transpose(psF[par][:, 0:P], BWV[:, par, :], IDF[:, :]).then_inc(b_wvT, 1)
                pe.wait_ge(b_wvt, T + 1)
                pe.matmul(psF[par][:, 0:D], BWVT[:, par, :], BO_W[:, :], start=True, stop=False)
                pe.matmul(psF[par][:, 0:D], ONER[:, :], BO_B[:, :], start=False, stop=True).then_inc(b_o, 1)

            def slot(T, s):
                if exists(T + 2):
                    project(T + 2, (s + 2) % TPB)
                if exists(T - 1):
                    finish(T - 1, (s - 1) % TPB)

            over_fours(pe, slot)

        def attb_act(act):
            def copies(T, s):
                par = s % 2
                ps_ = psP[par]
                act.wait_ge(b_xsT, T + 1)
                act.activation(XST[:, par, :], ps_[:, 0:P], ACT.Copy).then_inc(b_xst, 1)
                act.wait_ge(b_ql, T + 1)
                act.activation(LT[0:LATENT, par, :], ps_[0:LATENT, D:D + P], ACT.Identity, bias=BD_B[:, :]).then_inc(b_lat, 1)
                act.wait_ge(b_kv, T + 1)
                kv = ps_[:, 2 * D:4 * D].rearrange("p (h c) -> p h c", h=H)
                wait(act, b_rot, T - 1)
                act.activation(QKR[:, par, 0], ps_[:, 0:D].rearrange("p (h c) -> p h c", h=H), ACT.Copy).then_inc(b_qk, 1)
                act.activation(QKR[:, par, 1], kv[:, :, 0:HD], ACT.Copy).then_inc(b_qk, 1)
                wait(act, b_p2, T - 3)
                act.activation(VB[:, s % 4], kv[:, :, HD:2 * HD], ACT.Copy).then_inc(b_v, 1)

            def slot(T, s):
                if exists(T):
                    act.wait_ge(b_sh, T + 1)
                    wait(act, b_red2, T - 1)
                    act.activation(EX[:, s % 2], SH[:, s % 2], ACT.Exp, scale=float(HD) ** -0.5).then_inc(b_ex, 1)
                if exists(T + 2):
                    copies(T + 2, (s + 2) % TPB)
                if exists(T - 1):
                    act.wait_ge(b_wvT, T)
                    act.activation(BWVT[:, (s - 1) % 2, :], psF[(s - 1) % 2][:, 0:P], ACT.Copy).then_inc(b_wvt, 1)

            over_fours(act, slot)

        def attb_dve(dve):
            def tile_at(x, T):
                return x[:, bass.ds(T, 1), :].rearrange("p a d -> p (a d)")

            def normalize(T, s):
                wait(dve, b_xsT, T - 1)
                dve.tensor_scalar(XS[:, s % 2, :], tile_at(X, T), MEAN[:, bass.ds(T, 1)], RSD[:, bass.ds(T, 1)],
                                  ALU.subtract, ALU.mult).then_inc(b_xs, 1)

            def scores(T, s):
                dve.wait_ge(b_prod, T + 1)
                wait(dve, b_sh, T)
                dve.tensor_reduce(ATT[:, :, :], PROD[:, s % 2], AX.X, ALU.add).then_inc(b_att, 1)
                dve.wait_ge(b_att, T + 1)
                dve.tensor_reduce(AMX[:, :], ATT[:, :, :], AX.X, ALU.max).then_inc(b_max, 1)
                dve.wait_ge(b_max, T + 1)
                wait(dve, b_ex, T - 1)
                dve.tensor_tensor(SH[:, s % 2], ATT[:, :, :], AMX[:, :].unsqueeze(2).broadcast_to([P, H, H]),
                                  ALU.subtract).then_inc(b_sh, 1)

            def values(T, s):
                dve.wait_ge(b_ex, T + 1)
                wait(dve, b_wv, T)
                dve.tensor_tensor(PROD2[:, :, :, :], EX[:, s % 2].unsqueeze(2).broadcast_to([P, H, HD, H]),
                                  VB[:, s % 4].rearrange("p g d -> p d g").unsqueeze(1).broadcast_to([P, H, HD, H]),
                                  ALU.mult).then_inc(b_p2, 1)
                dve.tensor_reduce(ASUM[:, :], EX[:, s % 2], AX.X, ALU.add).then_inc(b_red2, 1)
                dve.wait_ge(b_p2, T + 1)
                dve.tensor_reduce(AO[:, :, :], PROD2[:, :, :, :], AX.X, ALU.add).then_inc(b_red2b, 1)
                dve.wait_ge(b_red2, T + 1)
                dve.reciprocal(ARS[:, :], ASUM[:, :]).then_inc(b_rs, 1)
                dve.wait_ge(b_rs, T + 1)
                dve.wait_ge(b_red2b, T + 1)
                wait(dve, b_wvT, T - 1)
                dve.tensor_tensor(BWV[:, s % 2, :].rearrange("p (h d) -> p h d", h=H), AO[:, :, :],
                                  ARS[:, :].unsqueeze(2).broadcast_to([P, H, HD]), ALU.mult).then_inc(b_wv, 1)

            def slot(T, s):
                if exists(T + 2):
                    normalize(T + 2, (s + 2) % TPB)
                if exists(T):
                    scores(T, s)
                if exists(T - 1):
                    values(T - 1, (s - 1) % TPB)
                if exists(T - 2):
                    dve.wait_ge(b_o, T - 1)
                    dve.tensor_tensor(tile_at(X, T - 2), tile_at(X, T - 2), psF[s % 2][:, 0:D], ALU.add).then_inc(b_x, 1)

            over_fours(dve, slot)
            dve.wait_ge(b_x, TILES)

        @block.sync
        def _(sp):
            for b in range(BATCH):
                sp.dma_start(X[:, b * TPB:(b + 1) * TPB, :], h_v[:, b * TPB:(b + 1) * TPB, :]).then_inc(x_in[b], 16)
            sp.dma_start(WQ[:, :], Wqvk).then_inc(w_in, 16)
            sp.dma_start(WO[:, :], Wo).then_inc(w_in, 16)
            ffn_consts_sp(sp)
            attb_load(sp)
            ffn_sp(sp, 0)
            ffn_sp(sp, 1)
            sp.wait_ge(f_done, 2 * TILES)
            sp.dma_start(out_v, X[:, :, :]).then_inc(out_sent, 16)
            sp.wait_ge(out_sent, 16)

        def split_parts(pool, T, par):
            q, k = (QK[:, i, :].rearrange("p (h d) -> p h d", h=H) for i in range(2))
            qs, ks = (m[:, :, 0:K48].rearrange("p h (c d) -> p h c d", c=SLOTS) for m in (QS[:, par], KS))
            rq, rk = (R1[:, i, :].rearrange("p (h d) -> p h d", h=H) for i in range(2))

            def spread(x, n):
                return x.unsqueeze(2).broadcast_to([P, H, n, HD])

            def ones(n):
                return ONE[:, :].unsqueeze(2).unsqueeze(3).broadcast_to([P, H, n, HD])

            wait(pool, q2T_done, T - 1)
            pool.tensor_tensor(QS[:, par, :, K48:K48 + 2], ZERO[:, :].rearrange("p (h c) -> p h c", h=H),
                               ZERO[:, :].rearrange("p (h c) -> p h c", h=H), ALU.mult).then_inc(hi_done, 1)
            pool.wait_ge(qk_copied, 2 * T + 2)
            wait(pool, kT_done, T)
            pool.tensor_tensor(qs[:, :, 0:3, :], spread(q, 3), ones(3), ALU.mult).then_inc(hi_done, 1)
            pool.tensor_tensor(ks[:, :, 2:5, :], spread(k, 3), ones(3), ALU.mult).then_inc(hi_done, 1)
            pool.wait_ge(hi_done, 3 * T + 3)
            pool.tensor_tensor(rq, q, qs[:, :, 2, :], ALU.subtract).then_inc(r1_done, 1)
            pool.tensor_tensor(rk, k, ks[:, :, 2, :], ALU.subtract).then_inc(r1_done, 1)
            pool.wait_ge(r1_done, 2 * T + 2)
            pool.tensor_tensor(qs[:, :, 3:6:2, :], spread(rq, 2), ones(2), ALU.mult).then_inc(mid_done, 1)
            pool.tensor_tensor(ks[:, :, 0:6:5, :], spread(rk, 2), ones(2), ALU.mult).then_inc(mid_done, 1)
            pool.wait_ge(mid_done, 2 * T + 2)
            pool.tensor_tensor(qs[:, :, 4, :], rq, qs[:, :, 5, :], ALU.subtract).then_inc(parts_done, 1)
            pool.tensor_tensor(ks[:, :, 1, :], rk, ks[:, :, 5, :], ALU.subtract).then_inc(parts_done, 1)

        @block.gpsimd
        def _(pool):
            pool.memset(NHALF[:, :], -0.5).then_inc(const_a, 1)
            pool.memset(ZERO[:, :], 0.0).then_inc(const_a, 1)
            pool.memset(ONE[:, :], 1.0).then_inc(const_a, 1)
            pool.memset(IDF[:, :], 0.0).then_inc(const_a, 1)
            pool.memset(IDB[:, :], 0.0).then_inc(const_a, 1)
            pool.memset(MASK[:, :], 0.0).then_inc(const_a, 1)
            pool.memset(MASKT[:, :], 0.0).then_inc(const_a, 1)
            pool.memset(QS[:, :, :, :], 0.0).then_inc(const_a, 1)
            pool.memset(KS[:, :, 0:K48 + 2], 1.0).then_inc(const_a, 1)
            pool.memset(KS[:, :, K48 + 2:HEADW], 0.0).then_inc(const_a, 1)
            pool.wait_ge(const_a, 10)
            for m in (IDF, IDB):
                pool.affine_select(out=m[:, :], in_=m[:, :], compare_op=ALU.not_equal, fill=1.0, base=0,
                                   pattern=[[-1, P]], channel_multiplier=1).then_inc(const_ready, 1)
            for m, sign in ((MASK, 1), (MASKT, -1)):
                pool.affine_select(out=m[:, :], in_=m[:, :], compare_op=ALU.is_ge, fill=NEG, base=0,
                                   pattern=[[-sign, P]], channel_multiplier=sign).then_inc(const_ready, 1)
            ffn_consts_pool(pool)
            deviations(pool, 0)
            split_parts(pool, 0, 0)
            split_parts(pool, 1, 1)
            with pool.Fori(1, TILES // 2) as i:
                split_parts(pool, 2 * i, 0)
                split_parts(pool, 2 * i + 1, 1)
            ffn_pool(pool, 0)
            deviations(pool, 2)
            attb_pool(pool)
            ffn_pool(pool, 1)

        @block.tensor
        def _(pe):
            def x_transpose(T):
                pe.wait_ge(xn_done, T + 1)
                wait(pe, x1_done, T - 3)
                pe.transpose(psM[:, 0:P], XN[:, :], IDF[:, :]).then_inc(xT_done, 1)

            def project(T):
                pe.wait_ge(xT_copied, T + 1)
                pe.matmul(psM[:, 0:3 * D], XT[:, :], WQ[:, :], start=True, stop=True).then_inc(qkv_done, 1)

            def transposes(src, done):
                for g in range(PAIRS):
                    mm = pe.transpose(psT[:, g, :], src[:, 2 * g:2 * g + 2, :], IDB[:, :])
                mm.then_inc(done, 1)

            def q_transposes(T, r):
                pe.wait_ge(parts_done, 2 * T + 2)
                wait(pe, q2T_copied, T - 1)
                wait(pe, kT_copied, T)
                transposes(QS[:, r % 2], qT_done)

            def k_transposes(T):
                pe.wait_ge(qT_copied, T + 1)
                transposes(KS, kT_done)

            def q2_transposes(T, r):
                pe.wait_ge(m_done, T + 1)
                wait(pe, kT_copied, min(T + 2, TILES) if isinstance(T, int) else T + 2)
                transposes(QS[:, r % 2], q2T_done)

            def scoresA(T, r, k):
                s, g, rows = r % TPB, k // 2, slice(HEADW * (k % 2), HEADW * (k % 2 + 1))
                if k == 0:
                    pe.wait_ge(kT_copied, T + 1)
                wait(pe, max_done, H * T + k - 1)
                k0 = r - s
                for t in range(s + 1):
                    pe.matmul(psA[k % 2][:, t * P:(t + 1) * P], QT[rows, r % 2, g, :], KT[rows, k0 + t, g, :],
                              start=(t == 0), stop=False, skip_group_check=True)
                pe.matmul(psA[k % 2][:, s * P:(s + 1) * P], IDB[:, :], MASK[:, :], start=False, stop=True,
                          skip_group_check=True).then_inc(scoresA_done, 1)

            def scoresB(T, r, k):
                s, g, rows = r % TPB, k // 2, slice(HEADW * (k % 2), HEADW * (k % 2 + 1))
                if k == 0:
                    pe.wait_ge(q2T_copied, T + 1)
                wait(pe, exp_done, H * T + k - 1)
                for t in range(s + 1):
                    pe.matmul(psB[k % 2][:, t * P:(t + 1) * P], KT[rows, r - s + t, g, :], QT2[rows, r % 2, g, :],
                              start=(t == 0), stop=False, skip_group_check=True)
                pe.matmul(psB[k % 2][:, s * P:(s + 1) * P], IDB[:, :], MASKT[:, :], start=False, stop=True,
                          skip_group_check=True).then_inc(scoresB_done, 1)

            def pv(T, r, q):
                s = r % TPB
                pe.wait_ge(exp_done, H * T + 4 * q + 4)
                if q == 0:
                    pe.wait_ge(v_copied, T + 1)
                    wait(pe, o_copied, T)
                for t in range(s + 1):
                    for j in range(4):
                        mm = pe.matmul(psO[32 * j:32 * j + 32, q, :], V32[:, r - s + t, 4 * q + j, :],
                                       PT[:, q % 2, j, t * P:(t + 1) * P], start=(t == 0), stop=(t == s))
                mm.then_inc(pv_done, 1)

            def o_transposes(T):
                pe.wait_ge(o_copied, T + 1)
                pe.wait_ge(v_copied, min(T + 4, TILES) if isinstance(T, int) else T + 4)
                wait(pe, x1_done, T)
                for q in range(G4):
                    mm = pe.transpose(psM[:, q * P:(q + 1) * P], OS[:, q, :], IDF[:, :])
                mm.then_inc(oT_done, 1)

            def wv_transpose(T):
                pe.wait_ge(wv_done, T + 1)
                pe.transpose(psM[:, 0:P], WV[:, :], IDF[:, :]).then_inc(wvT_done, 1)

            def out_project(T):
                pe.wait_ge(wvT_copied, T + 1)
                pe.matmul(psM[:, 0:D], WVT[:, :], WO[:, :], start=True, stop=True).then_inc(wo_done, 1)

            def slot(T, r):
                before = (r - 1) % RING
                for k in range(H):
                    if exists(T + 2) and k == 0:
                        x_transpose(T + 2)
                    if exists(T) and k == 1:
                        q2_transposes(T, r)
                    if exists(T + 2) and k == 2:
                        project(T + 2)
                    if exists(T + 1):
                        scoresA(T + 1, (r + 1) % RING, k)
                    if k >= LAG and exists(T):
                        scoresB(T, r, k - LAG)
                    if k < LAG and exists(T - 1):
                        scoresB(T - 1, before, k + H - LAG)
                    if k in (0, 4) and exists(T - 1):
                        pv(T - 1, before, k // 4 + 2)
                    if k in (8, 12) and exists(T):
                        pv(T, r, k // 4 - 2)
                    if exists(T - 1):
                        if k == 6:
                            o_transposes(T - 1)
                        if k == 8:
                            wv_transpose(T - 1)
                        if k == 10:
                            out_project(T - 1)
                    if exists(T + 2):
                        if k == 13:
                            q_transposes(T + 2, (r + 2) % RING)
                        if k == 14:
                            k_transposes(T + 2)

            pe.wait_ge(const_ready, 4)
            pe.wait_ge(w_in, 32)
            pe.wait_ge(const_v, 2)
            over_tiles(pe, slot)
            pe.wait_ge(x1_done, TILES)
            pe.wait_ge(f_const, 10)
            pe.wait_ge(f_w_in, 32)
            ffn_pe(pe, 0)
            pe.wait_ge(b_w_in, 16 * 9)
            pe.wait_ge(f_y, ROW_TILES)
            attb_pe(pe)
            pe.wait_ge(b_x, TILES)
            ffn_pe(pe, 1)

        @block.scalar
        def _(act):
            def xT_copy(T):
                act.wait_ge(xT_done, T + 1)
                act.activation(XT[:, :], psM[:, 0:P], ACT.Copy).then_inc(xT_copied, 1)

            def qkv_copy(T, r):
                act.wait_ge(qkv_done, T + 1)
                wait(act, parts_done, 2 * T)
                act.activation(QK[:, 0, :], psM[:, 0:D], ACT.Copy, scale=float(D) ** -0.5).then_inc(qk_copied, 1)
                act.activation(QK[:, 1, :], psM[:, 2 * D:3 * D], ACT.Copy).then_inc(qk_copied, 1)
                act.activation(V32[:, r, :, 0:HD], psM[:, D:2 * D].rearrange("p (h d) -> p h d", h=H),
                               ACT.Copy).then_inc(v_copied, 1)

            def qT_copy(T, r):
                act.wait_ge(qT_done, T + 1)
                act.activation(QT[:, r % 2, :, :], psT, ACT.Copy).then_inc(qT_copied, 1)

            def exps(T, r, k):
                n = (r % TPB + 1) * P
                q = k // 4
                if k % 4 == 0:
                    wait(act, pv_done, G4 * T + q - 1)
                act.wait_ge(scoresB_done, H * T + k + 1)
                act.activation(PT[:, q % 2, k % 4, 0:n], psB[k % 2][:, 0:n], ACT.Exp).then_inc(exp_done, 1)

            def o_copy(T):
                act.wait_ge(pv_done, G4 * (T + 1))
                wait(act, oT_done, T)
                act.activation(OS[:, :, :], psO[:, :, :], ACT.Copy).then_inc(o_copied, 1)

            def wvT_copy(T):
                act.wait_ge(wvT_done, T + 1)
                act.activation(WVT[:, :], psM[:, 0:P], ACT.Copy).then_inc(wvT_copied, 1)

            def slot(T, r):
                before = (r - 1) % RING
                for k in range(H):
                    if exists(T + 2) and k == 0:
                        xT_copy(T + 2)
                    if exists(T + 2) and k == 2:
                        qkv_copy(T + 2, (r + 2) % RING)
                    if k >= LAG and exists(T):
                        exps(T, r, k - LAG)
                    if k < LAG and exists(T - 1):
                        exps(T - 1, before, k + H - LAG)
                    if exists(T - 1):
                        if k == 4:
                            o_copy(T - 1)
                        if k == 8:
                            wvT_copy(T - 1)
                    if exists(T + 2) and k == 13:
                        qT_copy(T + 2, (r + 2) % RING)

            over_tiles(act, slot)
            ffn_act(act, 0)
            act.wait_ge(b_w_in, 16 * 9)
            attb_act(act)
            ffn_act(act, 1)

        @block.vector
        def _(dve):
            def tile_of(x, T):
                return x[:, bass.ds(T, 1), :].rearrange("p a d -> p (a d)")

            def normalize(T):
                wait(dve, xT_done, T)
                dve.tensor_scalar(XN[:, :], tile_of(X, T), MEAN[:, bass.ds(T, 1)], RSD[:, bass.ds(T, 1)],
                                  ALU.subtract, ALU.mult).then_inc(xn_done, 1)

            def kT_copy(T, r):
                dve.wait_ge(kT_done, T + 1)
                dve.tensor_copy(KT[:, r, :, :], psT).then_inc(kT_copied, 1)

            def q2T_copy(T, r):
                dve.wait_ge(q2T_done, T + 1)
                dve.tensor_copy(QT2[:, r % 2, :, :], psT).then_inc(q2T_copied, 1)

            def maxes(T, r, k):
                n = (r % TPB + 1) * P
                dve.wait_ge(scoresA_done, H * T + k + 1)
                dve.tensor_reduce(NM[:, r % 2, k:k + 1], psA[k % 2][:, 0:n], AX.X, ALU.max,
                                  negate=True).then_inc(max_done, 1)

            def m_parts(T, r):
                dve.wait_ge(max_done, H * (T + 1))
                dve.wait_ge(qT_done, T + 1)
                dve.tensor_copy(QS[:, r % 2, :, K48], NM[:, r % 2, :]).then_inc(m_hi_done, 1)
                dve.wait_ge(m_hi_done, T + 1)
                dve.tensor_tensor(QS[:, r % 2, :, K48 + 1], NM[:, r % 2, :], QS[:, r % 2, :, K48],
                                  ALU.subtract).then_inc(m_done, 1)

            def weigh(T):
                o = psM[:, :].rearrange("p (h d) -> p h d", h=H)
                dve.wait_ge(oT_done, T + 1)
                dve.reciprocal(RS[:, :], o[:, :, HD]).then_inc(rs_done, 1)
                dve.wait_ge(rs_done, T + 1)
                wait(dve, wvT_done, T)
                dve.tensor_tensor(WV[:, :].rearrange("p (h d) -> p h d", h=H), o[:, :, 0:HD],
                                  RS[:, :].unsqueeze(2).broadcast_to([P, H, HD]), ALU.mult).then_inc(wv_done, 1)

            def add_attention(T):
                dve.wait_ge(wo_done, T + 1)
                dve.tensor_tensor(tile_of(X, T), tile_of(X, T), psM[:, 0:D], ALU.add).then_inc(x1_done, 1)

            def slot(T, r):
                for k in range(H):
                    if exists(T) and k == 0:
                        m_parts(T, r)
                    if exists(T + 2) and k == 0:
                        normalize(T + 2)
                    if exists(T) and k == 1:
                        q2T_copy(T, r)
                    if exists(T + 1):
                        maxes(T + 1, (r + 1) % RING, k)
                    if exists(T - 1):
                        if k == 6:
                            weigh(T - 1)
                        if k == 10:
                            add_attention(T - 1)
                    if exists(T + 2) and k == 14:
                        kT_copy(T + 2, (r + 2) % RING)

            dve.memset(V32[:, :, :, HD + 1:32], 0.0).then_inc(const_v, 1)
            dve.memset(V32[:, :, :, HD], 1.0).then_inc(const_v, 1)
            dve.memset(LT[LATENT:LATENT + 1, :, :], 1.0).then_inc(b_const, 1)
            for b in range(BATCH):
                dve.wait_ge(x_in[b], 16)
            statistics(dve, 0)
            over_tiles(dve, slot)
            dve.wait_ge(x1_done, TILES)
            dve.wait_ge(f_const, 10)
            ffn_dve(dve, 0)
            statistics(dve, 2)
            attb_dve(dve)
            ffn_dve(dve, 1)


_OUTS = [((BATCH, SEQ, D), 'float32')]


def rope_table(np):
    inv = (1.0 / 10000.0 ** (np.arange(0, HD, 2, dtype=np.float32) / HD)).astype(np.float32)
    angle = np.arange(SEQ, dtype=np.float32)[:, None] * inv[None, :]
    cos, sin = np.cos(angle), np.sin(angle)
    table = np.stack([np.concatenate([cos, cos], 1), np.concatenate([-sin, sin], 1)], 1)
    return table.reshape(TPB, P, 2, HD).transpose(1, 0, 2, 3).astype(np.float32)


def kernel(**inputs):
    import numpy as _np
    import concourse.bacc as _bacc
    from concourse import mybir as _mybir
    from concourse.bass_utils import run_bass_kernel_spmd as _run

    nc = _bacc.Bacc("TRN2", target_bir_lowering=False, num_devices=1)
    w1, w2, b1 = (_np.asarray(inputs[f"L0_ffn_{n}"]) for n in ("w1", "w2", "b1"))
    given = {
        "h": inputs["L0_attn_a_h"],
        "Wqvk": inputs["L0_attn_a_Wqvk"],
        "Wo": inputs["L0_attn_a_Wo"],
        "gate_w": inputs["L0_ffn_gate_w"],
        "gate_b": _np.asarray(inputs["L0_ffn_gate_b"]).reshape(1, NE),
        "wpack": _np.concatenate([w1, w2.reshape(NE, FC, P, D).transpose(0, 2, 1, 3).reshape(NE, P, FC * D),
                                  b1.reshape(NE, FC, P).transpose(0, 2, 1)], axis=2),
        "b2": inputs["L0_ffn_b2"],
        "Wq": inputs["L0_attn_b_Wq"],
        "bq": _np.asarray(inputs["L0_attn_b_bq"]).reshape(1, D),
        "Wdown": inputs["L0_attn_b_Wdown"],
        "bdown": _np.asarray(inputs["L0_attn_b_bdown"]).reshape(LATENT, 1),
        "Wup": inputs["L0_attn_b_Wup"],
        "bup": _np.asarray(inputs["L0_attn_b_bup"]).reshape(1, 2 * D),
        "Wout": inputs["L0_attn_b_Wout"],
        "bout": _np.asarray(inputs["L0_attn_b_bout"]).reshape(1, D),
        "rope": rope_table(_np),
    }
    arrays, args = {}, []
    for name, x in given.items():
        a = _np.ascontiguousarray(x)
        arrays[f"in_{name}_dram"] = a
        args.append(nc.dram_tensor(f"in_{name}_dram", a.shape, _mybir.dt.from_np(a.dtype), kind="ExternalInput").ap())
    for i, (shape, dtype) in enumerate(_OUTS):
        dt = _mybir.dt.from_np(_np.dtype(dtype))
        args.append(nc.dram_tensor(f"out_{i}_dram", shape, dt, kind="ExternalOutput").ap())
    hybrid_layer(nc, *args)
    r = _run(nc, [arrays], core_ids=[0])
    return r.results[0]["out_0_dram"]
```

```python
from contextlib import ExitStack

import concourse.bass as bass
from concourse import mybir

F32 = mybir.dt.float32
BF16 = mybir.dt.bfloat16
I32 = mybir.dt.int32
U32 = mybir.dt.uint32
ALU = mybir.AluOpType
ACT = mybir.ActivationFunctionType
AX = mybir.AxisListType

P = 128
D = 128
BATCH, SEQ = 8, 512
TILES = BATCH * SEQ // P
TPB = SEQ // P
H, HD = 16, 8
PAIRS = H // 2
G4 = H // 4
LAG = 6
NORM_AT, X_AT, QKV_AT, QT_AT, KT_AT = 0, 1, 2, 12, 14
MAX_AT = 2
PV_AFTER = LAG + 5
O_COPY_AT, O_AT, WV_AT, OUT_AT = LAG + 1, LAG + 3, LAG + 5, LAG + 7
STATS_AT, RN_AT, RT_AT, RL_AT, TOP_AT, RANK_AT, ROWS_AT = 14, 17, 19, 21, 23, 36, 39
RING = 2 * TPB
EPS = 1e-5
NEG = -1e30
SLOTS = 6
HEADW = 64
K48 = SLOTS * HD


LATENT = 32
NE, FF = 24, 512
FC = FF // P
GT = 4
TOKENS = TILES * P
REGION = TOKENS + P
DUMMY = NE * REGION
ROW_W = D + 2
STEP = 8
ROW_TILES = STEP * -(-((2 * TOKENS - NE) // P + NE) // STEP)
B2_EXPERTS = 6
NOWHERE = 2 * 2 * TOKENS


def hybrid_layer(nc, h, Wqvk, Wo, gate_w, gate_b, w1, w2pack, b1, b2, Wq, bq, Wdown, bdown, Wup, bup, Wout, bout, rope, out):
    ctx = ExitStack()
    with ctx:
        def sb(name, shape, dt=F32):
            return ctx.enter_context(nc.sbuf_tensor(name, shape, dt))

        def ps(name, shape, dt=F32):
            return ctx.enter_context(nc.psum_tensor(name, shape, dt))

        def sem(name):
            return ctx.enter_context(nc.semaphore(name))

        X = sb("X", [P, TILES, D])
        NHALF = sb("NHALF", [P, TILES])
        ZERO = sb("ZERO", [P, 2 * H])
        ONE = sb("ONE", [P, 1])
        IDF = sb("IDF", [P, P])
        IDB = sb("IDB", [P, P], BF16)
        MASK = sb("MASK", [P, P], BF16)
        MASKT = sb("MASKT", [P, P], BF16)
        WQ = sb("WQ", [D, 3 * D])
        WO = sb("WO", [D, D])
        XN = sb("XN", [P, D])
        XT = sb("XT", [D, P])
        QK = sb("QK", [P, 2, D])
        R1 = sb("R1", [P, 2, D])
        QS = sb("QS", [P, 2, H, HEADW], BF16)
        KS = sb("KS", [P, H, HEADW], BF16)
        QT = sb("QT", [P, 2, PAIRS, P], BF16)
        QT2 = sb("QT2", [P, 2, PAIRS, P], BF16)
        KT = sb("KT", [P, RING, PAIRS, P], BF16)
        V32 = sb("V32", [P, RING, H, 32])
        NM = sb("NM", [P, 2, H])
        PT = sb("PT", [P, 2, 4, SEQ])
        OS = sb("OS", [P, G4, P])
        RS = sb("RS", [P, H])
        WV = sb("WV", [P, D])
        WVT = sb("WVT", [D, P])


        XG = sb("XG", [P, GT, 2, ROW_W])
        XGT = sb("XGT", [D, GT, P])
        XS = sb("XS", [P, 2, D])
        XST = sb("XST", [D, 2, P])
        GW = sb("GW", [D, NE])
        GB = sb("GB", [P, NE])
        ONER = sb("ONER", [1, P])
        UT = sb("UT", [P, P], BF16)
        ONESB = sb("ONESB", [P, P], BF16)
        STAT = sb("STAT", [P, TILES, 6])
        MEAN = sb("MEAN", [P, TILES])
        VAR = sb("VAR", [P, TILES])
        DIFF = sb("DIFF", [P, TILES])
        RSD = sb("RSD", [P, TILES])
        STG = sb("STG", [P, GT, 6])
        MEG = sb("MEG", [P, GT])
        VAG = sb("VAG", [P, GT])
        DIG = sb("DIG", [P, GT])
        RSG = sb("RSG", [P, GT])
        LG = sb("LG", [P, GT, NE])
        IOTA_E = sb("IOTA_E", [P, NE])
        IOTA_J = sb("IOTA_J", [ROW_TILES, 1])
        DEST = sb("DEST", [P, TILES, 2], I32)
        O1H = [sb(f"O1H{k}", [P, GT, NE]) for k in range(2)]
        CAND = sb("CAND", [P, GT, NE])
        MSK = sb("MSK", [P, GT, NE], BF16)
        TOP = sb("TOP", [P, 2, GT])
        TDIF = sb("TDIF", [P, GT])
        IDX = sb("IDX", [P, GT])
        EXPD = sb("EXPD", [P, GT])
        EXP1 = sb("EXP1", [P, GT])
        RUN0 = sb("RUN0", [P, NE])
        RUN = sb("RUN", [P, NE])
        POSF = sb("POSF", [P, GT, 2])
        POS = sb("POS", [P, GT, 2], I32)
        CE = sb("CE", [ROW_TILES, NE])
        TI = sb("TI", [ROW_TILES, NE], I32)
        TF = sb("TF", [ROW_TILES, NE])
        TEND = sb("TEND", [ROW_TILES, NE])
        ONES_E = sb("ONES_E", [ROW_TILES, NE])
        CMP = sb("CMP", [ROW_TILES, NE])
        ERF = sb("ERF", [ROW_TILES, 2])
        EJ = sb("EJ", [1, ROW_TILES], I32)
        RJ = sb("RJ", [1, ROW_TILES], I32)
        PADR = sb("PADR", [1, NE], I32)
        PAD = sb("PAD", [P, ROW_W])
        B1 = sb("B1", [P, NE * FC])
        W2 = sb("W2", [P, NE, FC * D])
        B2P = sb("B2P", [96, NE * D], BF16)
        B2F = sb("B2F", [96, B2_EXPERTS * D])
        SEL3 = sb("SEL3", [96, P], BF16)
        XI = sb("XI", [P, STEP, ROW_W])
        XI_I, XG_I, PAD_I = (x.bitcast(I32) for x in (XI[:, :, :], XG[:, :, :, :], PAD[:, :]))
        XIT = sb("XIT", [D, 2, P])
        in_keys = KT[:, :, :, :].rearrange("p r g t -> p (r g t)").bitcast(F32)
        W1 = in_keys.rearrange("p (a n) -> p a n", a=STEP)
        HT = QT[:, :, :, :].rearrange("p a g t -> p (a g t)").bitcast(F32).rearrange("p (a c t) -> p a c t", a=2, c=FC)
        SETTLE = sb("SETTLE", [P, 1])
        OVER_D = sb("OVER_D", [P, GT])
        EPS4 = sb("EPS4", [P, GT])
        Y = sb("Y", [P, 4, D])
        YC = in_keys[:, 4 * GT * D:8 * GT * D].rearrange("p (a k t d) -> p a k t d", a=2, k=2, t=GT)

        f_w_in = sem("f_w_in")
        f_const = sem("f_const")
        f_dummy = sem("f_dummy")
        f_stat = sem("f_stat")
        f_stat1 = sem("f_stat1")
        f_stat2 = sem("f_stat2")
        f_var = sem("f_var")
        f_eps = sem("f_eps")
        f_rstd = sem("f_rstd")
        r_stat = sem("r_stat")
        r_s1 = sem("r_s1")
        r_s2 = sem("r_s2")
        r_var = sem("r_var")
        r_eps0 = sem("r_eps0")
        r_g1 = sem("r_g1")
        r_g2 = sem("r_g2")
        r_eps = sem("r_eps")
        r_rstd = sem("r_rstd")
        r_xg = sem("r_xg")
        r_xg2 = sem("r_xg2")
        r_xadd = sem("r_xadd")
        r_xT = sem("r_xT")
        r_xTc = sem("r_xTc")
        r_lg = sem("r_lg")
        r_link = sem("r_link")
        r_mask = sem("r_mask")
        r_top = sem("r_top")
        r_exp = sem("r_exp")
        r_rank = sem("r_rank")
        r_pos = sem("r_pos")
        r_gate = sem("r_gate")
        r_scat = sem("r_scat")
        e_link = sem("e_link")
        e_flat = sem("e_flat")
        e_turned = sem("e_turned")
        w2_in = sem("w2_in")
        b2_in = sem("b2_in")
        b2_split = sem("b2_split")
        e_settled = sem("e_settled")
        e_pad = sem("e_pad")
        e_tables = sem("e_tables")
        e_padded = sem("e_padded")
        f_load = [sem(f"f_load{i}") for i in range(STEP)]
        f_xiT = sem("f_xiT")
        f_xit = sem("f_xit")
        f_up = sem("f_up")
        f_gelu = sem("f_gelu")
        f_down = sem("f_down")
        f_y = sem("f_y")
        f_ys = [sem(f"f_ys{i}") for i in range(STEP)]
        f_yc = [sem(f"f_yc{i}") for i in range(2)]
        f_ysum = sem("f_ysum")
        f_done = sem("f_done")

        rows_in = nc.dram_tensor("rows_in", [(NE + 1) * REGION, ROW_W], F32, kind="Internal").ap()
        rows_out = nc.dram_tensor("rows_out", [2 * TOKENS, D], F32, kind="Internal").ap()
        rows_out_v = rows_out.rearrange("(k t p) d -> p k t d", p=P, k=2)
        GROUPS = TILES // GT
        R_LINKS = 15
        E_LINKS = 10
        B2_STEPS = 6

        BQ_W = sb("BQ_W", [D, D])
        BQ_B = sb("BQ_B", [1, D])
        BD_W = sb("BD_W", [D, LATENT])
        BD_B = sb("BD_B", [LATENT, 1])
        BU_W = sb("BU_W", [LATENT + 1, 2 * D])
        BO_W = sb("BO_W", [D, D])
        BO_B = sb("BO_B", [1, D])
        ROPE = sb("ROPE", [P, TPB, 2, HD])
        LT = sb("LT", [LATENT + 1, 2, P])
        QKR = in_keys[:, 0 * 4 * D:1 * 4 * D].rearrange("p (a b h d) -> p a b h d", a=2, b=2, h=H)
        VB = in_keys[:, 1 * 4 * D:2 * 4 * D].rearrange("p (a h d) -> p a h d", a=4, h=H)
        T1 = sb("T1", [P, 2, H, HD])
        T2 = sb("T2", [P, 2, H, HD])
        ROT = in_keys[:, 2 * 4 * D:3 * 4 * D].rearrange("p (a b h d) -> p a b h d", a=2, b=2, h=H)
        PROD = PT[:, :, :, :].rearrange("p a j (h g d) -> p a (j h) g d", g=H, d=HD)
        ATT = sb("ATT", [P, H, H])
        AMX = sb("AMX", [P, H])
        SH = in_keys[:, 3 * 4 * D:4 * 4 * D].rearrange("p (a h g) -> p a h g", a=2, h=H)
        EX = sb("EX", [P, 2, H, H])
        PROD2 = V32[:, 0:TPB, :, :].rearrange("p t h (a b) -> p (t h a b)", b=H).rearrange("p (h d g) -> p h d g", d=HD, g=H)
        ASUM = sb("ASUM", [P, H])
        ARS = sb("ARS", [P, H])
        AO = sb("AO", [P, H, HD])
        BWV = sb("BWV", [P, 2, D])
        BWVT = sb("BWVT", [D, 2, P])

        b_w_in = sem("b_w_in")
        b_const = sem("b_const")
        b_xs = sem("b_xs")
        b_xsT = sem("b_xsT")
        b_xst = sem("b_xst")
        b_ql = sem("b_ql")
        b_lat = sem("b_lat")
        b_kv = sem("b_kv")
        b_qk = sem("b_qk")
        b_v = sem("b_v")
        b_rope1 = sem("b_rope1")
        b_rot = sem("b_rot")
        b_prod = sem("b_prod")
        b_att = sem("b_att")
        b_max = sem("b_max")
        b_sh = sem("b_sh")
        b_ex = sem("b_ex")
        b_p2 = sem("b_p2")
        b_red2 = sem("b_red2")
        b_red2b = sem("b_red2b")
        b_rs = sem("b_rs")
        b_wv = sem("b_wv")
        b_wvT = sem("b_wvT")
        b_wvt = sem("b_wvt")
        b_o = sem("b_o")
        b_x = sem("b_x")
        banks = [ps(f"bank{i}", [P, SEQ]) for i in range(8)]
        psA, psB = banks[0:2], banks[2:4]
        psO = banks[4][:, :].rearrange("p (q t) -> p q t", q=G4)
        psM = banks[5]
        psT, psK = (b[:, :].bitcast(BF16).rearrange("p (g t) -> p g t", g=PAIRS) for b in banks[6:8])
        psG = banks[7]
        psXI, psH, psY = banks[0:2], banks[2:4], banks[4:6]
        psP, psF = banks[0:2], banks[2:4]

        x_in = [sem(f"x_in{b}") for b in range(BATCH)]
        w_in = sem("w_in")
        const_a = sem("const_a")
        const_ready = sem("const_ready")
        stats_done = sem("stats_done")
        mv_done = sem("mv_done")
        rstd_step = sem("rstd_step")
        rstd_done = sem("rstd_done")
        xn_done = sem("xn_done")
        xT_done = sem("xT_done")
        xT_copied = sem("xT_copied")
        qkv_done = sem("qkv_done")
        qk_copied = sem("qk_copied")
        v_copied = sem("v_copied")
        hi_done = sem("hi_done")
        mid_done = sem("mid_done")
        r1_done = sem("r1_done")
        parts_done = sem("parts_done")
        qT_done = sem("qT_done")
        kT_done = sem("kT_done")
        q2T_done = sem("q2T_done")
        qT_copied = sem("qT_copied")
        kT_copied = sem("kT_copied")
        q2T_copied = sem("q2T_copied")
        scoresA_done = sem("scoresA_done")
        max_done = sem("max_done")
        m_hi_done = sem("m_hi_done")
        m_done = sem("m_done")
        scoresB_done = sem("scoresB_done")
        exp_done = sem("exp_done")
        pv_done = sem("pv_done")
        o_copied = sem("o_copied")
        oT_done = sem("oT_done")
        rs_done = sem("rs_done")
        wv_done = sem("wv_done")
        wvT_done = sem("wvT_done")
        wvT_copied = sem("wvT_copied")
        wo_done = sem("wo_done")
        x1_done = sem("x1_done")
        out_sent = sem("out_sent")
        const_v = sem("const_v")

        h_v = h.rearrange("b (t p) d -> p (b t) d", p=P)
        out_v = out.rearrange("b (t p) d -> p (b t) d", p=P)

        block = ctx.enter_context(nc.Block())

        def wait(eng, semaphore, n):
            if not isinstance(n, int) or n > 0:
                eng.wait_ge(semaphore, n)

        def exists(T):
            return not isinstance(T, int) or 0 <= T < TILES

        def routed(n):
            return not isinstance(n, int) or 0 <= n < TILES // GT

        def over_tiles(eng, slot):
            for T in range(-2, RING):
                slot(T, T % RING, T // GT - 1)
            with eng.Fori(1, TILES // RING - 1) as i:
                for r in range(RING):
                    slot(RING * i + r, r, RING // GT * i + (r // GT - 1))
            for T in range(TILES - RING, TILES + 3):
                slot(T, T % RING, T // GT - 1)


        def ffn_consts_pool(pool):
            pool.memset(UT[:, :], 1.0).then_inc(f_const, 1)
            pool.memset(ONESB[:, :], 1.0).then_inc(f_const, 1)
            pool.memset(ONES_E[:, :], 1.0).then_inc(f_const, 1)
            pool.memset(ONER[:, :], 1.0).then_inc(f_const, 1)
            pool.memset(PAD[:, :], 0.0).then_inc(f_const, 1)
            pool.iota(IOTA_E[:, :], pattern=[[1, NE]], base=0, channel_multiplier=0,
                      allow_small_or_imprecise_dtypes=True).then_inc(f_const, 1)
            pool.iota(IOTA_J[:, :], pattern=[[0, 1]], base=0, channel_multiplier=1,
                      allow_small_or_imprecise_dtypes=True).then_inc(f_const, 1)
            pool.iota(RUN0[:, :], pattern=[[REGION, NE]], base=0, channel_multiplier=0,
                      allow_small_or_imprecise_dtypes=True).then_inc(f_const, 1)
            pool.iota(DEST[:, :, :], pattern=[[P, TILES], [TOKENS, 2]], base=0, channel_multiplier=1).then_inc(f_const, 1)
            pool.memset(OVER_D[:, :], 1.0 / D).then_inc(f_const, 1)
            pool.memset(EPS4[:, :], EPS).then_inc(f_const, 1)
            pool.wait_ge(f_const, 11)
            pool.affine_select(out=UT[:, :], in_=UT[:, :], compare_op=ALU.is_gt, fill=0.0, base=0,
                               pattern=[[1, P]], channel_multiplier=-1).then_inc(f_const, 1)
            pool.iota(PAD_I[:, D + 1:D + 2], pattern=[[0, 1]], base=NOWHERE, channel_multiplier=0).then_inc(f_const, 1)

        def ffn_consts_sp(sp):
            sp.dma_start(GW[:, :], gate_w).then_inc(f_w_in, 16)
            sp.dma_start(GB[:, :], gate_b.broadcast_to([P, NE])).then_inc(f_w_in, 16)
            sp.wait_ge(f_const, 13)
            sp.dma_start(rows_in[DUMMY:DUMMY + P, :], PAD[:, :]).then_inc(f_dummy, 16)

        def split_b2(pool, c):
            done = [B2_STEPS * c]

            def step(rows, out_, a, b, op):
                wait(pool, b2_split, done[0])
                pool.tensor_tensor(out_[rows, :], a[rows, :], b[rows, :], op).then_inc(b2_split, 1)
                done[0] += 1

            part = B2P[:, c * B2_EXPERTS * D:(c + 1) * B2_EXPERTS * D]
            every, second, third = slice(0, 96), slice(32, 64), slice(64, 96)
            one = ONE[0:96, :].broadcast_to([96, B2_EXPERTS * D])
            pool.wait_ge(b2_in, 16 * (c + 1))
            step(every, part, B2F, one, ALU.mult)
            step(every, B2F, B2F, part, ALU.subtract)
            step(second, part, B2F, one, ALU.mult)
            step(third, part, B2F, one, ALU.mult)
            step(third, B2F, B2F, part, ALU.subtract)
            step(third, part, B2F, one, ALU.mult)
            pool.wait_ge(b2_split, done[0])

        def statistics(dve, n):
            with dve.Fori(0, TILES) as T:
                dve.bn_stats(STAT[:, bass.ds(T, 1), :].rearrange("p a d -> p (a d)"),
                             X[:, bass.ds(T, 1), :].rearrange("p a d -> p (a d)")).then_inc(f_stat, 1)
            dve.wait_ge(f_stat, TILES * (n + 1))
            dve.tensor_tensor(MEAN[:, :], STAT[:, :, 1], STAT[:, :, 4], ALU.add).then_inc(f_stat1, 1)
            dve.tensor_tensor(DIFF[:, :], STAT[:, :, 1], STAT[:, :, 4], ALU.subtract).then_inc(f_stat1, 1)
            dve.wait_ge(f_stat1, 4 * n + 2)
            dve.tensor_scalar(MEAN[:, :], MEAN[:, :], 0.5, None, ALU.mult).then_inc(f_stat2, 1)
            dve.tensor_tensor(VAR[:, :], STAT[:, :, 2], STAT[:, :, 5], ALU.add).then_inc(f_stat1, 1)
            dve.tensor_tensor(DIFF[:, :], DIFF[:, :], DIFF[:, :], ALU.mult).then_inc(f_stat1, 1)
            dve.wait_ge(f_stat1, 4 * n + 4)
            dve.scalar_tensor_tensor(VAR[:, :], DIFF[:, :], D / 4.0, VAR[:, :], ALU.mult, ALU.add).then_inc(f_var, 1)
            dve.wait_ge(f_stat2, n + 1)
            dve.wait_ge(f_rstd, n + 1)

        def deviations(pool, n):
            pool.wait_ge(f_var, n + 1)
            pool.tensor_scalar(RSD[:, :], VAR[:, :], 1.0 / D, EPS, ALU.mult, ALU.add).then_inc(f_eps, 1)
            pool.wait_ge(f_eps, n + 1)
            pool.tensor_tensor(RSD[:, :], RSD[:, :], NHALF[:, :], ALU.pow).then_inc(f_rstd, 1)


        def tiles_at(x, T, count=1):
            return x[:, bass.ds(T, count), :]

        def row_at(x, T):
            return x[:, bass.ds(T, 1), :].rearrange("p a d -> p (a d)")

        def route_stats(dve, n, T0, x_done):
            dve.wait_ge(x_done, T0 + GT)
            wait(dve, r_var, n)
            for t in range(GT):
                i = dve.bn_stats(STG[:, t, :], row_at(X, T0 + t))
            i.then_inc(r_stat, 1)
            dve.wait_ge(r_stat, n + 1)
            wait(dve, r_eps, n)
            wait(dve, r_xg, n)
            dve.tensor_tensor(MEG[:, :], STG[:, :, 1], STG[:, :, 4], ALU.add)
            dve.tensor_tensor(VAG[:, :], STG[:, :, 2], STG[:, :, 5], ALU.add)
            dve.tensor_tensor(DIG[:, :], STG[:, :, 1], STG[:, :, 4], ALU.subtract).then_inc(r_s1, 1)
            dve.wait_ge(r_s1, n + 1)
            dve.tensor_scalar(MEG[:, :], MEG[:, :], 0.5, None, ALU.mult)
            dve.tensor_tensor(DIG[:, :], DIG[:, :], DIG[:, :], ALU.mult).then_inc(r_s2, 1)
            dve.wait_ge(r_s2, n + 1)
            dve.scalar_tensor_tensor(VAG[:, :], DIG[:, :], D / 4.0, VAG[:, :], ALU.mult, ALU.add).then_inc(r_var, 1)

        def route_deviation(pool, n):
            pool.wait_ge(r_var, n + 1)
            pool.tensor_tensor(RSG[:, :], VAG[:, :], OVER_D[:, :], ALU.mult).then_inc(r_eps0, 1)
            pool.wait_ge(r_eps0, n + 1)
            pool.tensor_tensor(RSG[:, :], RSG[:, :], EPS4[:, :], ALU.add).then_inc(r_eps, 1)
            pool.wait_ge(r_eps, n + 1)
            pool.tensor_tensor(RSG[:, :], RSG[:, :], NHALF[:, 0:GT], ALU.pow).then_inc(r_rstd, 1)

        def route_normalize(dve, n, T0):
            dve.wait_ge(r_rstd, n + 1)
            wait(dve, r_scat, 16 * 2 * GT * n)
            for t in range(GT):
                dve.tensor_scalar(XG[:, t, 0, 0:D], row_at(X, T0 + t), MEG[:, t:t + 1], RSG[:, t:t + 1],
                                  ALU.subtract, ALU.mult)
            dve.tensor_copy(XG_I[:, :, :, D + 1], tiles_at(DEST, T0, GT)).then_inc(r_xg, 1)

        def route_transpose(pe, n, keys_copied=None, bank_keys=0):
            pe.wait_ge(r_xg, n + 1)
            wait(pe, r_pos, n)
            wait(pe, keys_copied, bank_keys)
            for t in range(GT):
                mm = pe.transpose(psG[:, t * P:(t + 1) * P], XG[:, t, 0, 0:D], IDF[:, :])
            mm.then_inc(r_xT, 1)

        def route_copy(act, n):
            act.wait_ge(r_xT, n + 1)
            act.activation(XGT[:, :, :], psG[:, :].rearrange("p (t c) -> p t c", t=GT), ACT.Copy).then_inc(r_xTc, 1)

        def route_second(act, n):
            act.wait_ge(r_xg, n + 1)
            act.activation(XG[:, :, 1, 0:D], XG[:, :, 0, 0:D], ACT.Copy).then_inc(r_xg2, 1)

        def route_logits(pe, n):
            pe.wait_ge(r_xTc, n + 1)
            for t in range(GT):
                mm = pe.matmul(psG[:, t * NE:(t + 1) * NE], XGT[:, t, :], GW[:, :], start=True, stop=True)
            mm.then_inc(r_lg, 1)

        def linker(dve, done, base):
            count = [0]

            def link(ins):
                count[0] += 1
                ins.then_inc(done, 1)
                dve.wait_ge(done, base + count[0])
            return link

        def over_e(x):
            return x.unsqueeze(2).broadcast_to([P, GT, NE])

        def over_t(x):
            return x.unsqueeze(1).broadcast_to([P, GT, NE])

        def route_top(dve, n, i):
            k = 0 if i < 7 else 1
            wait(dve, r_link, R_LINKS * n + i)
            if i == 0:
                dve.wait_ge(r_lg, n + 1)
                a = dve.tensor_tensor(LG[:, :, :], psG[:, 0:GT * NE].rearrange("p (t e) -> p t e", e=NE), over_t(GB[:, :]), ALU.add)
            if i in (1, 7):
                a = dve.tensor_reduce(TOP[:, k, :], LG[:, :, :], AX.X, ALU.max)
            if i in (2, 8):
                a = dve.tensor_tensor(CAND[:, :, :], LG[:, :, :], over_e(TOP[:, k, :]), ALU.is_lt)
            if i in (3, 9):
                a = dve.scalar_tensor_tensor(CAND[:, :, :], CAND[:, :, :], float(NE), over_t(IOTA_E[:, :]), ALU.mult, ALU.add)
            if i in (4, 10):
                a = dve.tensor_reduce(IDX[:, :], CAND[:, :, :], AX.X, ALU.min)
            if i in (5, 11):
                a = dve.tensor_tensor(O1H[k][:, :, :], over_t(IOTA_E[:, :]), over_e(IDX[:, :]), ALU.is_equal)
            if i == 6:
                a = dve.scalar_tensor_tensor(LG[:, :, :], O1H[0][:, :, :], NEG, LG[:, :, :], ALU.mult, ALU.add)
            a.then_inc(r_link, 1)
            if i == 8:
                dve.tensor_tensor(TDIF[:, :], TOP[:, 1, :], TOP[:, 0, :], ALU.subtract).then_inc(r_top, 1)
            if i == 11:
                dve.wait_ge(r_link, R_LINKS * n + 12)
                dve.tensor_tensor(MSK[:, :, :], O1H[0][:, :, :], O1H[1][:, :, :], ALU.add).then_inc(r_mask, 1)

        def route_exp(act, n):
            act.wait_ge(r_top, n + 1)
            act.activation(EXPD[:, :], TDIF[:, :], ACT.Exp).then_inc(r_exp, 1)

        def route_ranks(pe, n):
            pe.wait_ge(r_mask, n + 1)
            for t in range(GT + 1):
                out_ = psG[:, (GT + t) * NE:(GT + t + 1) * NE]
                for b in range(t):
                    mm = pe.matmul(out_, ONESB[:, :], MSK[:, b, :], start=(b == 0), stop=(t == GT and b == t - 1))
                if t < GT:
                    mm = pe.matmul(out_, UT[:, :], MSK[:, t, :], start=(t == 0), stop=True)
            mm.then_inc(r_rank, 1)

        def route_rows(dve, n, i):
            wait(dve, r_link, R_LINKS * n + 12 + min(i, 3))
            if i == 0:
                dve.wait_ge(r_rank, n + 1)
                ranks = psG[:, GT * NE:2 * GT * NE].rearrange("p (t e) -> p t e", e=NE)
                dve.tensor_tensor(CAND[:, :, :], ranks, over_t(RUN[:, :]), ALU.add).then_inc(r_link, 1)
                dve.wait_ge(r_exp, n + 1)
                dve.tensor_scalar(EXP1[:, :], EXPD[:, :], 1.0, None, ALU.add).then_inc(r_g1, 1)
            if i == 1:
                dve.tensor_tensor(RUN[:, :], RUN[:, :], psG[:, 2 * GT * NE:(2 * GT + 1) * NE], ALU.add)
                for k in range(2):
                    c = dve.tensor_tensor(O1H[k][:, :, :], O1H[k][:, :, :], CAND[:, :, :], ALU.mult)
                c.then_inc(r_link, 1)
                dve.wait_ge(r_g1, n + 1)
                dve.reciprocal(XG[:, :, 0, D], EXP1[:, :]).then_inc(r_g2, 1)
            if i == 2:
                for k in range(2):
                    c = dve.tensor_reduce(POSF[:, :, k], O1H[k][:, :, :], AX.X, ALU.add)
                c.then_inc(r_link, 1)
                dve.wait_ge(r_g2, n + 1)
                dve.tensor_tensor(XG[:, :, 1, D], EXPD[:, :], XG[:, :, 0, D], ALU.mult).then_inc(r_gate, 1)
            if i == 3:
                dve.tensor_copy(POS[:, :, :], POSF[:, :, :]).then_inc(r_pos, 1)

        def route_send(pool, n, T0):
            pool.wait_ge(r_gate, n + 1)
            pool.wait_ge(r_pos, n + 1)
            pool.wait_ge(r_xg2, n + 1)
            pool.tensor_tensor(tiles_at(X, T0, GT), tiles_at(X, T0, GT), XG[:, :, 0, 0:D], ALU.add).then_inc(r_xadd, 1)
            for t in range(GT):
                for k in range(2):
                    pool.indirect_dma_start(out=rows_in, out_offset=bass.IndirectOffsetOnAxis(ap=POS[:, t, k:k + 1], axis=0),
                                            in_=XG[:, t, k, :], in_offset=None).then_inc(r_scat, 16)


        def expert_tables(dve, ph):
            link = linker(dve, e_link, E_LINKS * ph)
            dve.wait_ge(r_link, R_LINKS * GROUPS * (ph + 1))
            rows = slice(0, ROW_TILES)
            link(dve.tensor_tensor(CE[:, :], RUN[rows, :], RUN0[rows, :], ALU.subtract))
            dve.tensor_copy(PADR[:, :], RUN[0:1, :]).then_inc(e_pad, 1)
            link(dve.tensor_scalar(TI[:, :], CE[:, :], float(P - 1), None, ALU.add))
            link(dve.tensor_scalar(TI[:, :], TI[:, :], 7, None, ALU.arith_shift_right))
            link(dve.tensor_copy(TF[:, :], TI[:, :]))
            link(dve.tensor_tensor_scan(TEND[:, :], ONES_E[:, :], TF[:, :], 0.0, ALU.mult, ALU.add))
            link(dve.tensor_scalar(CMP[:, :], TEND[:, :], IOTA_J[:, :], None, ALU.is_le))
            dve.tensor_scalar(TF[:, :], TF[:, :], -float(P), float(REGION), ALU.mult, ALU.add)
            link(dve.tensor_reduce(ERF[:, 0:1], CMP[:, :], AX.X, ALU.add))
            link(dve.tensor_tensor(CMP[:, :], CMP[:, :], TF[:, :], ALU.mult))
            link(dve.tensor_reduce(ERF[:, 1:2], CMP[:, :], AX.X, ALU.add))
            dve.scalar_tensor_tensor(ERF[:, 1:2], IOTA_J[:, :], float(P), ERF[:, 1:2], ALU.mult, ALU.add).then_inc(e_flat, 1)
            dve.wait_ge(e_turned, ph + 1)
            dve.tensor_scalar(EJ[:, :], psG[0:1, 0:ROW_TILES], float(NE - 1), None, ALU.min)
            dve.tensor_scalar(RJ[:, :], psG[0:1, P:P + ROW_TILES], float(DUMMY), None, ALU.min).then_inc(e_tables, 1)
            link(dve.tensor_copy(RUN[:, :], RUN0[:, :]))

        now = {}

        def numbers(eng, name, table, most):
            regs = [eng.alloc_register(f"{name}{u}") for u in range(STEP)]

            def read(j0):
                eng.load(regs, table[0:1, bass.ds(j0, STEP)])
                return [eng.snap(r, min_val=0, max_val=most) for r in regs]
            return read

        def over_rows(eng, body, head=None):
            rounds = ROW_TILES // STEP
            now.update(head(0) if head else {})
            for j in range(STEP):
                body(j, j, True)
            with eng.Fori(1, rounds - 1) as i:
                now.update(head(STEP * i) if head else {})
                for u in range(STEP):
                    body(STEP * i + u, u, False)
            now.update(head(ROW_TILES - STEP) if head else {})
            for j in range(ROW_TILES - STEP, ROW_TILES):
                body(j, j % STEP, False)

        def per_buffer(ph, j, u, dmas):
            n = ph * (ROW_TILES // STEP) + 1
            if isinstance(j, int):
                return 16 * dmas * (n + j // STEP)
            return (j - u) * (16 * dmas // STEP) + 16 * dmas * n

        def sent_before(eng, ph, j, u, back):
            if not (isinstance(j, int) and j < back and ph == 0):
                v = (u - back) % STEP
                eng.wait_ge(f_ys[v], per_buffer(ph, j - back, v, 1))

        def pad_rows(eng, half):
            with eng.Fori(0, NE // 8) as i:
                for u in range(4):
                    r = eng.value_load(PADR[0:1, bass.ds(4 * i + (half * NE // 2 + u), 1)], min_val=0, max_val=DUMMY - P)
                    eng.dma_start(rows_in[bass.ds(r, P), :], PAD[:, :]).then_inc(e_padded, 16)

        def experts_sp(sp, ph):
            base = ph * ROW_TILES
            sp.wait_ge(e_pad, ph + 1)
            pad_rows(sp, 0)
            sp.wait_ge(e_tables, ph + 1)
            sp.wait_ge(f_dummy, 16)
            sp.wait_ge(e_padded, 16 * NE * (ph + 1))
            sp.wait_ge(r_scat, 16 * 2 * GT * GROUPS * (ph + 1))

            def load(j, u, first):
                sent_before(sp, ph, j, u, STEP)
                e, r = now["experts"][u], now["rows"][u]
                sp.dma_start(XI[:, u, :], rows_in[bass.ds(r, P), :]).then_inc(f_load[u], 16)
                sp.dma_start(W1[:, u, :], w1[bass.ds(e, 1), :, :].rearrange("a p n -> (a p) n")).then_inc(f_load[u], 16)

            experts, rows = numbers(sp, f"sp_expert{ph}_", EJ, NE - 1), numbers(sp, f"sp_row{ph}_", RJ, DUMMY)
            over_rows(sp, load, lambda j: {"experts": experts(j), "rows": rows(j)})
            for i in range(STEP):
                sp.wait_ge(f_ys[i], 16 * (ROW_TILES // STEP) * (ph + 1))
            for g in range(GROUPS):
                n = ph * GROUPS + g
                if n >= 2:
                    sp.wait_ge(f_done, n - 1)
                for k in range(2):
                    sp.dma_start(YC[:, g % 2, k, :, :], rows_out_v[:, k, g * GT:(g + 1) * GT, :]).then_inc(f_yc[g % 2], 16)

        def experts_pool(pool, ph):
            base = ph * ROW_TILES

            def body(j, u, first):
                pool.wait_ge(f_y, base + j + 1)
                wait(pool, e_settled, base + j)
                pool.tensor_tensor(SETTLE[:, :], ONE[:, :], ONE[:, :], ALU.mult).then_inc(e_settled, 1)
                pool.indirect_dma_start(out=rows_out, out_offset=bass.IndirectOffsetOnAxis(ap=XI_I[:, u, D + 1:D + 2], axis=0),
                                        in_=Y[:, u % 4, :], in_offset=None, bounds_check=2 * TOKENS - 1,
                                        oob_is_err=False).then_inc(f_ys[u], 16)

            over_rows(pool, body)

        def experts_act(act, ph):
            base = ph * ROW_TILES

            act.wait_ge(e_pad, ph + 1)
            pad_rows(act, 1)
            act.wait_ge(e_tables, ph + 1)
            act.wait_ge(w2_in, 16 * (NE // B2_EXPERTS + 1))

            def gelu(j, u, first):
                e = now["experts"][u]
                act.wait_ge(f_up, base + j + 1)
                for c in range(FC):
                    a = act.activation(HT[:, u % 2, c, :], psH[u % 2][:, c * P:(c + 1) * P], ACT.Gelu,
                                       bias=B1[:, bass.ds(e * FC + c, 1)])
                a.then_inc(f_gelu, 1)

            experts = numbers(act, f"act_expert{ph}_", EJ, NE - 1)
            over_rows(act, gelu, lambda j: {"experts": experts(j)})

        def experts_pe(pe, ph):
            base = ph * ROW_TILES

            def turn(j, u, first):
                pe.wait_ge(f_load[u], per_buffer(ph, j, u, 2))
                pe.transpose(psXI[u % 2][:, 0:P], XI[:, u, 0:D], IDF[:, :]).then_inc(f_xiT, 1)

            def up(j, u, first):
                pe.wait_ge(f_xit, base + j + 1)
                for c in range(FC):
                    mm = pe.matmul(psH[u % 2][:, c * P:(c + 1) * P], W1[:, u, c * P:(c + 1) * P], XIT[:, u % 2, :],
                                   start=True, stop=True)
                mm.then_inc(f_up, 1)

            def down(j, u, first):
                e = now["experts"][u]
                if isinstance(j, int) and j + 1 >= ROW_TILES:
                    pe.wait_ge(f_y, base + j - 1)
                pe.wait_ge(f_gelu, base + j + 1)
                for c in range(FC):
                    pe.matmul(psY[u % 2][:, 0:D], HT[:, u % 2, c, :],
                              W2[:, bass.ds(e, 1), c * D:(c + 1) * D].rearrange("p a d -> p (a d)"),
                              start=(c == 0), stop=False)
                pe.matmul(psY[u % 2][:, 0:D], SEL3[:, :], B2P[:, bass.ds(e * D, D)], start=False, stop=True).then_inc(f_down, 1)

            def body(j, u, first):
                if not (isinstance(j, int) and j + 1 >= ROW_TILES):
                    up(j + 1, (u + 1) % STEP, first and u < STEP - 1)
                if not (isinstance(j, int) and j + 2 >= ROW_TILES):
                    turn(j + 2, (u + 2) % STEP, first and u < STEP - 2)
                down(j, u, first)

            pe.wait_ge(e_flat, ph + 1)
            for i in range(2):
                mm = pe.matmul(psG[0:1, i * P:i * P + ROW_TILES], ERF[:, i:i + 1], IDF[0:ROW_TILES, 0:ROW_TILES],
                               start=True, stop=True)
            mm.then_inc(e_turned, 1)
            pe.wait_ge(e_tables, ph + 1)
            pe.wait_ge(w2_in, 16 * (NE // B2_EXPERTS + 1))
            pe.wait_ge(b2_split, B2_STEPS * (NE // B2_EXPERTS))
            turn(0, 0, True)
            turn(1, 1, True)
            up(0, 0, True)
            experts = numbers(pe, f"pe_expert{ph}_", EJ, NE - 1)
            over_rows(pe, body, lambda j: {"experts": experts(j)})

        def experts_dve(dve, ph):
            base = ph * ROW_TILES

            def xi_copy(j, u, first):
                dve.wait_ge(f_xiT, base + j + 1)
                dve.tensor_copy(XIT[:, u % 2, :], psXI[u % 2][:, 0:P]).then_inc(f_xit, 1)

            def gated(j, u, first):
                dve.wait_ge(f_down, base + j + 1)
                sent_before(dve, ph, j, u, 4)
                dve.tensor_scalar(Y[:, u % 4, :], psY[u % 2][:, 0:D], XI[:, u, D:D + 1], None, ALU.mult).then_inc(f_y, 1)

            def body(j, u, first):
                if not (isinstance(j, int) and j + 2 >= ROW_TILES):
                    xi_copy(j + 2, (u + 2) % STEP, first and u < STEP - 2)
                gated(j, u, first)

            xi_copy(0, 0, True)
            xi_copy(1, 1, True)
            over_rows(dve, body)
            dve.wait_ge(r_xadd, GROUPS * (ph + 1))
            for g in range(GROUPS):
                n = ph * GROUPS + g
                dve.wait_ge(f_yc[g % 2], 32 * (ph * GROUPS // 2 + g // 2 + 1))
                x = X[:, g * GT:(g + 1) * GT, :]
                dve.tensor_tensor(YC[:, g % 2, 0], YC[:, g % 2, 0], YC[:, g % 2, 1], ALU.add).then_inc(f_ysum, 1)
                dve.wait_ge(f_ysum, n + 1)
                dve.tensor_tensor(x, x, YC[:, g % 2, 0], ALU.add).then_inc(f_done, 1)
            dve.wait_ge(f_done, GROUPS * (ph + 1))

        def over_fours(eng, slot):
            for T in range(-2, TPB):
                slot(T, T % TPB, T // TPB - 1)
            with eng.Fori(1, TILES // TPB - 1) as i:
                for s in range(TPB):
                    slot(TPB * i + s, s, i - 1)
            for T in range(TILES - TPB, TILES + 3):
                slot(T, T % TPB, T // TPB - 1)

        def attb_load(sp):
            for dst, src in ((BQ_W[:, :], Wq), (BQ_B[:, :], bq), (BD_W[:, :], Wdown), (BD_B[:, :], bdown),
                             (BU_W[0:LATENT, :], Wup), (BU_W[LATENT:LATENT + 1, :], bup), (BO_W[:, :], Wout),
                             (BO_B[:, :], bout), (ROPE[:, :, :, :], rope)):
                sp.dma_start(dst, src).then_inc(b_w_in, 16)

        def attb_pool(pool):
            def rotate(T, s):
                par = s % 2
                x, r = QKR[:, par], ROT[:, par]
                half = HD // 2

                def table(i, a, b):
                    return ROPE[:, s, i, a:b].unsqueeze(1).unsqueeze(1).broadcast_to([P, 2, H, b - a])

                pool.wait_ge(b_qk, 2 * (T + 1))
                wait(pool, b_rot, T)
                wait(pool, b_prod, T - 1)
                pool.tensor_tensor(T1[:, :, :, :], x, table(0, 0, HD), ALU.mult).then_inc(b_rope1, 1)
                pool.tensor_tensor(T2[:, :, :, 0:half], x[:, :, :, half:HD], table(1, 0, half), ALU.mult).then_inc(b_rope1, 1)
                pool.tensor_tensor(T2[:, :, :, half:HD], x[:, :, :, 0:half], table(1, half, HD), ALU.mult).then_inc(b_rope1, 1)
                pool.wait_ge(b_rope1, 3 * (T + 1))
                pool.tensor_tensor(r, T1[:, :, :, :], T2[:, :, :, :], ALU.add).then_inc(b_rot, 1)

            def products(T, s):
                par = s % 2
                pool.wait_ge(b_rot, T + 1)
                wait(pool, b_att, T - 1)
                pool.tensor_tensor(PROD[:, par], ROT[:, par, 0].unsqueeze(2).broadcast_to([P, H, H, HD]),
                                   ROT[:, par, 1].unsqueeze(1).broadcast_to([P, H, H, HD]), ALU.mult).then_inc(b_prod, 1)

            def slot(T, s, g):
                if exists(T + 1):
                    rotate(T + 1, (s + 1) % TPB)
                    products(T + 1, (s + 1) % TPB)
                if routed(g) and s == 1:
                    route_deviation(pool, GROUPS + g)
                if routed(g) and s == 2:
                    route_send(pool, GROUPS + g, GT * g)

            over_fours(pool, slot)

        def attb_pe(pe):
            def project(T, s):
                par = s % 2
                ps_ = psP[par]
                pe.wait_ge(b_xs, T + 1)
                wait(pe, b_v, T - 1)
                pe.transpose(ps_[:, 0:P], XS[:, par, :], IDF[:, :]).then_inc(b_xsT, 1)
                pe.wait_ge(b_xst, T + 1)
                pe.matmul(ps_[:, 0:D], XST[:, par, :], BQ_W[:, :], start=True, stop=False)
                pe.matmul(ps_[:, 0:D], ONER[:, :], BQ_B[:, :], start=False, stop=True)
                pe.matmul(ps_[0:LATENT, D:D + P], BD_W[:, :], XST[:, par, :], start=True, stop=True).then_inc(b_ql, 1)
                pe.wait_ge(b_lat, T + 1)
                pe.matmul(ps_[:, 2 * D:4 * D], LT[:, par, :], BU_W[:, :], start=True, stop=True).then_inc(b_kv, 1)

            def finish(T, s):
                par = s % 2
                pe.wait_ge(b_wv, T + 1)
                wait(pe, b_x, T - 1)
                pe.transpose(psF[par][:, 0:P], BWV[:, par, :], IDF[:, :]).then_inc(b_wvT, 1)
                pe.wait_ge(b_wvt, T + 1)
                pe.matmul(psF[par][:, 0:D], BWVT[:, par, :], BO_W[:, :], start=True, stop=False)
                pe.matmul(psF[par][:, 0:D], ONER[:, :], BO_B[:, :], start=False, stop=True).then_inc(b_o, 1)

            def slot(T, s, g):
                if exists(T + 2):
                    project(T + 2, (s + 2) % TPB)
                if routed(g) and s == 2:
                    route_logits(pe, GROUPS + g)
                if exists(T - 1):
                    finish(T - 1, (s - 1) % TPB)
                if routed(g) and s == 1:
                    route_transpose(pe, GROUPS + g)
                if routed(g) and s == 2:
                    route_ranks(pe, GROUPS + g)

            over_fours(pe, slot)

        def attb_act(act):
            def copies(T, s):
                par = s % 2
                ps_ = psP[par]
                act.wait_ge(b_xsT, T + 1)
                act.activation(XST[:, par, :], ps_[:, 0:P], ACT.Copy).then_inc(b_xst, 1)
                act.wait_ge(b_ql, T + 1)
                act.activation(LT[0:LATENT, par, :], ps_[0:LATENT, D:D + P], ACT.Identity, bias=BD_B[:, :]).then_inc(b_lat, 1)
                act.wait_ge(b_kv, T + 1)
                kv = ps_[:, 2 * D:4 * D].rearrange("p (h c) -> p h c", h=H)
                wait(act, b_rot, T - 1)
                act.activation(QKR[:, par, 0], ps_[:, 0:D].rearrange("p (h c) -> p h c", h=H), ACT.Copy).then_inc(b_qk, 1)
                act.activation(QKR[:, par, 1], kv[:, :, 0:HD], ACT.Copy).then_inc(b_qk, 1)
                wait(act, b_p2, T - 3)
                act.activation(VB[:, s % 4], kv[:, :, HD:2 * HD], ACT.Copy).then_inc(b_v, 1)

            def slot(T, s, g):
                if exists(T):
                    act.wait_ge(b_sh, T + 1)
                    wait(act, b_red2, T - 1)
                    act.activation(EX[:, s % 2], SH[:, s % 2], ACT.Exp, scale=float(HD) ** -0.5).then_inc(b_ex, 1)
                if exists(T + 2):
                    copies(T + 2, (s + 2) % TPB)
                if exists(T - 1):
                    act.wait_ge(b_wvT, T)
                    act.activation(BWVT[:, (s - 1) % 2, :], psF[(s - 1) % 2][:, 0:P], ACT.Copy).then_inc(b_wvt, 1)
                if routed(g) and s == 1:
                    route_copy(act, GROUPS + g)
                    route_second(act, GROUPS + g)
                if routed(g) and s == 2:
                    route_exp(act, GROUPS + g)

            over_fours(act, slot)

        def attb_dve(dve):
            def tile_at(x, T):
                return x[:, bass.ds(T, 1), :].rearrange("p a d -> p (a d)")

            def normalize(T, s):
                wait(dve, b_xsT, T - 1)
                dve.tensor_scalar(XS[:, s % 2, :], tile_at(X, T), MEAN[:, bass.ds(T, 1)], RSD[:, bass.ds(T, 1)],
                                  ALU.subtract, ALU.mult).then_inc(b_xs, 1)

            def scores(T, s):
                dve.wait_ge(b_prod, T + 1)
                wait(dve, b_sh, T)
                dve.tensor_reduce(ATT[:, :, :], PROD[:, s % 2], AX.X, ALU.add).then_inc(b_att, 1)
                dve.wait_ge(b_att, T + 1)
                dve.tensor_reduce(AMX[:, :], ATT[:, :, :], AX.X, ALU.max).then_inc(b_max, 1)
                dve.wait_ge(b_max, T + 1)
                wait(dve, b_ex, T - 1)
                dve.tensor_tensor(SH[:, s % 2], ATT[:, :, :], AMX[:, :].unsqueeze(2).broadcast_to([P, H, H]),
                                  ALU.subtract).then_inc(b_sh, 1)

            def values(T, s):
                dve.wait_ge(b_ex, T + 1)
                wait(dve, b_wv, T)
                dve.tensor_tensor(PROD2[:, :, :, :], EX[:, s % 2].unsqueeze(2).broadcast_to([P, H, HD, H]),
                                  VB[:, s % 4].rearrange("p g d -> p d g").unsqueeze(1).broadcast_to([P, H, HD, H]),
                                  ALU.mult).then_inc(b_p2, 1)
                dve.tensor_reduce(ASUM[:, :], EX[:, s % 2], AX.X, ALU.add).then_inc(b_red2, 1)
                dve.wait_ge(b_p2, T + 1)
                dve.tensor_reduce(AO[:, :, :], PROD2[:, :, :, :], AX.X, ALU.add).then_inc(b_red2b, 1)
                dve.wait_ge(b_red2, T + 1)
                dve.reciprocal(ARS[:, :], ASUM[:, :]).then_inc(b_rs, 1)
                dve.wait_ge(b_rs, T + 1)
                dve.wait_ge(b_red2b, T + 1)
                wait(dve, b_wvT, T - 1)
                dve.tensor_tensor(BWV[:, s % 2, :].rearrange("p (h d) -> p h d", h=H), AO[:, :, :],
                                  ARS[:, :].unsqueeze(2).broadcast_to([P, H, HD]), ALU.mult).then_inc(b_wv, 1)

            def slot(T, s, g):
                if exists(T + 2):
                    normalize(T + 2, (s + 2) % TPB)
                if exists(T):
                    scores(T, s)
                if exists(T - 1):
                    values(T - 1, (s - 1) % TPB)
                if exists(T - 2):
                    dve.wait_ge(b_o, T - 1)
                    dve.tensor_tensor(tile_at(X, T - 2), tile_at(X, T - 2), psF[s % 2][:, 0:D], ALU.add).then_inc(b_x, 1)
                if routed(g) and s == 1:
                    route_stats(dve, GROUPS + g, GT * g, b_x)
                    route_normalize(dve, GROUPS + g, GT * g)
                if routed(g) and s == 2:
                    for i in range(12):
                        route_top(dve, GROUPS + g, i)
                    for i in range(4):
                        route_rows(dve, GROUPS + g, i)

            over_fours(dve, slot)
            dve.wait_ge(b_x, TILES)

        @block.sync
        def _(sp):
            for b in range(BATCH):
                sp.dma_start(X[:, b * TPB:(b + 1) * TPB, :], h_v[:, b * TPB:(b + 1) * TPB, :]).then_inc(x_in[b], 16)
            sp.dma_start(WQ[:, :], Wqvk).then_inc(w_in, 16)
            sp.dma_start(WO[:, :], Wo).then_inc(w_in, 16)
            ffn_consts_sp(sp)
            for a in range(0, NE, B2_EXPERTS):
                sp.dma_start(W2[:, a:a + B2_EXPERTS, :],
                             w2pack[a:a + B2_EXPERTS, :, :].rearrange("e p n -> p e n")).then_inc(w2_in, 16)
            sp.dma_start(B1[:, :], b1).then_inc(w2_in, 16)
            attb_load(sp)
            for c in range(NE // B2_EXPERTS):
                if c > 0:
                    sp.wait_ge(b2_split, B2_STEPS * c)
                sp.dma_start(B2F[:, :], b2[:, c * B2_EXPERTS * D:(c + 1) * B2_EXPERTS * D].broadcast_to(
                    [96, B2_EXPERTS * D])).then_inc(b2_in, 16)
            experts_sp(sp, 0)
            experts_sp(sp, 1)
            sp.wait_ge(f_done, 2 * GROUPS)
            sp.dma_start(out_v, X[:, :, :]).then_inc(out_sent, 16)
            sp.wait_ge(out_sent, 16)

        def split_parts(pool, T, par):
            q, k = (QK[:, i, :].rearrange("p (h d) -> p h d", h=H) for i in range(2))
            qs, ks = (m[:, :, 0:K48].rearrange("p h (c d) -> p h c d", c=SLOTS) for m in (QS[:, par], KS))
            rq, rk = (R1[:, i, :].rearrange("p (h d) -> p h d", h=H) for i in range(2))

            def spread(x, n):
                return x.unsqueeze(2).broadcast_to([P, H, n, HD])

            def ones(n):
                return ONE[:, :].unsqueeze(2).unsqueeze(3).broadcast_to([P, H, n, HD])

            wait(pool, q2T_done, T - 1)
            pool.tensor_tensor(QS[:, par, :, K48:K48 + 2], ZERO[:, :].rearrange("p (h c) -> p h c", h=H),
                               ZERO[:, :].rearrange("p (h c) -> p h c", h=H), ALU.mult).then_inc(hi_done, 1)
            pool.wait_ge(qk_copied, 2 * T + 2)
            wait(pool, kT_done, T)
            pool.tensor_tensor(qs[:, :, 0:3, :], spread(q, 3), ones(3), ALU.mult).then_inc(hi_done, 1)
            pool.tensor_tensor(ks[:, :, 2:5, :], spread(k, 3), ones(3), ALU.mult).then_inc(hi_done, 1)
            pool.wait_ge(hi_done, 3 * T + 3)
            pool.tensor_tensor(rq, q, qs[:, :, 2, :], ALU.subtract).then_inc(r1_done, 1)
            pool.tensor_tensor(rk, k, ks[:, :, 2, :], ALU.subtract).then_inc(r1_done, 1)
            pool.wait_ge(r1_done, 2 * T + 2)
            pool.tensor_tensor(qs[:, :, 3:6:2, :], spread(rq, 2), ones(2), ALU.mult).then_inc(mid_done, 1)
            pool.tensor_tensor(ks[:, :, 0:6:5, :], spread(rk, 2), ones(2), ALU.mult).then_inc(mid_done, 1)
            pool.wait_ge(mid_done, 2 * T + 2)
            pool.tensor_tensor(qs[:, :, 4, :], rq, qs[:, :, 5, :], ALU.subtract).then_inc(parts_done, 1)
            pool.tensor_tensor(ks[:, :, 1, :], rk, ks[:, :, 5, :], ALU.subtract).then_inc(parts_done, 1)

        @block.gpsimd
        def _(pool):
            pool.memset(NHALF[:, :], -0.5).then_inc(const_a, 1)
            pool.memset(ZERO[:, :], 0.0).then_inc(const_a, 1)
            pool.memset(ONE[:, :], 1.0).then_inc(const_a, 1)
            pool.memset(IDF[:, :], 0.0).then_inc(const_a, 1)
            pool.memset(IDB[:, :], 0.0).then_inc(const_a, 1)
            pool.memset(MASK[:, :], 0.0).then_inc(const_a, 1)
            pool.memset(MASKT[:, :], 0.0).then_inc(const_a, 1)
            pool.memset(QS[:, :, :, :], 0.0).then_inc(const_a, 1)
            pool.memset(KS[:, :, 0:K48 + 2], 1.0).then_inc(const_a, 1)
            pool.memset(KS[:, :, K48 + 2:HEADW], 0.0).then_inc(const_a, 1)
            pool.wait_ge(const_a, 10)
            for m in (IDF, IDB):
                pool.affine_select(out=m[:, :], in_=m[:, :], compare_op=ALU.not_equal, fill=1.0, base=0,
                                   pattern=[[-1, P]], channel_multiplier=1).then_inc(const_ready, 1)
            for m, sign in ((MASK, 1), (MASKT, -1)):
                pool.affine_select(out=m[:, :], in_=m[:, :], compare_op=ALU.is_ge, fill=NEG, base=0,
                                   pattern=[[-sign, P]], channel_multiplier=sign).then_inc(const_ready, 1)
            ffn_consts_pool(pool)
            deviations(pool, 0)

            def slot(T, r, n):
                if exists(T + 2):
                    split_parts(pool, T + 2, r % 2)
                if isinstance(T, int) and 2 <= T < 2 + NE // B2_EXPERTS:
                    split_b2(pool, T - 2)
                if routed(n) and r % GT == 0:
                    route_deviation(pool, n)
                if routed(n) and r % GT == 2:
                    route_send(pool, n, GT * n)

            over_tiles(pool, slot)
            experts_pool(pool, 0)
            deviations(pool, 1)
            attb_pool(pool)
            experts_pool(pool, 1)

        @block.tensor
        def _(pe):
            def x_transpose(T):
                pe.wait_ge(xn_done, T + 1)
                wait(pe, x1_done, T - 3)
                pe.transpose(psM[:, 0:P], XN[:, :], IDF[:, :]).then_inc(xT_done, 1)

            def project(T):
                pe.wait_ge(xT_copied, T + 1)
                pe.matmul(psM[:, 0:3 * D], XT[:, :], WQ[:, :], start=True, stop=True).then_inc(qkv_done, 1)

            def transposes(out_, src, done):
                for g in range(PAIRS):
                    mm = pe.transpose(out_[:, g, :], src[:, 2 * g:2 * g + 2, :], IDB[:, :])
                mm.then_inc(done, 1)

            def q_transposes(T, r):
                pe.wait_ge(parts_done, 2 * T + 2)
                wait(pe, q2T_copied, T - 1)
                transposes(psT, QS[:, r % 2], qT_done)

            def k_transposes(T):
                pe.wait_ge(parts_done, 2 * T + 2)
                wait(pe, kT_copied, T)
                transposes(psK, KS, kT_done)

            def q2_transposes(T, r):
                pe.wait_ge(m_done, T + 1)
                wait(pe, qT_copied, min(T + 2, TILES) if isinstance(T, int) else T + 2)
                transposes(psT, QS[:, r % 2], q2T_done)

            def scoresA(T, r, k):
                s, g, rows = r % TPB, k // 2, slice(HEADW * (k % 2), HEADW * (k % 2 + 1))
                if k == 0:
                    pe.wait_ge(kT_copied, T + 1)
                    pe.wait_ge(qT_copied, T + 1)
                wait(pe, max_done, H * T + k - 1)
                k0 = r - s
                for t in range(s + 1):
                    pe.matmul(psA[k % 2][:, t * P:(t + 1) * P], QT[rows, r % 2, g, :], KT[rows, k0 + t, g, :],
                              start=(t == 0), stop=False, skip_group_check=True)
                pe.matmul(psA[k % 2][:, s * P:(s + 1) * P], IDB[:, :], MASK[:, :], start=False, stop=True,
                          skip_group_check=True).then_inc(scoresA_done, 1)

            def scoresB(T, r, k):
                s, g, rows = r % TPB, k // 2, slice(HEADW * (k % 2), HEADW * (k % 2 + 1))
                if k == 0:
                    pe.wait_ge(q2T_copied, T + 1)
                wait(pe, exp_done, H * T + k - 1)
                for t in range(s + 1):
                    pe.matmul(psB[k % 2][:, t * P:(t + 1) * P], KT[rows, r - s + t, g, :], QT2[rows, r % 2, g, :],
                              start=(t == 0), stop=False, skip_group_check=True)
                pe.matmul(psB[k % 2][:, s * P:(s + 1) * P], IDB[:, :], MASKT[:, :], start=False, stop=True,
                          skip_group_check=True).then_inc(scoresB_done, 1)

            def pv(T, r, q):
                s = r % TPB
                pe.wait_ge(exp_done, H * T + 4 * q + 4)
                if q == 0:
                    pe.wait_ge(v_copied, T + 1)
                    wait(pe, o_copied, T)
                for t in range(s + 1):
                    for j in range(4):
                        mm = pe.matmul(psO[32 * j:32 * j + 32, q, :], V32[:, r - s + t, 4 * q + j, :],
                                       PT[:, q % 2, j, t * P:(t + 1) * P], start=(t == 0), stop=(t == s))
                mm.then_inc(pv_done, 1)

            def o_transposes(T):
                pe.wait_ge(o_copied, T + 1)
                pe.wait_ge(v_copied, min(T + 4, TILES) if isinstance(T, int) else T + 4)
                wait(pe, x1_done, T)
                for q in range(G4):
                    mm = pe.transpose(psM[:, q * P:(q + 1) * P], OS[:, q, :], IDF[:, :])
                mm.then_inc(oT_done, 1)

            def wv_transpose(T):
                pe.wait_ge(wv_done, T + 1)
                pe.transpose(psM[:, 0:P], WV[:, :], IDF[:, :]).then_inc(wvT_done, 1)

            def out_project(T):
                pe.wait_ge(wvT_copied, T + 1)
                pe.matmul(psM[:, 0:D], WVT[:, :], WO[:, :], start=True, stop=True).then_inc(wo_done, 1)

            def slot(T, r, n):
                before = (r - 1) % RING
                for k in range(H):
                    if exists(T + 2) and k == X_AT:
                        x_transpose(T + 2)
                    if exists(T) and k == MAX_AT:
                        q2_transposes(T, r)
                    if exists(T + 2) and k == QKV_AT:
                        project(T + 2)
                    if exists(T + 1):
                        scoresA(T + 1, (r + 1) % RING, k)
                    if k >= LAG and exists(T):
                        scoresB(T, r, k - LAG)
                    if k < LAG and exists(T - 1):
                        scoresB(T - 1, before, k + H - LAG)
                    for q in range(G4):
                        if k == (4 * q + PV_AFTER) % H:
                            if 4 * q + PV_AFTER < H and exists(T):
                                pv(T, r, q)
                            if 4 * q + PV_AFTER >= H and exists(T - 1):
                                pv(T - 1, before, q)
                    if exists(T - 1):
                        if k == O_AT:
                            o_transposes(T - 1)
                        if k == WV_AT:
                            wv_transpose(T - 1)
                        if k == OUT_AT:
                            out_project(T - 1)
                    if routed(n):
                        u = H * (r % GT) + k
                        if u == RT_AT:
                            route_transpose(pe, n, kT_copied, min(T + 2, TILES) if isinstance(T, int) else T + 2)
                        if u == RL_AT:
                            route_logits(pe, n)
                        if u == RANK_AT:
                            route_ranks(pe, n)
                    if exists(T + 2):
                        if k == QT_AT:
                            q_transposes(T + 2, (r + 2) % RING)
                        if k == KT_AT:
                            if r % GT in (1, 2) and routed(n):
                                pe.wait_ge(r_link, R_LINKS * n + (1 if r % GT == 1 else 14))
                            k_transposes(T + 2)

            pe.wait_ge(f_const, 13)
            pe.wait_ge(f_w_in, 32)
            pe.wait_ge(const_ready, 4)
            pe.wait_ge(w_in, 32)
            pe.wait_ge(const_v, 6)
            over_tiles(pe, slot)
            pe.wait_ge(x1_done, TILES)
            experts_pe(pe, 0)
            pe.wait_ge(b_w_in, 16 * 9)
            pe.wait_ge(f_y, ROW_TILES)
            attb_pe(pe)
            pe.wait_ge(b_x, TILES)
            experts_pe(pe, 1)

        @block.scalar
        def _(act):
            def xT_copy(T):
                act.wait_ge(xT_done, T + 1)
                act.activation(XT[:, :], psM[:, 0:P], ACT.Copy).then_inc(xT_copied, 1)

            def qkv_copy(T, r):
                act.wait_ge(qkv_done, T + 1)
                wait(act, parts_done, 2 * T)
                act.activation(QK[:, 0, :], psM[:, 0:D], ACT.Copy, scale=float(D) ** -0.5).then_inc(qk_copied, 1)
                act.activation(QK[:, 1, :], psM[:, 2 * D:3 * D], ACT.Copy).then_inc(qk_copied, 1)
                act.activation(V32[:, r, :, 0:HD], psM[:, D:2 * D].rearrange("p (h d) -> p h d", h=H),
                               ACT.Copy).then_inc(v_copied, 1)

            def qT_copy(T, r):
                act.wait_ge(qT_done, T + 1)
                act.activation(QT[:, r % 2, :, :], psT, ACT.Copy).then_inc(qT_copied, 1)

            def exps(T, r, k):
                n = (r % TPB + 1) * P
                q = k // 4
                if k % 4 == 0:
                    wait(act, pv_done, G4 * T + q - 1)
                act.wait_ge(scoresB_done, H * T + k + 1)
                act.activation(PT[:, q % 2, k % 4, 0:n], psB[k % 2][:, 0:n], ACT.Exp).then_inc(exp_done, 1)

            def o_copy(T):
                act.wait_ge(pv_done, G4 * (T + 1))
                wait(act, oT_done, T)
                act.activation(OS[:, :, :], psO[:, :, :], ACT.Copy).then_inc(o_copied, 1)

            def wvT_copy(T):
                act.wait_ge(wvT_done, T + 1)
                act.activation(WVT[:, :], psM[:, 0:P], ACT.Copy).then_inc(wvT_copied, 1)

            def slot(T, r, n):
                before = (r - 1) % RING
                for k in range(H):
                    if exists(T + 2) and k == X_AT:
                        xT_copy(T + 2)
                    if exists(T + 2) and k == QKV_AT:
                        qkv_copy(T + 2, (r + 2) % RING)
                    if k >= LAG and exists(T):
                        exps(T, r, k - LAG)
                    if k < LAG and exists(T - 1):
                        exps(T - 1, before, k + H - LAG)
                    if exists(T - 1):
                        if k == O_COPY_AT:
                            o_copy(T - 1)
                        if k == WV_AT:
                            wvT_copy(T - 1)
                    if exists(T + 2) and k == QT_AT:
                        qT_copy(T + 2, (r + 2) % RING)
                    if routed(n):
                        u = H * (r % GT) + k
                        if u == RT_AT:
                            route_copy(act, n)
                        if u == RL_AT:
                            route_second(act, n)
                        if u == RANK_AT - 1:
                            route_exp(act, n)

            over_tiles(act, slot)
            experts_act(act, 0)
            act.wait_ge(b_w_in, 16 * 9)
            attb_act(act)
            experts_act(act, 1)

        @block.vector
        def _(dve):
            def tile_of(x, T):
                return x[:, bass.ds(T, 1), :].rearrange("p a d -> p (a d)")

            def normalize(T):
                wait(dve, xT_done, T)
                dve.tensor_scalar(XN[:, :], tile_of(X, T), MEAN[:, bass.ds(T, 1)], RSD[:, bass.ds(T, 1)],
                                  ALU.subtract, ALU.mult).then_inc(xn_done, 1)

            def kT_copy(T, r):
                dve.wait_ge(kT_done, T + 1)
                dve.tensor_copy(KT[:, r, :, :], psK).then_inc(kT_copied, 1)

            def q2T_copy(T, r):
                dve.wait_ge(q2T_done, T + 1)
                dve.tensor_copy(QT2[:, r % 2, :, :], psT).then_inc(q2T_copied, 1)

            def maxes(T, r, k):
                n = (r % TPB + 1) * P
                dve.wait_ge(scoresA_done, H * T + k + 1)
                dve.tensor_reduce(NM[:, r % 2, k:k + 1], psA[k % 2][:, 0:n], AX.X, ALU.max,
                                  negate=True).then_inc(max_done, 1)

            def m_parts(T, r):
                dve.wait_ge(max_done, H * (T + 1))
                dve.wait_ge(qT_done, T + 1)
                dve.tensor_copy(QS[:, r % 2, :, K48], NM[:, r % 2, :]).then_inc(m_hi_done, 1)
                dve.wait_ge(m_hi_done, T + 1)
                dve.tensor_tensor(QS[:, r % 2, :, K48 + 1], NM[:, r % 2, :], QS[:, r % 2, :, K48],
                                  ALU.subtract).then_inc(m_done, 1)

            def weigh(T):
                o = psM[:, :].rearrange("p (h d) -> p h d", h=H)
                dve.wait_ge(oT_done, T + 1)
                dve.reciprocal(RS[:, :], o[:, :, HD]).then_inc(rs_done, 1)
                dve.wait_ge(rs_done, T + 1)
                wait(dve, wvT_done, T)
                dve.tensor_tensor(WV[:, :].rearrange("p (h d) -> p h d", h=H), o[:, :, 0:HD],
                                  RS[:, :].unsqueeze(2).broadcast_to([P, H, HD]), ALU.mult).then_inc(wv_done, 1)

            def add_attention(T):
                dve.wait_ge(wo_done, T + 1)
                dve.tensor_tensor(tile_of(X, T), tile_of(X, T), psM[:, 0:D], ALU.add).then_inc(x1_done, 1)

            def slot(T, r, n):
                for k in range(H):
                    if exists(T) and k == 0:
                        m_parts(T, r)
                    if exists(T + 2) and k == NORM_AT:
                        normalize(T + 2)
                    if exists(T) and k == MAX_AT:
                        q2T_copy(T, r)
                    if exists(T + 1):
                        maxes(T + 1, (r + 1) % RING, k)
                    if exists(T - 1):
                        if k == O_AT:
                            weigh(T - 1)
                        if k == OUT_AT:
                            add_attention(T - 1)
                    if exists(T + 2) and k == KT_AT:
                        kT_copy(T + 2, (r + 2) % RING)
                    if routed(n):
                        u = H * (r % GT) + k
                        if u == STATS_AT:
                            route_stats(dve, n, GT * n, x1_done)
                        if u == RN_AT:
                            route_normalize(dve, n, GT * n)
                        if TOP_AT <= u < TOP_AT + 12:
                            route_top(dve, n, u - TOP_AT)
                        if ROWS_AT <= u < ROWS_AT + 4:
                            route_rows(dve, n, u - ROWS_AT)

            dve.memset(V32[:, :, :, HD + 1:32], 0.0).then_inc(const_v, 1)
            dve.memset(V32[:, :, :, HD], 1.0).then_inc(const_v, 1)
            dve.memset(SEL3[:, :], 0.0).then_inc(const_v, 1)
            dve.wait_ge(const_v, 3)
            for part in range(3):
                dve.memset(SEL3[32 * part:32 * part + 1, :], 1.0).then_inc(const_v, 1)
            dve.memset(LT[LATENT:LATENT + 1, :, :], 1.0).then_inc(b_const, 1)
            for b in range(BATCH):
                dve.wait_ge(x_in[b], 16)
            statistics(dve, 0)
            dve.wait_ge(f_w_in, 32)
            dve.wait_ge(f_const, 13)
            dve.tensor_copy(RUN[:, :], RUN0[:, :]).then_inc(b_const, 1)
            dve.wait_ge(b_const, 2)
            over_tiles(dve, slot)
            expert_tables(dve, 0)
            experts_dve(dve, 0)
            statistics(dve, 1)
            dve.wait_ge(e_link, E_LINKS)
            attb_dve(dve)
            expert_tables(dve, 1)
            experts_dve(dve, 1)


_OUTS = [((BATCH, SEQ, D), 'float32')]


def rope_table(np):
    inv = (1.0 / 10000.0 ** (np.arange(0, HD, 2, dtype=np.float32) / HD)).astype(np.float32)
    angle = np.arange(SEQ, dtype=np.float32)[:, None] * inv[None, :]
    cos, sin = np.cos(angle), np.sin(angle)
    table = np.stack([np.concatenate([cos, cos], 1), np.concatenate([-sin, sin], 1)], 1)
    return table.reshape(TPB, P, 2, HD).transpose(1, 0, 2, 3).astype(np.float32)


def kernel(**inputs):
    import numpy as _np
    import concourse.bacc as _bacc
    from concourse import mybir as _mybir
    from concourse.bass_utils import run_bass_kernel_spmd as _run

    nc = _bacc.Bacc("TRN2", target_bir_lowering=False, num_devices=1)
    w1, w2, b1 = (_np.asarray(inputs[f"L0_ffn_{n}"]) for n in ("w1", "w2", "b1"))
    given = {
        "h": inputs["L0_attn_a_h"],
        "Wqvk": inputs["L0_attn_a_Wqvk"],
        "Wo": inputs["L0_attn_a_Wo"],
        "gate_w": inputs["L0_ffn_gate_w"],
        "gate_b": _np.asarray(inputs["L0_ffn_gate_b"]).reshape(1, NE),
        "w1": w1,
        "w2pack": w2.reshape(NE, FC, P, D).transpose(0, 2, 1, 3).reshape(NE, P, FC * D),
        "b1": b1.reshape(NE, FC, P).transpose(2, 0, 1).reshape(P, NE * FC),
        "b2": _np.asarray(inputs["L0_ffn_b2"]).reshape(1, NE * D),
        "Wq": inputs["L0_attn_b_Wq"],
        "bq": _np.asarray(inputs["L0_attn_b_bq"]).reshape(1, D),
        "Wdown": inputs["L0_attn_b_Wdown"],
        "bdown": _np.asarray(inputs["L0_attn_b_bdown"]).reshape(LATENT, 1),
        "Wup": inputs["L0_attn_b_Wup"],
        "bup": _np.asarray(inputs["L0_attn_b_bup"]).reshape(1, 2 * D),
        "Wout": inputs["L0_attn_b_Wout"],
        "bout": _np.asarray(inputs["L0_attn_b_bout"]).reshape(1, D),
        "rope": rope_table(_np),
    }
    arrays, args = {}, []
    for name, x in given.items():
        a = _np.ascontiguousarray(x)
        arrays[f"in_{name}_dram"] = a
        args.append(nc.dram_tensor(f"in_{name}_dram", a.shape, _mybir.dt.from_np(a.dtype), kind="ExternalInput").ap())
    for i, (shape, dtype) in enumerate(_OUTS):
        dt = _mybir.dt.from_np(_np.dtype(dtype))
        args.append(nc.dram_tensor(f"out_{i}_dram", shape, dt, kind="ExternalOutput").ap())
    hybrid_layer(nc, *args)
    r = _run(nc, [arrays], core_ids=[0])
    return r.results[0]["out_0_dram"]
```

```python
from contextlib import ExitStack

import concourse.bass as bass
from concourse import mybir

F32 = mybir.dt.float32
BF16 = mybir.dt.bfloat16
I32 = mybir.dt.int32
ALU = mybir.AluOpType
ACT = mybir.ActivationFunctionType
AX = mybir.AxisListType

P = 128
D = 128
BATCH, SEQ = 8, 512
TILES = BATCH * SEQ // P
TPB = SEQ // P
H, HD = 16, 8
PAIRS = H // 2
G4 = H // 4
LAG = 6
NORM_AT, X_AT, QKV_AT, QT_AT, KT_AT = 0, 1, 2, 12, 14
GROUP_AT = 4
MAX_AT = 2
PV_AFTER = LAG + 5
O_COPY_AT, O_AT, WV_AT, OUT_AT = LAG + 1, LAG + 3, LAG + 5, LAG + 7
STATS_AT, RN_AT, RT_AT, RL_AT, TOP_AT, RANK_AT, ROWS_AT = 14, 17, 19, 21, 23, 36, 39
RING = 2 * TPB
EPS = 1e-5
NEG = -1e30
SLOTS = 6
HEADW = 64
K48 = SLOTS * HD

LATENT = 32
NE, FF = 24, 512
FC = FF // P
GT = 4
TOKENS = TILES * P
REGION = TOKENS + P
DUMMY = NE * REGION
ROW_W = D + 2
STEP = 8
ROW_TILES = STEP * -(-((2 * TOKENS - NE) // P + NE) // STEP)
B2_EXPERTS = 6
SEND_LAG = 3
NOWHERE = 2 * 2 * TOKENS


def hybrid_layer(nc, h, Wqvk, Wo, gate_w, gate_b, w1, w2pack, b1, b2, Wq, bq, Wdown, bdown, Wup, bup, Wout, bout, rope, out):
    ctx = ExitStack()
    with ctx:
        def sb(name, shape, dt=F32):
            return ctx.enter_context(nc.sbuf_tensor(name, shape, dt))

        def ps(name, shape, dt=F32):
            return ctx.enter_context(nc.psum_tensor(name, shape, dt))

        def sem(name):
            return ctx.enter_context(nc.semaphore(name))

        X = sb("X", [P, TILES, D])
        NHALF = sb("NHALF", [P, GT])
        ZERO = sb("ZERO", [P, 2 * H])
        ONE = sb("ONE", [P, 1])
        IDF = sb("IDF", [P, P])
        IDB = sb("IDB", [P, P], BF16)
        MASK = sb("MASK", [P, P], BF16)
        MASKT = sb("MASKT", [P, P], BF16)
        WQ = sb("WQ", [D, 3 * D])
        WO = sb("WO", [D, D])
        XN = sb("XN", [P, D])
        XT = sb("XT", [D, P])
        QK = sb("QK", [P, 2, D])
        R1 = sb("R1", [P, 2, D])
        QS = sb("QS", [P, 2, H, HEADW], BF16)
        KS = sb("KS", [P, H, HEADW], BF16)
        QT = sb("QT", [P, 2, PAIRS, P], BF16)
        QT2 = sb("QT2", [P, 2, PAIRS, P], BF16)
        KT = sb("KT", [P, RING, PAIRS, P], BF16)
        V32 = sb("V32", [P, RING, H, 32])
        NM = sb("NM", [P, 2, H])
        PT = sb("PT", [P, 2, 4, SEQ])
        OS = sb("OS", [P, G4, P])
        RS = sb("RS", [P, H])
        WV = sb("WV", [P, D])
        WVT = sb("WVT", [D, P])

        XG = sb("XG", [P, 2, GT, 2, ROW_W])
        XGT = sb("XGT", [D, GT, P])
        XS = sb("XS", [P, 2, D])
        XST = sb("XST", [D, 2, P])
        GW = sb("GW", [D, NE])
        GB = sb("GB", [P, NE])
        ONER = sb("ONER", [1, P])
        UT = sb("UT", [P, P], BF16)
        ONESB = sb("ONESB", [P, P], BF16)
        STAT = sb("STAT", [P, GT, 6])
        MEAN = sb("MEAN", [P, RING])
        VAR = sb("VAR", [P, RING])
        DIFF = sb("DIFF", [P, GT])
        RSD = sb("RSD", [P, RING])
        SHIFT = sb("SHIFT", [P, RING])
        STG = sb("STG", [P, GT, 6])
        MEG = sb("MEG", [P, GT])
        VAG = sb("VAG", [P, GT])
        DIG = sb("DIG", [P, GT])
        RSG = sb("RSG", [P, GT])
        SHG = sb("SHG", [P, GT])
        LG = sb("LG", [P, GT, NE])
        IOTA_E = sb("IOTA_E", [P, NE])
        IOTA_J = sb("IOTA_J", [ROW_TILES, 1])
        DEST = sb("DEST", [P, TILES, 2], I32)
        O1H = [sb(f"O1H{k}", [P, GT, NE]) for k in range(2)]
        CAND = sb("CAND", [P, GT, NE])
        MSK = sb("MSK", [P, GT, NE], BF16)
        TOP = sb("TOP", [P, 2, GT])
        TDIF = sb("TDIF", [P, GT])
        IDX = sb("IDX", [P, GT])
        EXPD = sb("EXPD", [P, GT])
        EXP1 = sb("EXP1", [P, GT])
        RUN0 = sb("RUN0", [P, NE])
        RUN = sb("RUN", [P, NE])
        POSF = sb("POSF", [P, GT, 2])
        POS = sb("POS", [P, 2, GT, 2], I32)
        CE = sb("CE", [ROW_TILES, NE])
        TI = sb("TI", [ROW_TILES, NE], I32)
        TF = sb("TF", [ROW_TILES, NE])
        TEND = sb("TEND", [ROW_TILES, NE])
        ONES_E = sb("ONES_E", [ROW_TILES, NE])
        CMP = sb("CMP", [ROW_TILES, NE])
        ERF = sb("ERF", [ROW_TILES, 2])
        EJ = sb("EJ", [1, ROW_TILES], I32)
        RJ = sb("RJ", [1, ROW_TILES], I32)
        PADR = sb("PADR", [1, NE], I32)
        PAD = sb("PAD", [P, ROW_W])
        B1 = sb("B1", [P, NE * FC])
        W2 = sb("W2", [P, NE, FC * D])
        B2P = sb("B2P", [96, NE * D], BF16)
        B2F = sb("B2F", [96, B2_EXPERTS * D])
        SEL3 = sb("SEL3", [96, P], BF16)
        XI = sb("XI", [P, STEP, ROW_W])
        XI_I, XG_I, PAD_I = (x.bitcast(I32) for x in (XI[:, :, :], XG[:, :, :, :, :], PAD[:, :]))
        XIT = sb("XIT", [D, 2, P])
        in_keys = KT[:, :, :, :].rearrange("p r g t -> p (r g t)").bitcast(F32)
        W1 = in_keys.rearrange("p (a n) -> p a n", a=STEP)
        HT = QT[:, :, :, :].rearrange("p a g t -> p (a g t)").bitcast(F32).rearrange("p (a c t) -> p a c t", a=2, c=FC)
        WARM = sb("WARM", [P, 1])
        SETTLE = sb("SETTLE", [P, 2])
        Y = sb("Y", [P, 4, D])
        YC = in_keys.rearrange("p (a k t d) -> p a k t d", a=4, k=2, t=GT)

        f_w_in = sem("f_w_in")
        f_const = sem("f_const")
        f_dummy = sem("f_dummy")
        f_stat = sem("f_stat")
        f_stat1 = sem("f_stat1")
        f_stat2 = sem("f_stat2")
        f_var = sem("f_var")
        f_sq = sem("f_sq")
        f_pow = sem("f_pow")
        f_rstd = sem("f_rstd")
        r_stat = sem("r_stat")
        r_s1 = sem("r_s1")
        r_s2 = sem("r_s2")
        r_var = sem("r_var")
        r_g1 = sem("r_g1")
        r_g2 = sem("r_g2")
        r_sq = sem("r_sq")
        r_pow = sem("r_pow")
        r_rstd = sem("r_rstd")
        r_xg = sem("r_xg")
        r_xg2 = sem("r_xg2")
        r_xadd = sem("r_xadd")
        r_xT = sem("r_xT")
        r_xTc = sem("r_xTc")
        r_lg = sem("r_lg")
        r_link = sem("r_link")
        r_mask = sem("r_mask")
        r_top = sem("r_top")
        r_settled = sem("r_settled")
        r_exp = sem("r_exp")
        r_rank = sem("r_rank")
        r_pos = sem("r_pos")
        r_gate = sem("r_gate")
        r_scat = [sem(f"r_scat{i}") for i in range(2)]
        e_link = sem("e_link")
        e_flat = sem("e_flat")
        e_turned = sem("e_turned")
        w2_in = sem("w2_in")
        b2_in = sem("b2_in")
        b2_split = sem("b2_split")
        e_settled = sem("e_settled")
        e_pad = sem("e_pad")
        e_tables = sem("e_tables")
        e_padded = sem("e_padded")
        f_load = [sem(f"f_load{i}") for i in range(STEP)]
        f_xiT = sem("f_xiT")
        f_xit = sem("f_xit")
        f_up = sem("f_up")
        f_gelu = sem("f_gelu")
        f_down = sem("f_down")
        f_y = sem("f_y")
        f_ys = [sem(f"f_ys{i}") for i in range(STEP)]
        f_yc = [[sem(f"f_yc{ph}{i}") for i in range(2 + 2 * ph)] for ph in range(2)]
        f_ysum = sem("f_ysum")
        f_done = sem("f_done")

        rows_in = nc.dram_tensor("rows_in", [(NE + 1) * REGION, ROW_W], F32, kind="Internal").ap()
        rows_out = nc.dram_tensor("rows_out", [2 * TOKENS, D], F32, kind="Internal").ap()
        rows_out_v = rows_out.rearrange("(k t p) d -> p k t d", p=P, k=2)
        GROUPS = TILES // GT
        R_LINKS = 15
        E_LINKS = 10
        B2_STEPS = 6

        BQ_W = sb("BQ_W", [D, D])
        BQ_B = sb("BQ_B", [1, D])
        BD_W = sb("BD_W", [D, LATENT])
        BD_B = sb("BD_B", [LATENT, 1])
        BU_W = sb("BU_W", [LATENT + 1, 2 * D])
        BO_W = sb("BO_W", [D, D])
        BO_B = sb("BO_B", [1, D])
        ROPE = sb("ROPE", [P, TPB, 2, HD])
        LT = sb("LT", [LATENT + 1, 2, P])
        QKR = in_keys[:, 0:4 * D].rearrange("p (a b h d) -> p a b h d", a=2, b=2, h=H)
        VB = sb("VB", [P, 8, H, HD])
        T1 = sb("T1", [P, 2, 2, H, HD])
        T2 = sb("T2", [P, 2, H, HD])
        ROT = in_keys[:, 8 * D:12 * D].rearrange("p (a b h d) -> p a b h d", a=2, b=2, h=H)
        PROD = PT[:, :, :, :].rearrange("p a j (h g d) -> p a (j h) g d", g=H, d=HD)
        ATT = sb("ATT", [P, H, H])
        AMX = sb("AMX", [P, H])
        SH = in_keys[:, 12 * D:16 * D].rearrange("p (a h g) -> p a h g", a=2, h=H)
        EX = sb("EX", [P, 2, H, H])
        PROD2 = V32[:, 0:TPB, :, :].rearrange("p t h a -> p (t h a)").rearrange("p (g h d) -> p g h d", g=H, h=H)
        ASUM = sb("ASUM", [P, H])
        ARS = sb("ARS", [P, H])
        BWV = sb("BWV", [P, 2, D])
        BWVT = sb("BWVT", [D, 2, P])

        b_w_in = sem("b_w_in")
        b_const = sem("b_const")
        b_xs = sem("b_xs")
        b_xsT = sem("b_xsT")
        b_xst = sem("b_xst")
        b_ql = sem("b_ql")
        b_lat = sem("b_lat")
        b_kv = sem("b_kv")
        b_qk = sem("b_qk")
        b_v = sem("b_v")
        b_rope1 = sem("b_rope1")
        b_cos = sem("b_cos")
        b_rot = sem("b_rot")
        b_prod = sem("b_prod")
        b_att = sem("b_att")
        b_max = sem("b_max")
        b_sh = sem("b_sh")
        b_ex = sem("b_ex")
        b_p2 = sem("b_p2")
        b_red2 = sem("b_red2")
        b_sum = sem("b_sum")
        b_rs = sem("b_rs")
        b_wv = sem("b_wv")
        b_wvT = sem("b_wvT")
        b_wvt = sem("b_wvt")
        b_o = sem("b_o")
        b_x = sem("b_x")
        banks = [ps(f"bank{i}", [P, SEQ]) for i in range(8)]
        psA, psB = banks[0:2], banks[2:4]
        psO = banks[4][:, :].rearrange("p (q t) -> p q t", q=G4)
        psM = banks[5]
        psT, psK = (b[:, :].bitcast(BF16).rearrange("p (g t) -> p g t", g=PAIRS) for b in banks[6:8])
        psG = banks[7]
        psXI, psH, psY = banks[0:2], banks[2:4], banks[4:6]
        psP, psF, psS = banks[0:2], banks[2:4], banks[4:6]

        x_in = [sem(f"x_in{b}") for b in range(BATCH)]
        w_in = sem("w_in")
        const_a = sem("const_a")
        const_ready = sem("const_ready")
        xn_done = sem("xn_done")
        xT_done = sem("xT_done")
        xT_copied = sem("xT_copied")
        qkv_done = sem("qkv_done")
        qk_copied = sem("qk_copied")
        v_copied = sem("v_copied")
        hi_done = sem("hi_done")
        mid_done = sem("mid_done")
        r1_done = sem("r1_done")
        parts_done = sem("parts_done")
        qT_done = sem("qT_done")
        kT_done = sem("kT_done")
        q2T_done = sem("q2T_done")
        qT_copied = sem("qT_copied")
        kT_copied = sem("kT_copied")
        q2T_copied = sem("q2T_copied")
        scoresA_done = sem("scoresA_done")
        max_done = sem("max_done")
        m_hi_done = sem("m_hi_done")
        m_done = sem("m_done")
        scoresB_done = sem("scoresB_done")
        exp_done = sem("exp_done")
        pv_done = sem("pv_done")
        o_copied = sem("o_copied")
        oT_done = sem("oT_done")
        rs_done = sem("rs_done")
        wv_done = sem("wv_done")
        wvT_done = sem("wvT_done")
        wvT_copied = sem("wvT_copied")
        wo_done = sem("wo_done")
        x1_done = sem("x1_done")
        out_sent = sem("out_sent")
        const_v = sem("const_v")

        h_v = h.rearrange("b (t p) d -> p (b t) d", p=P)
        out_v = out.rearrange("b (t p) d -> p (b t) d", p=P)

        block = ctx.enter_context(nc.Block())

        def wait(eng, semaphore, n):
            if not isinstance(n, int) or n > 0:
                eng.wait_ge(semaphore, n)

        def exists(T):
            return not isinstance(T, int) or 0 <= T < TILES

        def routed(n):
            return not isinstance(n, int) or 0 <= n < TILES // GT

        def over_tiles(eng, slot):
            for T in range(-2, RING):
                slot(T, T % RING, T // GT - 1)
            with eng.Fori(1, TILES // RING - 1) as i:
                for r in range(RING):
                    slot(RING * i + r, r, RING // GT * i + (r // GT - 1))
            for T in range(TILES - RING, TILES + 4):
                slot(T, T % RING, T // GT - 1)

        def ffn_consts_pool(pool):
            pool.memset(UT[:, :], 1.0).then_inc(f_const, 1)
            pool.memset(ONESB[:, :], 1.0).then_inc(f_const, 1)
            pool.memset(ONES_E[:, :], 1.0).then_inc(f_const, 1)
            pool.memset(ONER[:, :], 1.0).then_inc(f_const, 1)
            pool.memset(PAD[:, :], 0.0).then_inc(f_const, 1)
            pool.iota(IOTA_E[:, :], pattern=[[1, NE]], base=0, channel_multiplier=0,
                      allow_small_or_imprecise_dtypes=True).then_inc(f_const, 1)
            pool.iota(IOTA_J[:, :], pattern=[[0, 1]], base=0, channel_multiplier=1,
                      allow_small_or_imprecise_dtypes=True).then_inc(f_const, 1)
            pool.iota(RUN0[:, :], pattern=[[REGION, NE]], base=0, channel_multiplier=0,
                      allow_small_or_imprecise_dtypes=True).then_inc(f_const, 1)
            pool.iota(DEST[:, :, :], pattern=[[P, TILES], [TOKENS, 2]], base=0, channel_multiplier=1).then_inc(f_const, 1)
            pool.wait_ge(f_const, 9)
            pool.affine_select(out=UT[:, :], in_=UT[:, :], compare_op=ALU.is_gt, fill=0.0, base=0,
                               pattern=[[1, P]], channel_multiplier=-1).then_inc(f_const, 1)
            pool.iota(PAD_I[:, D + 1:D + 2], pattern=[[0, 1]], base=NOWHERE, channel_multiplier=0).then_inc(f_const, 1)

        def ffn_consts_sp(sp):
            sp.dma_start(GW[:, :], gate_w).then_inc(f_w_in, 16)
            sp.dma_start(GB[:, :], gate_b.broadcast_to([P, NE])).then_inc(f_w_in, 16)
            sp.wait_ge(f_const, 11)
            sp.dma_start(rows_in[DUMMY:DUMMY + P, :], PAD[:, :]).then_inc(f_dummy, 16)

        def split_b2(pool, c):
            done = [B2_STEPS * c]

            def step(rows, out_, a, b, op):
                wait(pool, b2_split, done[0])
                pool.tensor_tensor(out_[rows, :], a[rows, :], b[rows, :], op).then_inc(b2_split, 1)
                done[0] += 1

            part = B2P[:, c * B2_EXPERTS * D:(c + 1) * B2_EXPERTS * D]
            every, second, third = slice(0, 96), slice(32, 64), slice(64, 96)
            one = ONE[0:96, :].broadcast_to([96, B2_EXPERTS * D])
            pool.wait_ge(b2_in, 16 * (c + 1))
            step(every, part, B2F, one, ALU.mult)
            step(every, B2F, B2F, part, ALU.subtract)
            step(second, part, B2F, one, ALU.mult)
            step(third, part, B2F, one, ALU.mult)
            step(third, B2F, B2F, part, ALU.subtract)
            step(third, part, B2F, one, ALU.mult)
            pool.wait_ge(b2_split, done[0])

        def tiles_at(x, T, count=1):
            return x[:, bass.ds(T, count), :]

        def row_at(x, T):
            return x[:, bass.ds(T, 1), :].rearrange("p a d -> p (a d)")

        def group_stats(dve, n, T0, par):
            mean, var = MEAN[:, par * GT:(par + 1) * GT], VAR[:, par * GT:(par + 1) * GT]
            for t in range(GT):
                i = dve.bn_stats(STAT[:, t, :], row_at(X, T0 + t))
            i.then_inc(f_stat, 1)
            dve.wait_ge(f_stat, n + 1)
            dve.tensor_tensor(mean, STAT[:, :, 1], STAT[:, :, 4], ALU.add)
            dve.tensor_tensor(var, STAT[:, :, 2], STAT[:, :, 5], ALU.add)
            dve.tensor_tensor(DIFF[:, :], STAT[:, :, 1], STAT[:, :, 4], ALU.subtract).then_inc(f_stat1, 1)
            dve.wait_ge(f_stat1, n + 1)
            dve.tensor_scalar(mean, mean, -0.5, None, ALU.mult)
            dve.tensor_tensor(DIFF[:, :], DIFF[:, :], DIFF[:, :], ALU.mult).then_inc(f_stat2, 1)
            dve.wait_ge(f_stat2, n + 1)
            dve.scalar_tensor_tensor(var, DIFF[:, :], D / 4.0, var, ALU.mult, ALU.add).then_inc(f_sq, 1)
            dve.wait_ge(f_sq, n + 1)
            dve.tensor_scalar(var, var, 1.0 / D, EPS, ALU.mult, ALU.add).then_inc(f_var, 1)

        def group_deviation(pool, n, par):
            group = slice(par * GT, (par + 1) * GT)
            pool.wait_ge(f_var, n + 1)
            pool.tensor_tensor(RSD[:, group], VAR[:, group], NHALF[:, :], ALU.pow).then_inc(f_pow, 1)
            pool.wait_ge(f_pow, n + 1)
            pool.tensor_tensor(SHIFT[:, group], MEAN[:, group], RSD[:, group], ALU.mult).then_inc(f_rstd, 1)


        def route_stats(dve, n, T0, x_done):
            dve.wait_ge(x_done, T0 + GT)
            wait(dve, r_var, n)
            for t in range(GT):
                i = dve.bn_stats(STG[:, t, :], row_at(X, T0 + t))
            i.then_inc(r_stat, 1)
            dve.wait_ge(r_stat, n + 1)
            wait(dve, r_xg, n)
            dve.tensor_tensor(MEG[:, :], STG[:, :, 1], STG[:, :, 4], ALU.add)
            dve.tensor_tensor(VAG[:, :], STG[:, :, 2], STG[:, :, 5], ALU.add)
            dve.tensor_tensor(DIG[:, :], STG[:, :, 1], STG[:, :, 4], ALU.subtract).then_inc(r_s1, 1)
            dve.wait_ge(r_s1, n + 1)
            dve.tensor_scalar(MEG[:, :], MEG[:, :], -0.5, None, ALU.mult)
            dve.tensor_tensor(DIG[:, :], DIG[:, :], DIG[:, :], ALU.mult).then_inc(r_s2, 1)
            dve.wait_ge(r_s2, n + 1)
            dve.scalar_tensor_tensor(VAG[:, :], DIG[:, :], D / 4.0, VAG[:, :], ALU.mult, ALU.add).then_inc(r_sq, 1)
            dve.wait_ge(r_sq, n + 1)
            dve.tensor_scalar(VAG[:, :], VAG[:, :], 1.0 / D, EPS, ALU.mult, ALU.add).then_inc(r_var, 1)

        def route_deviation(pool, n):
            pool.wait_ge(r_var, n + 1)
            pool.tensor_tensor(RSG[:, :], VAG[:, :], NHALF[:, :], ALU.pow).then_inc(r_pow, 1)
            pool.wait_ge(r_pow, n + 1)
            pool.tensor_tensor(SHG[:, :], MEG[:, :], RSG[:, :], ALU.mult).then_inc(r_rstd, 1)

        def route_normalize(act, n, par, T0):
            wait(act, r_scat[par], 16 * GT * (n - par))
            act.wait_ge(r_rstd, n + 1)
            for t in range(GT):
                a = act.activation(XG[:, par, t, 0, 0:D], row_at(X, T0 + t), ACT.Identity, scale=RSG[:, t:t + 1],
                                   bias=SHG[:, t:t + 1])
            a.then_inc(r_xg, 1)

        def route_numbers(dve, n, par, T0):
            wait(dve, r_scat[par], 16 * GT * (n - par))
            dve.tensor_copy(XG_I[:, par, :, :, D + 1], tiles_at(DEST, T0, GT))

        def route_transpose(pe, n, par, keys_copied=None, bank_keys=0):
            pe.wait_ge(r_xg, n + 1)
            wait(pe, r_pos, n)
            wait(pe, keys_copied, bank_keys)
            for t in range(GT):
                mm = pe.transpose(psG[:, t * P:(t + 1) * P], XG[:, par, t, 0, 0:D], IDF[:, :])
            mm.then_inc(r_xT, 1)

        def route_copy(act, n):
            act.wait_ge(r_xT, n + 1)
            act.activation(XGT[:, :, :], psG[:, :].rearrange("p (t c) -> p t c", t=GT), ACT.Copy).then_inc(r_xTc, 1)

        def route_second(act, n, par):
            act.wait_ge(r_xg, n + 1)
            act.activation(XG[:, par, :, 1, 0:D], XG[:, par, :, 0, 0:D], ACT.Copy).then_inc(r_xg2, 1)

        def route_logits(pe, n):
            pe.wait_ge(r_xTc, n + 1)
            for t in range(GT):
                mm = pe.matmul(psG[:, t * NE:(t + 1) * NE], XGT[:, t, :], GW[:, :], start=True, stop=True)
            mm.then_inc(r_lg, 1)

        def linker(dve, done, base):
            count = [0]

            def link(ins):
                count[0] += 1
                ins.then_inc(done, 1)
                dve.wait_ge(done, base + count[0])
            return link

        def over_e(x):
            return x.unsqueeze(2).broadcast_to([P, GT, NE])

        def over_t(x):
            return x.unsqueeze(1).broadcast_to([P, GT, NE])

        def route_top(dve, n, i):
            k = 0 if i < 7 else 1
            wait(dve, r_link, R_LINKS * n + i)
            if i == 0:
                dve.wait_ge(r_lg, n + 1)
                a = dve.tensor_tensor(LG[:, :, :], psG[:, 0:GT * NE].rearrange("p (t e) -> p t e", e=NE), over_t(GB[:, :]), ALU.add)
            if i in (1, 7):
                a = dve.tensor_reduce(TOP[:, k, :], LG[:, :, :], AX.X, ALU.max)
            if i in (2, 8):
                a = dve.tensor_tensor(CAND[:, :, :], LG[:, :, :], over_e(TOP[:, k, :]), ALU.is_lt)
            if i in (3, 9):
                a = dve.scalar_tensor_tensor(CAND[:, :, :], CAND[:, :, :], float(NE), over_t(IOTA_E[:, :]), ALU.mult, ALU.add)
            if i in (4, 10):
                a = dve.tensor_reduce(IDX[:, :], CAND[:, :, :], AX.X, ALU.min)
            if i in (5, 11):
                a = dve.tensor_tensor(O1H[k][:, :, :], over_t(IOTA_E[:, :]), over_e(IDX[:, :]), ALU.is_equal)
            if i == 6:
                a = dve.scalar_tensor_tensor(LG[:, :, :], O1H[0][:, :, :], NEG, LG[:, :, :], ALU.mult, ALU.add)
            a.then_inc(r_link, 1)
            if i == 8:
                dve.tensor_tensor(TDIF[:, :], TOP[:, 1, :], TOP[:, 0, :], ALU.subtract).then_inc(r_top, 1)
            if i == 11:
                dve.wait_ge(r_link, R_LINKS * n + 12)
                dve.tensor_tensor(MSK[:, :, :], O1H[0][:, :, :], O1H[1][:, :, :], ALU.add).then_inc(r_mask, 1)

        def route_exp(act, n):
            act.wait_ge(r_top, n + 1)
            act.activation(EXPD[:, :], TDIF[:, :], ACT.Exp).then_inc(r_exp, 1)

        def route_ranks(pe, n):
            pe.wait_ge(r_mask, n + 1)
            for t in range(GT + 1):
                out_ = psG[:, (GT + t) * NE:(GT + t + 1) * NE]
                for b in range(t):
                    mm = pe.matmul(out_, ONESB[:, :], MSK[:, b, :], start=(b == 0), stop=(t == GT and b == t - 1))
                if t < GT:
                    mm = pe.matmul(out_, UT[:, :], MSK[:, t, :], start=(t == 0), stop=True)
            mm.then_inc(r_rank, 1)

        def route_rows(dve, n, par, i):
            wait(dve, r_link, R_LINKS * n + 12 + min(i, 3))
            if i == 0:
                dve.wait_ge(r_rank, n + 1)
                ranks = psG[:, GT * NE:2 * GT * NE].rearrange("p (t e) -> p t e", e=NE)
                dve.tensor_tensor(CAND[:, :, :], ranks, over_t(RUN[:, :]), ALU.add).then_inc(r_link, 1)
                dve.wait_ge(r_exp, n + 1)
                dve.tensor_scalar(EXP1[:, :], EXPD[:, :], 1.0, None, ALU.add).then_inc(r_g1, 1)
            if i == 1:
                dve.tensor_tensor(RUN[:, :], RUN[:, :], psG[:, 2 * GT * NE:(2 * GT + 1) * NE], ALU.add)
                for k in range(2):
                    c = dve.tensor_tensor(O1H[k][:, :, :], O1H[k][:, :, :], CAND[:, :, :], ALU.mult)
                c.then_inc(r_link, 1)
                dve.wait_ge(r_g1, n + 1)
                dve.reciprocal(XG[:, par, :, 0, D], EXP1[:, :]).then_inc(r_g2, 1)
            if i == 2:
                for k in range(2):
                    c = dve.tensor_reduce(POSF[:, :, k], O1H[k][:, :, :], AX.X, ALU.add)
                c.then_inc(r_link, 1)
                dve.wait_ge(r_g2, n + 1)
                dve.tensor_tensor(XG[:, par, :, 1, D], EXPD[:, :], XG[:, par, :, 0, D], ALU.mult).then_inc(r_gate, 1)
            if i == 3:
                dve.tensor_copy(POS[:, par, :, :], POSF[:, :, :]).then_inc(r_pos, 1)

        def route_keep(eng, n, par, T0):
            eng.tensor_tensor(tiles_at(X, T0, GT), tiles_at(X, T0, GT), XG[:, par, :, 0, 0:D], ALU.add).then_inc(r_xadd, 1)

        def route_settle(pool, n):
            pool.wait_ge(r_xg2, n + 1)
            pool.wait_ge(r_pos, n + 1)
            pool.wait_ge(r_gate, n + 1)

        def route_send(pool, n, par, tiles):
            for t in tiles:
                for k in range(2):
                    pool.indirect_dma_start(out=rows_in, in_=XG[:, par, t, k, :], in_offset=None,
                                            out_offset=bass.IndirectOffsetOnAxis(ap=POS[:, par, t, k:k + 1], axis=0),
                                            ).then_inc(r_scat[par], 16)


        def expert_tables(dve, ph):
            link = linker(dve, e_link, E_LINKS * ph)
            dve.wait_ge(r_link, R_LINKS * GROUPS * (ph + 1))
            rows = slice(0, ROW_TILES)
            link(dve.tensor_tensor(CE[:, :], RUN[rows, :], RUN0[rows, :], ALU.subtract))
            dve.tensor_copy(PADR[:, :], RUN[0:1, :]).then_inc(e_pad, 1)
            link(dve.tensor_scalar(TI[:, :], CE[:, :], float(P - 1), None, ALU.add))
            link(dve.tensor_scalar(TI[:, :], TI[:, :], 7, None, ALU.arith_shift_right))
            link(dve.tensor_copy(TF[:, :], TI[:, :]))
            link(dve.tensor_tensor_scan(TEND[:, :], ONES_E[:, :], TF[:, :], 0.0, ALU.mult, ALU.add))
            link(dve.tensor_scalar(CMP[:, :], TEND[:, :], IOTA_J[:, :], None, ALU.is_le))
            dve.tensor_scalar(TF[:, :], TF[:, :], -float(P), float(REGION), ALU.mult, ALU.add)
            link(dve.tensor_reduce(ERF[:, 0:1], CMP[:, :], AX.X, ALU.add))
            link(dve.tensor_tensor(CMP[:, :], CMP[:, :], TF[:, :], ALU.mult))
            link(dve.tensor_reduce(ERF[:, 1:2], CMP[:, :], AX.X, ALU.add))
            dve.scalar_tensor_tensor(ERF[:, 1:2], IOTA_J[:, :], float(P), ERF[:, 1:2], ALU.mult, ALU.add).then_inc(e_flat, 1)
            dve.wait_ge(e_turned, ph + 1)
            dve.tensor_scalar(EJ[:, :], psG[0:1, 0:ROW_TILES], float(NE - 1), None, ALU.min)
            dve.tensor_scalar(RJ[:, :], psG[0:1, P:P + ROW_TILES], float(DUMMY), None, ALU.min).then_inc(e_tables, 1)
            link(dve.tensor_copy(RUN[:, :], RUN0[:, :]))

        now = {}

        def numbers(eng, name, table, most, count=STEP):
            regs = [eng.alloc_register(f"{name}{u}") for u in range(count)]

            def read(j0):
                eng.load(regs, table[0:1, bass.ds(j0, count)])
                return [eng.snap(r, min_val=0, max_val=most) for r in regs]
            return read

        def over_rows(eng, body, head=None):
            rounds = ROW_TILES // STEP
            now.update(head(0) if head else {})
            for j in range(STEP):
                body(j, j, True)
            with eng.Fori(1, rounds - 1) as i:
                now.update(head(STEP * i) if head else {})
                for u in range(STEP):
                    body(STEP * i + u, u, False)
            now.update(head(ROW_TILES - STEP) if head else {})
            for j in range(ROW_TILES - STEP, ROW_TILES):
                body(j, j % STEP, False)

        def per_buffer(ph, j, u, dmas):
            n = ph * (ROW_TILES // STEP) + 1
            if isinstance(j, int):
                return 16 * dmas * (n + j // STEP)
            return (j - u) * (16 * dmas // STEP) + 16 * dmas * n

        def sent_before(eng, ph, j, u, back):
            if not (isinstance(j, int) and j < back and ph == 0):
                v = (u - back) % STEP
                eng.wait_ge(f_ys[v], per_buffer(ph, j - back, v, 1))

        def pad_rows(eng, ph, half):
            name = f"end{ph}{half}_"
            ends = numbers(eng, name, PADR, DUMMY - P, NE // 2)
            for r in ends(half * NE // 2):
                eng.dma_start(rows_in[bass.ds(r, P), :], PAD[:, :]).then_inc(e_padded, 16)

        def fetch(eng, ph, g, k):
            buffers = len(f_yc[ph])
            before = ph * GROUPS + max(g + 1 - buffers, 0)
            if before > 0:
                eng.wait_ge(f_done, before)
            eng.dma_start(YC[:, 4 - buffers + g % buffers, k, :, :],
                          rows_out_v[:, k, g * GT:(g + 1) * GT, :]).then_inc(f_yc[ph][g % buffers], 16)

        def experts_sp(sp, ph):
            base = ph * ROW_TILES
            sp.wait_ge(e_pad, ph + 1)
            pad_rows(sp, ph, 0)
            sp.wait_ge(e_tables, ph + 1)
            sp.wait_ge(f_dummy, 16)
            sp.wait_ge(e_padded, 16 * NE * (ph + 1))
            for par in range(2):
                sp.wait_ge(r_scat[par], 16 * GT * GROUPS * (ph + 1))

            def load(j, u, first):
                sent_before(sp, ph, j, u, STEP)
                e, r = now["experts"][u], now["rows"][u]
                sp.dma_start(XI[:, u, :], rows_in[bass.ds(r, P), :]).then_inc(f_load[u], 16)
                sp.dma_start(W1[:, u, :], w1[bass.ds(e, 1), :, :].rearrange("a p n -> (a p) n")).then_inc(f_load[u], 16)

            experts, rows = numbers(sp, f"sp_expert{ph}_", EJ, NE - 1), numbers(sp, f"sp_row{ph}_", RJ, DUMMY)
            over_rows(sp, load, lambda j: {"experts": experts(j), "rows": rows(j)})

            def send_group(g):
                sp.wait_ge(f_done, GROUPS + g + 1)
                sp.dma_start(out_v[:, g * GT:(g + 1) * GT, :], X[:, g * GT:(g + 1) * GT, :]).then_inc(out_sent, 16)

            for i in range(STEP):
                sp.wait_ge(f_ys[i], 16 * (ROW_TILES // STEP) * (ph + 1))
            for g in range(GROUPS):
                fetch(sp, ph, g, 0)
                if ph == 0:
                    fetch(sp, ph, g, 1)
                if ph == 1 and g >= SEND_LAG:
                    send_group(g - SEND_LAG)
            if ph == 1:
                for g in range(GROUPS - SEND_LAG, GROUPS):
                    send_group(g)

        def experts_pool(pool, ph):
            base = ph * ROW_TILES

            def body(j, u, first):
                pool.wait_ge(f_y, base + j + 1)
                wait(pool, e_settled, base + j)
                pool.tensor_tensor(SETTLE[:, 0:1], ONE[:, :], ONE[:, :], ALU.mult).then_inc(e_settled, 1)
                pool.indirect_dma_start(out=rows_out, out_offset=bass.IndirectOffsetOnAxis(ap=XI_I[:, u, D + 1:D + 2], axis=0),
                                        in_=Y[:, u % 4, :], in_offset=None, bounds_check=2 * TOKENS - 1,
                                        oob_is_err=False).then_inc(f_ys[u], 16)

            over_rows(pool, body)

        def experts_act(act, ph):
            base = ph * ROW_TILES

            act.activation(WARM[:, :], ONE[:, :], ACT.Gelu)
            act.wait_ge(e_pad, ph + 1)
            pad_rows(act, ph, 1)
            act.wait_ge(e_tables, ph + 1)
            act.wait_ge(w2_in, 16 * (NE // B2_EXPERTS + 1))

            def gelu(j, u, first):
                e = now["experts"][u]
                act.wait_ge(f_up, base + j + 1)
                for c in range(FC):
                    a = act.activation(HT[:, u % 2, c, :], psH[u % 2][:, c * P:(c + 1) * P], ACT.Gelu,
                                       bias=B1[:, bass.ds(e * FC + c, 1)])
                a.then_inc(f_gelu, 1)

            experts = numbers(act, f"act_expert{ph}_", EJ, NE - 1)
            over_rows(act, gelu, lambda j: {"experts": experts(j)})
            if ph == 1:
                for i in range(STEP):
                    act.wait_ge(f_ys[i], 16 * (ROW_TILES // STEP) * (ph + 1))
                for g in range(GROUPS):
                    fetch(act, ph, g, 1)

        def experts_pe(pe, ph):
            base = ph * ROW_TILES

            def turn(j, u, first):
                pe.wait_ge(f_load[u], per_buffer(ph, j, u, 2))
                pe.transpose(psXI[u % 2][:, 0:P], XI[:, u, 0:D], IDF[:, :]).then_inc(f_xiT, 1)

            def up(j, u, first):
                pe.wait_ge(f_xit, base + j + 1)
                for c in range(FC):
                    mm = pe.matmul(psH[u % 2][:, c * P:(c + 1) * P], W1[:, u, c * P:(c + 1) * P], XIT[:, u % 2, :],
                                   start=True, stop=True)
                mm.then_inc(f_up, 1)

            def down(j, u, first):
                e = now["experts"][u]
                if isinstance(j, int) and j + 1 >= ROW_TILES:
                    pe.wait_ge(f_y, base + j - 1)
                pe.wait_ge(f_gelu, base + j + 1)
                for c in range(FC):
                    pe.matmul(psY[u % 2][:, 0:D], HT[:, u % 2, c, :],
                              W2[:, bass.ds(e, 1), c * D:(c + 1) * D].rearrange("p a d -> p (a d)"),
                              start=(c == 0), stop=False)
                pe.matmul(psY[u % 2][:, 0:D], SEL3[:, :], B2P[:, bass.ds(e * D, D)], start=False, stop=True).then_inc(f_down, 1)

            def body(j, u, first):
                if not (isinstance(j, int) and j + 1 >= ROW_TILES):
                    up(j + 1, (u + 1) % STEP, first and u < STEP - 1)
                if not (isinstance(j, int) and j + 2 >= ROW_TILES):
                    turn(j + 2, (u + 2) % STEP, first and u < STEP - 2)
                down(j, u, first)

            pe.wait_ge(e_flat, ph + 1)
            for i in range(2):
                mm = pe.matmul(psG[0:1, i * P:i * P + ROW_TILES], ERF[:, i:i + 1], IDF[0:ROW_TILES, 0:ROW_TILES],
                               start=True, stop=True)
            mm.then_inc(e_turned, 1)
            pe.wait_ge(e_tables, ph + 1)
            pe.wait_ge(w2_in, 16 * (NE // B2_EXPERTS + 1))
            pe.wait_ge(b2_split, B2_STEPS * (NE // B2_EXPERTS))
            turn(0, 0, True)
            turn(1, 1, True)
            up(0, 0, True)
            experts = numbers(pe, f"pe_expert{ph}_", EJ, NE - 1)
            over_rows(pe, body, lambda j: {"experts": experts(j)})

        def combine(dve, ph, g, par):
            n = ph * GROUPS + g
            x = tiles_at(X, GT * g, GT)
            buffers = len(f_yc[ph])
            y = YC[:, 4 - buffers + par]
            dve.wait_ge(f_yc[ph][par], (g - par) * (32 // buffers) + 32)
            dve.tensor_tensor(y[:, 0], y[:, 0], y[:, 1], ALU.add).then_inc(f_ysum, 1)
            dve.wait_ge(f_ysum, n + 1)
            dve.tensor_tensor(x, x, y[:, 0], ALU.add).then_inc(f_done, 1)

        def experts_dve(dve, ph):
            base = ph * ROW_TILES

            def xi_copy(j, u, first):
                dve.wait_ge(f_xiT, base + j + 1)
                dve.tensor_copy(XIT[:, u % 2, :], psXI[u % 2][:, 0:P]).then_inc(f_xit, 1)

            def gated(j, u, first):
                dve.wait_ge(f_down, base + j + 1)
                sent_before(dve, ph, j, u, 4)
                dve.tensor_scalar(Y[:, u % 4, :], psY[u % 2][:, 0:D], XI[:, u, D:D + 1], None, ALU.mult).then_inc(f_y, 1)

            def body(j, u, first):
                if not (isinstance(j, int) and j + 2 >= ROW_TILES):
                    xi_copy(j + 2, (u + 2) % STEP, first and u < STEP - 2)
                gated(j, u, first)

            xi_copy(0, 0, True)
            xi_copy(1, 1, True)
            over_rows(dve, body)
            dve.wait_ge(r_xadd, GROUPS * (ph + 1))

        def over_eights(eng, slot):
            for T in range(-3, RING):
                slot(T, T % RING, T // GT)
            with eng.Fori(1, TILES // RING - 1) as i:
                for s in range(RING):
                    slot(RING * i + s, s, RING // GT * i + s // GT)
            for T in range(TILES - RING, TILES + 2 * GT):
                slot(T, T % RING, T // GT)

        def attb_load(sp):
            for dst, src in ((BQ_W[:, :], Wq), (BQ_B[:, :], bq), (BD_W[:, :], Wdown), (BD_B[:, :], bdown),
                             (BU_W[0:LATENT, :], Wup), (BU_W[LATENT:LATENT + 1, :], bup), (BO_W[:, :], Wout),
                             (BO_B[:, :], bout), (ROPE[:, :, :, :], rope)):
                sp.dma_start(dst, src).then_inc(b_w_in, 16)

        def attb_pool(pool):
            def rotate(T, s):
                par = s % 2
                x, r = QKR[:, par], ROT[:, par]
                half = HD // 2

                def table(i, a, b):
                    return ROPE[:, s % TPB, i, a:b].unsqueeze(1).unsqueeze(1).broadcast_to([P, 2, H, b - a])

                pool.wait_ge(b_qk, 2 * (T + 1))
                wait(pool, b_rot, T)
                wait(pool, b_prod, T - 1)
                pool.tensor_tensor(T2[:, :, :, 0:half], x[:, :, :, half:HD], table(1, 0, half), ALU.mult).then_inc(b_rope1, 1)
                pool.tensor_tensor(T2[:, :, :, half:HD], x[:, :, :, 0:half], table(1, half, HD), ALU.mult).then_inc(b_rope1, 1)
                pool.wait_ge(b_rope1, 2 * (T + 1))
                pool.wait_ge(b_cos, T + 1)
                pool.tensor_tensor(r, T1[:, par], T2[:, :, :, :], ALU.add).then_inc(b_rot, 1)

            def products(T, s):
                par = s % 2
                pool.wait_ge(b_rot, T + 1)
                wait(pool, b_att, T - 1)
                pool.tensor_tensor(PROD[:, par], ROT[:, par, 0].unsqueeze(2).broadcast_to([P, H, H, HD]),
                                   ROT[:, par, 1].unsqueeze(1).broadcast_to([P, H, H, HD]), ALU.mult).then_inc(b_prod, 1)

            def slot(T, s, g):
                if exists(T + 1):
                    rotate(T + 1, (s + 1) % RING)
                if exists(T + 1):
                    products(T + 1, (s + 1) % RING)
                if s % GT == 0 and routed(g + 1) and exists(T):
                    group_deviation(pool, GROUPS + g + 1, (s // GT + 1) % 2)
                if s % GT == 2 and routed(g - 1):
                    route_deviation(pool, GROUPS + g - 1)
                if s % GT >= 2 and routed(g - 2):
                    if s % GT == 2:
                        wait(pool, r_settled, g - 2)
                        route_settle(pool, GROUPS + g - 2)
                        pool.tensor_tensor(SETTLE[:, 1:2], ONE[:, :], ONE[:, :], ALU.mult).then_inc(r_settled, 1)
                    route_send(pool, GROUPS + g - 2, s // GT, ((0, 1), (2, 3))[s % GT - 2])

            group_deviation(pool, GROUPS, 0)
            over_eights(pool, slot)

        def attb_pe(pe):
            def project(T, s):
                par = s % 2
                ps_ = psP[par]
                pe.wait_ge(b_xs, T + 1)
                wait(pe, b_v, T - 1)
                pe.transpose(ps_[:, 0:P], XS[:, par, :], IDF[:, :]).then_inc(b_xsT, 1)
                pe.wait_ge(b_xst, T + 1)
                pe.matmul(ps_[:, 0:D], XST[:, par, :], BQ_W[:, :], start=True, stop=False)
                pe.matmul(ps_[:, 0:D], ONER[:, :], BQ_B[:, :], start=False, stop=True)
                pe.matmul(ps_[0:LATENT, D:D + P], BD_W[:, :], XST[:, par, :], start=True, stop=True).then_inc(b_ql, 1)
                pe.wait_ge(b_lat, T + 1)
                pe.matmul(ps_[:, 2 * D:4 * D], LT[:, par, :], BU_W[:, :], start=True, stop=True).then_inc(b_kv, 1)

            def finish(T, s):
                par = s % 2
                pe.wait_ge(b_wv, T + 1)
                wait(pe, b_x, T - 1)
                pe.transpose(psF[par][:, 0:P], BWV[:, par, :], IDF[:, :]).then_inc(b_wvT, 1)
                pe.wait_ge(b_wvt, T + 1)
                pe.matmul(psF[par][:, 0:D], BWVT[:, par, :], BO_W[:, :], start=True, stop=False)
                pe.matmul(psF[par][:, 0:D], ONER[:, :], BO_B[:, :], start=False, stop=True).then_inc(b_o, 1)

            def total(T, s):
                pe.wait_ge(b_p2, T + 1)
                wait(pe, b_wv, T - 1)
                for v in range(H):
                    mm = pe.matmul(psS[s % 2][:, 0:D], IDF[:, :], PROD2[:, v, :, :], start=(v == 0), stop=(v == H - 1))
                mm.then_inc(b_sum, 1)

            def slot(T, s, g):
                if exists(T + 3):
                    project(T + 3, (s + 3) % RING)
                if exists(T - 2):
                    finish(T - 2, (s - 2) % RING)
                if s % GT == 3 and routed(g - 1):
                    route_logits(pe, GROUPS + g - 1)
                if s % GT == 1 and routed(g - 2):
                    route_ranks(pe, GROUPS + g - 2)
                if exists(T - 1):
                    total(T - 1, (s - 1) % RING)
                if s % GT == 2 and routed(g - 1):
                    route_transpose(pe, GROUPS + g - 1, 1 - s // GT)

            over_eights(pe, slot)

        def attb_act(act):
            def copies(T, s):
                par = s % 2
                ps_ = psP[par]
                act.wait_ge(b_xsT, T + 1)
                act.activation(XST[:, par, :], ps_[:, 0:P], ACT.Copy).then_inc(b_xst, 1)
                act.wait_ge(b_ql, T + 1)
                act.activation(LT[0:LATENT, par, :], ps_[0:LATENT, D:D + P], ACT.Identity, bias=BD_B[:, :]).then_inc(b_lat, 1)
                act.wait_ge(b_kv, T + 1)
                kv = ps_[:, 2 * D:4 * D].rearrange("p (h c) -> p h c", h=H)
                wait(act, b_rot, T - 1)
                act.activation(QKR[:, par, 0], ps_[:, 0:D].rearrange("p (h c) -> p h c", h=H), ACT.Copy).then_inc(b_qk, 1)
                act.activation(QKR[:, par, 1], kv[:, :, 0:HD], ACT.Copy).then_inc(b_qk, 1)
                wait(act, b_p2, T - 7)
                act.activation(VB[:, s], kv[:, :, HD:2 * HD], ACT.Copy).then_inc(b_v, 1)

            def normalize(T, s, g):
                if s % GT == 0:
                    act.wait_ge(f_rstd, GROUPS + g + 1)
                act.activation(XS[:, s % 2, :], row_at(X, T), ACT.Identity, scale=RSD[:, s:s + 1],
                               bias=SHIFT[:, s:s + 1]).then_inc(b_xs, 1)

            def slot(T, s, g):
                if exists(T + 3):
                    copies(T + 3, (s + 3) % RING)
                if exists(T - 2):
                    act.wait_ge(b_wvT, T - 1)
                    act.activation(BWVT[:, s % 2, :], psF[s % 2][:, 0:P], ACT.Copy).then_inc(b_wvt, 1)
                if exists(T):
                    act.wait_ge(b_sh, T + 1)
                    wait(act, b_red2, T - 1)
                    wait(act, b_p2, T - 1)
                    act.activation(EX[:, s % 2], SH[:, s % 2], ACT.Exp, scale=float(HD) ** -0.5).then_inc(b_ex, 1)
                if exists(T + 4):
                    normalize(T + 4, (s + 4) % RING, g + 1)
                if s % GT == 2 and routed(g - 1):
                    route_normalize(act, GROUPS + g - 1, 1 - s // GT, GT * (g - 1))
                    route_copy(act, GROUPS + g - 1)
                    route_second(act, GROUPS + g - 1, 1 - s // GT)
                if s % GT == 1 and routed(g - 2):
                    route_exp(act, GROUPS + g - 2)

            normalize(0, 0, 0)
            over_eights(act, slot)

        def attb_dve(dve):
            def tile_at(x, T):
                return x[:, bass.ds(T, 1), :].rearrange("p a d -> p (a d)")

            def cosines(T, s):
                dve.wait_ge(b_qk, 2 * (T + 1))
                wait(dve, b_rot, T - 1)
                dve.tensor_tensor(T1[:, s % 2], QKR[:, s % 2],
                                  ROPE[:, s % TPB, 0, :].unsqueeze(1).unsqueeze(1).broadcast_to([P, 2, H, HD]),
                                  ALU.mult).then_inc(b_cos, 1)

            def slot(T, s, g):
                def route(i):
                    if s % GT == 0 and routed(g - 2):
                        route_top(dve, GROUPS + g - 2, i)
                    if s % GT == 1 and routed(g - 2) and i < 4:
                        route_top(dve, GROUPS + g - 2, 8 + i)
                    if s % GT == 2 and routed(g - 2) and i < 4:
                        route_rows(dve, GROUPS + g - 2, s // GT, i)

                V = (s - 1) % RING
                if s % GT == 0 and routed(g + 1) and exists(T):
                    dve.wait_ge(f_done, g + 2)
                if exists(T):
                    dve.wait_ge(b_prod, T + 1)
                    wait(dve, b_sh, T)
                    dve.tensor_reduce(ATT[:, :, :], PROD[:, s % 2], AX.X, ALU.add).then_inc(b_att, 1)
                if exists(T - 3):
                    dve.wait_ge(b_o, T - 2)
                    dve.tensor_tensor(tile_at(X, T - 3), tile_at(X, T - 3), psF[(s - 3) % 2][:, 0:D],
                                      ALU.add).then_inc(b_x, 1)
                if s % GT == 2 and routed(g - 1):
                    route_stats(dve, GROUPS + g - 1, GT * (g - 1), b_x)
                if s % GT == 0 and routed(g + 1) and exists(T):
                    group_stats(dve, GROUPS + g + 1, GT * (g + 1), (s // GT + 1) % 2)
                route(0)
                if exists(T):
                    dve.wait_ge(b_att, T + 1)
                    dve.tensor_reduce(AMX[:, :], ATT[:, :, :], AX.X, ALU.max).then_inc(b_max, 1)
                route(1)
                if exists(T):
                    dve.wait_ge(b_max, T + 1)
                    wait(dve, b_ex, T - 1)
                    dve.tensor_tensor(SH[:, s % 2], ATT[:, :, :], AMX[:, :].unsqueeze(2).broadcast_to([P, H, H]),
                                      ALU.subtract).then_inc(b_sh, 1)
                route(2)
                if exists(T - 1):
                    dve.wait_ge(b_ex, T)
                    dve.tensor_reduce(ASUM[:, :], EX[:, V % 2], AX.X, ALU.add).then_inc(b_red2, 1)
                route(3)
                if exists(T - 2):
                    dve.wait_ge(b_sum, T - 1)
                    dve.wait_ge(b_rs, T - 1)
                    wait(dve, b_wvT, T - 3)
                    dve.tensor_tensor(BWV[:, s % 2, :].rearrange("p (h d) -> p h d", h=H),
                                      psS[s % 2][:, 0:D].rearrange("p (h d) -> p h d", h=H),
                                      ARS[:, :].unsqueeze(2).broadcast_to([P, H, HD]), ALU.mult).then_inc(b_wv, 1)
                if exists(T - 1):
                    dve.tensor_tensor(PROD2[:, :, :, :],
                                      EX[:, V % 2].rearrange("p h g -> p g h").unsqueeze(3).broadcast_to([P, H, H, HD]),
                                      VB[:, V].unsqueeze(2).broadcast_to([P, H, H, HD]), ALU.mult).then_inc(b_p2, 1)
                route(4)
                if exists(T - 1):
                    dve.wait_ge(b_red2, T)
                    wait(dve, b_wv, T - 1)
                    dve.reciprocal(ARS[:, :], ASUM[:, :]).then_inc(b_rs, 1)
                route(5)
                if exists(T + 2):
                    cosines(T + 2, (s + 2) % RING)
                route(6)
                if s % GT == 3 and routed(g + 2) and exists(T + 1):
                    combine(dve, 0, g + 2, s // GT)
                if s % GT == 3 and routed(g - 2):
                    route_keep(dve, GROUPS + g - 2, s // GT, GT * (g - 2))
                if s % GT == 2 and routed(g - 1):
                    route_numbers(dve, GROUPS + g - 1, 1 - s // GT, GT * (g - 1))
                route(7)

            combine(dve, 0, 0, 0)
            dve.wait_ge(f_done, 1)
            group_stats(dve, GROUPS, 0, 0)
            over_eights(dve, slot)
            dve.wait_ge(b_x, TILES)

        @block.sync
        def _(sp):
            for b in range(BATCH):
                sp.dma_start(X[:, b * TPB:(b + 1) * TPB, :], h_v[:, b * TPB:(b + 1) * TPB, :]).then_inc(x_in[b], 16)
            sp.dma_start(WQ[:, :], Wqvk).then_inc(w_in, 16)
            sp.dma_start(WO[:, :], Wo).then_inc(w_in, 16)
            ffn_consts_sp(sp)
            for a in range(0, NE, B2_EXPERTS):
                sp.dma_start(W2[:, a:a + B2_EXPERTS, :],
                             w2pack[a:a + B2_EXPERTS, :, :].rearrange("e p n -> p e n")).then_inc(w2_in, 16)
            sp.dma_start(B1[:, :], b1).then_inc(w2_in, 16)
            attb_load(sp)
            for c in range(NE // B2_EXPERTS):
                if c > 0:
                    sp.wait_ge(b2_split, B2_STEPS * c)
                sp.dma_start(B2F[:, :], b2[:, c * B2_EXPERTS * D:(c + 1) * B2_EXPERTS * D].broadcast_to(
                    [96, B2_EXPERTS * D])).then_inc(b2_in, 16)
            experts_sp(sp, 0)
            experts_sp(sp, 1)
            sp.wait_ge(out_sent, 16 * GROUPS)

        def split_parts(pool, T, par):
            q, k = (QK[:, i, :].rearrange("p (h d) -> p h d", h=H) for i in range(2))
            qs, ks = (m[:, :, 0:K48].rearrange("p h (c d) -> p h c d", c=SLOTS) for m in (QS[:, par], KS))
            rq, rk = (R1[:, i, :].rearrange("p (h d) -> p h d", h=H) for i in range(2))

            def spread(x, n):
                return x.unsqueeze(2).broadcast_to([P, H, n, HD])

            def ones(n):
                return ONE[:, :].unsqueeze(2).unsqueeze(3).broadcast_to([P, H, n, HD])

            wait(pool, q2T_done, T - 1)
            pool.tensor_tensor(QS[:, par, :, K48:K48 + 2], ZERO[:, :].rearrange("p (h c) -> p h c", h=H),
                               ZERO[:, :].rearrange("p (h c) -> p h c", h=H), ALU.mult).then_inc(hi_done, 1)
            pool.wait_ge(qk_copied, 2 * T + 2)
            wait(pool, kT_done, T)
            pool.tensor_tensor(qs[:, :, 0:3, :], spread(q, 3), ones(3), ALU.mult).then_inc(hi_done, 1)
            pool.tensor_tensor(ks[:, :, 2:5, :], spread(k, 3), ones(3), ALU.mult).then_inc(hi_done, 1)
            pool.wait_ge(hi_done, 3 * T + 3)
            pool.tensor_tensor(rq, q, qs[:, :, 2, :], ALU.subtract).then_inc(r1_done, 1)
            pool.tensor_tensor(rk, k, ks[:, :, 2, :], ALU.subtract).then_inc(r1_done, 1)
            pool.wait_ge(r1_done, 2 * T + 2)
            pool.tensor_tensor(qs[:, :, 3:6:2, :], spread(rq, 2), ones(2), ALU.mult).then_inc(mid_done, 1)
            pool.tensor_tensor(ks[:, :, 0:6:5, :], spread(rk, 2), ones(2), ALU.mult).then_inc(mid_done, 1)
            pool.wait_ge(mid_done, 2 * T + 2)
            pool.tensor_tensor(qs[:, :, 4, :], rq, qs[:, :, 5, :], ALU.subtract).then_inc(parts_done, 1)
            pool.tensor_tensor(ks[:, :, 1, :], rk, ks[:, :, 5, :], ALU.subtract).then_inc(parts_done, 1)

        @block.gpsimd
        def _(pool):
            pool.memset(NHALF[:, :], -0.5).then_inc(const_a, 1)
            pool.memset(ZERO[:, :], 0.0).then_inc(const_a, 1)
            pool.memset(ONE[:, :], 1.0).then_inc(const_a, 1)
            pool.memset(IDF[:, :], 0.0).then_inc(const_a, 1)
            pool.memset(IDB[:, :], 0.0).then_inc(const_a, 1)
            pool.memset(MASK[:, :], 0.0).then_inc(const_a, 1)
            pool.memset(MASKT[:, :], 0.0).then_inc(const_a, 1)
            pool.memset(QS[:, :, :, :], 0.0).then_inc(const_a, 1)
            pool.memset(KS[:, :, 0:K48 + 2], 1.0).then_inc(const_a, 1)
            pool.memset(KS[:, :, K48 + 2:HEADW], 0.0).then_inc(const_a, 1)
            pool.wait_ge(const_a, 10)
            for m in (IDF, IDB):
                pool.affine_select(out=m[:, :], in_=m[:, :], compare_op=ALU.not_equal, fill=1.0, base=0,
                                   pattern=[[-1, P]], channel_multiplier=1).then_inc(const_ready, 1)
            for m, sign in ((MASK, 1), (MASKT, -1)):
                pool.affine_select(out=m[:, :], in_=m[:, :], compare_op=ALU.is_ge, fill=NEG, base=0,
                                   pattern=[[-sign, P]], channel_multiplier=sign).then_inc(const_ready, 1)
            ffn_consts_pool(pool)
            group_deviation(pool, 0, 0)

            def slot(T, r, n):
                if exists(T + 2):
                    split_parts(pool, T + 2, r % 2)
                if r % GT == 0 and routed(n + 2) and routed(n + 1):
                    group_deviation(pool, n + 2, (r // GT + 1) % 2)
                if isinstance(T, int) and 2 <= T < 2 + NE // B2_EXPERTS:
                    split_b2(pool, T - 2)
                if routed(n) and r % GT == 0:
                    route_deviation(pool, n)
                if routed(n) and r % GT >= 2:
                    if r % GT == 2:
                        route_settle(pool, n)
                        route_keep(pool, n, 1 - r // GT, GT * n)
                    route_send(pool, n, 1 - r // GT, ((0, 1), (2, 3))[r % GT - 2])

            over_tiles(pool, slot)
            experts_pool(pool, 0)
            attb_pool(pool)
            experts_pool(pool, 1)

        @block.tensor
        def _(pe):
            def x_transpose(T):
                pe.wait_ge(xn_done, T + 1)
                wait(pe, x1_done, T - 3)
                pe.transpose(psM[:, 0:P], XN[:, :], IDF[:, :]).then_inc(xT_done, 1)

            def project(T):
                pe.wait_ge(xT_copied, T + 1)
                pe.matmul(psM[:, 0:3 * D], XT[:, :], WQ[:, :], start=True, stop=True).then_inc(qkv_done, 1)

            def transposes(out_, src, done):
                for g in range(PAIRS):
                    mm = pe.transpose(out_[:, g, :], src[:, 2 * g:2 * g + 2, :], IDB[:, :])
                mm.then_inc(done, 1)

            def q_transposes(T, r):
                pe.wait_ge(parts_done, 2 * T + 2)
                wait(pe, q2T_copied, T - 1)
                transposes(psT, QS[:, r % 2], qT_done)

            def k_transposes(T):
                pe.wait_ge(parts_done, 2 * T + 2)
                wait(pe, kT_copied, T)
                transposes(psK, KS, kT_done)

            def q2_transposes(T, r):
                pe.wait_ge(m_done, T + 1)
                wait(pe, qT_copied, min(T + 2, TILES) if isinstance(T, int) else T + 2)
                transposes(psT, QS[:, r % 2], q2T_done)

            def scoresA(T, r, k):
                s, g, rows = r % TPB, k // 2, slice(HEADW * (k % 2), HEADW * (k % 2 + 1))
                if k == 0:
                    pe.wait_ge(kT_copied, T + 1)
                    pe.wait_ge(qT_copied, T + 1)
                wait(pe, max_done, H * T + k - 1)
                pe.matmul(psA[k % 2][:, 0:(s + 1) * P], QT[rows, r % 2, g, :], KT[rows, r - s:r + 1, g, :],
                          start=True, stop=False, skip_group_check=True)
                pe.matmul(psA[k % 2][:, s * P:(s + 1) * P], IDB[:, :], MASK[:, :], start=False, stop=True,
                          skip_group_check=True).then_inc(scoresA_done, 1)

            def scoresB(T, r, k):
                s, g, rows = r % TPB, k // 2, slice(HEADW * (k % 2), HEADW * (k % 2 + 1))
                if k == 0:
                    pe.wait_ge(q2T_copied, T + 1)
                wait(pe, exp_done, H * T + k - 1)
                for t in range(s + 1):
                    pe.matmul(psB[k % 2][:, t * P:(t + 1) * P], KT[rows, r - s + t, g, :], QT2[rows, r % 2, g, :],
                              start=(t == 0), stop=False, skip_group_check=True)
                pe.matmul(psB[k % 2][:, s * P:(s + 1) * P], IDB[:, :], MASKT[:, :], start=False, stop=True,
                          skip_group_check=True).then_inc(scoresB_done, 1)

            def pv(T, r, q):
                s = r % TPB
                pe.wait_ge(exp_done, H * T + 4 * q + 4)
                if q == 0:
                    pe.wait_ge(v_copied, T + 1)
                    wait(pe, o_copied, T)
                for t in range(s + 1):
                    for j in range(4):
                        mm = pe.matmul(psO[32 * j:32 * j + 32, q, :], V32[:, r - s + t, 4 * q + j, :],
                                       PT[:, q % 2, j, t * P:(t + 1) * P], start=(t == 0), stop=(t == s))
                mm.then_inc(pv_done, 1)

            def o_transposes(T):
                pe.wait_ge(o_copied, T + 1)
                pe.wait_ge(v_copied, min(T + 4, TILES) if isinstance(T, int) else T + 4)
                wait(pe, x1_done, T)
                for q in range(G4):
                    mm = pe.transpose(psM[:, q * P:(q + 1) * P], OS[:, q, :], IDF[:, :])
                mm.then_inc(oT_done, 1)

            def wv_transpose(T):
                pe.wait_ge(wv_done, T + 1)
                pe.transpose(psM[:, 0:P], WV[:, :], IDF[:, :]).then_inc(wvT_done, 1)

            def out_project(T):
                pe.wait_ge(wvT_copied, T + 1)
                pe.matmul(psM[:, 0:D], WVT[:, :], WO[:, :], start=True, stop=True).then_inc(wo_done, 1)

            def slot(T, r, n):
                before = (r - 1) % RING
                for k in range(H):
                    if exists(T + 2) and k == X_AT:
                        x_transpose(T + 2)
                    if exists(T) and k == MAX_AT:
                        q2_transposes(T, r)
                    if exists(T + 2) and k == QKV_AT:
                        project(T + 2)
                    if exists(T + 1):
                        scoresA(T + 1, (r + 1) % RING, k)
                    if k >= LAG and exists(T):
                        scoresB(T, r, k - LAG)
                    if k < LAG and exists(T - 1):
                        scoresB(T - 1, before, k + H - LAG)
                    for q in range(G4):
                        if k == (4 * q + PV_AFTER) % H:
                            if 4 * q + PV_AFTER < H and exists(T):
                                pv(T, r, q)
                            if 4 * q + PV_AFTER >= H and exists(T - 1):
                                pv(T - 1, before, q)
                    if exists(T - 1):
                        if k == O_AT:
                            o_transposes(T - 1)
                        if k == WV_AT:
                            wv_transpose(T - 1)
                        if k == OUT_AT:
                            out_project(T - 1)
                    if routed(n):
                        u = H * (r % GT) + k
                        if u == RT_AT:
                            route_transpose(pe, n, 1 - r // GT, kT_copied, min(T + 2, TILES) if isinstance(T, int) else T + 2)
                        if u == RL_AT:
                            route_logits(pe, n)
                        if u == RANK_AT:
                            route_ranks(pe, n)
                    if exists(T + 2):
                        if k == QT_AT:
                            q_transposes(T + 2, (r + 2) % RING)
                        if k == KT_AT:
                            if r % GT in (1, 2) and routed(n):
                                pe.wait_ge(r_link, R_LINKS * n + (1 if r % GT == 1 else 14))
                            k_transposes(T + 2)

            pe.wait_ge(f_const, 11)
            pe.wait_ge(f_w_in, 32)
            pe.wait_ge(const_ready, 4)
            pe.wait_ge(w_in, 32)
            pe.wait_ge(const_v, 6)
            over_tiles(pe, slot)
            pe.wait_ge(x1_done, TILES)
            experts_pe(pe, 0)
            pe.wait_ge(b_w_in, 16 * 9)
            pe.wait_ge(f_y, ROW_TILES)
            attb_pe(pe)
            pe.wait_ge(b_x, TILES)
            experts_pe(pe, 1)

        @block.scalar
        def _(act):
            def xT_copy(T):
                act.wait_ge(xT_done, T + 1)
                act.activation(XT[:, :], psM[:, 0:P], ACT.Copy).then_inc(xT_copied, 1)

            def qkv_copy(T, r):
                act.wait_ge(qkv_done, T + 1)
                wait(act, parts_done, 2 * T)
                act.activation(QK[:, 0, :], psM[:, 0:D], ACT.Copy, scale=float(D) ** -0.5).then_inc(qk_copied, 1)
                act.activation(QK[:, 1, :], psM[:, 2 * D:3 * D], ACT.Copy).then_inc(qk_copied, 1)
                act.activation(V32[:, r, :, 0:HD], psM[:, D:2 * D].rearrange("p (h d) -> p h d", h=H),
                               ACT.Copy).then_inc(v_copied, 1)

            def qT_copy(T, r):
                act.wait_ge(qT_done, T + 1)
                act.activation(QT[:, r % 2, :, :], psT, ACT.Copy).then_inc(qT_copied, 1)

            def exps(T, r, k):
                n = (r % TPB + 1) * P
                q = k // 4
                if k % 4 == 0:
                    wait(act, pv_done, G4 * T + q - 1)
                act.wait_ge(scoresB_done, H * T + k + 1)
                act.activation(PT[:, q % 2, k % 4, 0:n], psB[k % 2][:, 0:n], ACT.Exp).then_inc(exp_done, 1)

            def o_copy(T):
                act.wait_ge(pv_done, G4 * (T + 1))
                wait(act, oT_done, T)
                act.activation(OS[:, :, :], psO[:, :, :], ACT.Copy).then_inc(o_copied, 1)

            def wvT_copy(T):
                act.wait_ge(wvT_done, T + 1)
                act.activation(WVT[:, :], psM[:, 0:P], ACT.Copy).then_inc(wvT_copied, 1)

            def slot(T, r, n):
                before = (r - 1) % RING
                for k in range(H):
                    if exists(T + 2) and k == X_AT:
                        xT_copy(T + 2)
                    if exists(T + 2) and k == QKV_AT:
                        qkv_copy(T + 2, (r + 2) % RING)
                    if k >= LAG and exists(T):
                        exps(T, r, k - LAG)
                    if k < LAG and exists(T - 1):
                        exps(T - 1, before, k + H - LAG)
                    if exists(T - 1):
                        if k == O_COPY_AT:
                            o_copy(T - 1)
                        if k == WV_AT:
                            wvT_copy(T - 1)
                    if exists(T + 2) and k == QT_AT:
                        qT_copy(T + 2, (r + 2) % RING)
                    if routed(n):
                        u = H * (r % GT) + k
                        if u == RN_AT:
                            route_normalize(act, n, 1 - r // GT, GT * n)
                        if u == RT_AT:
                            route_copy(act, n)
                        if u == RL_AT:
                            route_second(act, n, 1 - r // GT)
                        if u == RANK_AT - 1:
                            route_exp(act, n)

            over_tiles(act, slot)
            experts_act(act, 0)
            act.wait_ge(b_w_in, 16 * 9)
            attb_act(act)
            experts_act(act, 1)

        @block.vector
        def _(dve):
            def tile_of(x, T):
                return x[:, bass.ds(T, 1), :].rearrange("p a d -> p (a d)")

            def normalize(T, r):
                wait(dve, xT_done, T)
                dve.tensor_scalar(XN[:, :], tile_of(X, T), MEAN[:, r:r + 1], RSD[:, r:r + 1],
                                  ALU.add, ALU.mult).then_inc(xn_done, 1)

            def kT_copy(T, r):
                dve.wait_ge(kT_done, T + 1)
                dve.tensor_copy(KT[:, r, :, :], psK).then_inc(kT_copied, 1)

            def q2T_copy(T, r):
                dve.wait_ge(q2T_done, T + 1)
                dve.tensor_copy(QT2[:, r % 2, :, :], psT).then_inc(q2T_copied, 1)

            def maxes(T, r, k):
                n = (r % TPB + 1) * P
                dve.wait_ge(scoresA_done, H * T + k + 1)
                dve.tensor_reduce(NM[:, r % 2, k:k + 1], psA[k % 2][:, 0:n], AX.X, ALU.max,
                                  negate=True).then_inc(max_done, 1)

            def m_parts(T, r):
                dve.wait_ge(max_done, H * (T + 1))
                dve.wait_ge(qT_done, T + 1)
                dve.tensor_copy(QS[:, r % 2, :, K48], NM[:, r % 2, :]).then_inc(m_hi_done, 1)
                dve.wait_ge(m_hi_done, T + 1)
                dve.tensor_tensor(QS[:, r % 2, :, K48 + 1], NM[:, r % 2, :], QS[:, r % 2, :, K48],
                                  ALU.subtract).then_inc(m_done, 1)

            def weigh(T):
                o = psM[:, :].rearrange("p (h d) -> p h d", h=H)
                dve.wait_ge(oT_done, T + 1)
                dve.reciprocal(RS[:, :], o[:, :, HD]).then_inc(rs_done, 1)
                dve.wait_ge(rs_done, T + 1)
                wait(dve, wvT_done, T)
                dve.tensor_tensor(WV[:, :].rearrange("p (h d) -> p h d", h=H), o[:, :, 0:HD],
                                  RS[:, :].unsqueeze(2).broadcast_to([P, H, HD]), ALU.mult).then_inc(wv_done, 1)

            def add_attention(T):
                dve.wait_ge(wo_done, T + 1)
                dve.tensor_tensor(tile_of(X, T), tile_of(X, T), psM[:, 0:D], ALU.add).then_inc(x1_done, 1)

            def slot(T, r, n):
                for k in range(H):
                    if exists(T) and k == 0:
                        m_parts(T, r)
                    if exists(T + 2) and k == NORM_AT:
                        if r % GT == GT - 2:
                            dve.wait_ge(f_rstd, n + 3)
                        normalize(T + 2, (r + 2) % RING)
                    if k == GROUP_AT and r % GT == 0 and routed(n + 2) and routed(n + 1):
                        if isinstance(n, int) and n < 1:
                            for b in ((1,), range(2, BATCH))[n + 1]:
                                dve.wait_ge(x_in[b], 16)
                        group_stats(dve, n + 2, GT * (n + 2), (r // GT + 1) % 2)
                    if exists(T) and k == MAX_AT:
                        q2T_copy(T, r)
                    if exists(T + 1):
                        maxes(T + 1, (r + 1) % RING, k)
                    if exists(T - 1):
                        if k == O_AT:
                            weigh(T - 1)
                        if k == OUT_AT:
                            add_attention(T - 1)
                    if exists(T + 2) and k == KT_AT:
                        kT_copy(T + 2, (r + 2) % RING)
                    if routed(n):
                        u = H * (r % GT) + k
                        if u == STATS_AT:
                            route_stats(dve, n, GT * n, x1_done)
                        if u == RN_AT:
                            route_numbers(dve, n, 1 - r // GT, GT * n)
                        if TOP_AT <= u < TOP_AT + 12:
                            route_top(dve, n, u - TOP_AT)
                        if ROWS_AT <= u < ROWS_AT + 4:
                            route_rows(dve, n, 1 - r // GT, u - ROWS_AT)

            dve.memset(V32[:, :, :, HD + 1:32], 0.0).then_inc(const_v, 1)
            dve.memset(V32[:, :, :, HD], 1.0).then_inc(const_v, 1)
            dve.memset(SEL3[:, :], 0.0).then_inc(const_v, 1)
            dve.wait_ge(const_v, 3)
            for part in range(3):
                dve.memset(SEL3[32 * part:32 * part + 1, :], 1.0).then_inc(const_v, 1)
            dve.memset(LT[LATENT:LATENT + 1, :, :], 1.0).then_inc(b_const, 1)
            dve.wait_ge(x_in[0], 16)
            group_stats(dve, 0, 0, 0)
            dve.wait_ge(f_w_in, 32)
            dve.wait_ge(f_const, 11)
            dve.tensor_copy(RUN[:, :], RUN0[:, :]).then_inc(b_const, 1)
            dve.wait_ge(b_const, 2)
            over_tiles(dve, slot)
            expert_tables(dve, 0)
            experts_dve(dve, 0)
            dve.wait_ge(e_link, E_LINKS)
            attb_dve(dve)
            expert_tables(dve, 1)
            experts_dve(dve, 1)
            for g in range(GROUPS):
                combine(dve, 1, g, g % len(f_yc[1]))


_OUTS = [((BATCH, SEQ, D), 'float32')]


def rope_table(np):
    inv = (1.0 / 10000.0 ** (np.arange(0, HD, 2, dtype=np.float32) / HD)).astype(np.float32)
    angle = np.arange(SEQ, dtype=np.float32)[:, None] * inv[None, :]
    cos, sin = np.cos(angle), np.sin(angle)
    table = np.stack([np.concatenate([cos, cos], 1), np.concatenate([-sin, sin], 1)], 1)
    return table.reshape(TPB, P, 2, HD).transpose(1, 0, 2, 3).astype(np.float32)


def kernel(**inputs):
    import numpy as _np
    import concourse.bacc as _bacc
    from concourse import mybir as _mybir
    from concourse.bass_utils import run_bass_kernel_spmd as _run

    nc = _bacc.Bacc("TRN2", target_bir_lowering=False, num_devices=1)
    w1, w2, b1 = (_np.asarray(inputs[f"L0_ffn_{n}"]) for n in ("w1", "w2", "b1"))
    given = {
        "h": inputs["L0_attn_a_h"],
        "Wqvk": inputs["L0_attn_a_Wqvk"],
        "Wo": inputs["L0_attn_a_Wo"],
        "gate_w": inputs["L0_ffn_gate_w"],
        "gate_b": _np.asarray(inputs["L0_ffn_gate_b"]).reshape(1, NE),
        "w1": w1,
        "w2pack": w2.reshape(NE, FC, P, D).transpose(0, 2, 1, 3).reshape(NE, P, FC * D),
        "b1": b1.reshape(NE, FC, P).transpose(2, 0, 1).reshape(P, NE * FC),
        "b2": _np.asarray(inputs["L0_ffn_b2"]).reshape(1, NE * D),
        "Wq": inputs["L0_attn_b_Wq"],
        "bq": _np.asarray(inputs["L0_attn_b_bq"]).reshape(1, D),
        "Wdown": inputs["L0_attn_b_Wdown"],
        "bdown": _np.asarray(inputs["L0_attn_b_bdown"]).reshape(LATENT, 1),
        "Wup": inputs["L0_attn_b_Wup"],
        "bup": _np.asarray(inputs["L0_attn_b_bup"]).reshape(1, 2 * D),
        "Wout": inputs["L0_attn_b_Wout"],
        "bout": _np.asarray(inputs["L0_attn_b_bout"]).reshape(1, D),
        "rope": rope_table(_np),
    }
    arrays, args = {}, []
    for name, x in given.items():
        a = _np.ascontiguousarray(x)
        arrays[f"in_{name}_dram"] = a
        args.append(nc.dram_tensor(f"in_{name}_dram", a.shape, _mybir.dt.from_np(a.dtype), kind="ExternalInput").ap())
    for i, (shape, dtype) in enumerate(_OUTS):
        dt = _mybir.dt.from_np(_np.dtype(dtype))
        args.append(nc.dram_tensor(f"out_{i}_dram", shape, dt, kind="ExternalOutput").ap())
    hybrid_layer(nc, *args)
    r = _run(nc, [arrays], core_ids=[0])
    return r.results[0]["out_0_dram"]
```
